# Optimizing a Trainium2 kernel written in Bass

```python
import numpy as np
import jax
import jax.numpy as jnp

def _softmax(x, axis=-1):
    return jax.nn.softmax(x, axis=axis)

def _gelu(x):
    return jax.nn.gelu(x, approximate=True)

def _silu(x):
    return jax.nn.silu(x)

def _sigmoid(x):
    return jax.nn.sigmoid(x)

def _layernorm(x, axis=-1, eps=1e-05):
    m = jnp.mean(x, axis=axis, keepdims=True)
    v = jnp.var(x, axis=axis, keepdims=True)
    return (x - m) / jnp.sqrt(v + eps)

def _scatter_add(tgt, idx, src, axis=0):
    return tgt.at[idx].add(src)

def _segment_sum(src, seg, n):
    return jax.ops.segment_sum(src, seg, n)
kernel_name = 'mk_flamingo_gated_d4_seqx_r8_a94af6'

def setup_inputs(seed: int=0):
    np.random.seed(seed)
    _w = jnp.asarray

    def _rec_inputs():
        import jax
        import jax.numpy as jnp
        _rk = jax.random.key(seed)
        x = -0.0003929 + 0.9999 * jax.random.normal(jax.random.fold_in(_rk, 1), (32, 128, 128), jnp.float32)
        _lenS = 128 - jax.random.randint(jax.random.fold_in(_rk, 7), (32,), 0, max(1, 128 // 4) + 1, jnp.int32)
        _lenS2 = 128 - jax.random.randint(jax.random.fold_in(_rk, 8), (32,), 0, max(1, 128 // 4) + 1, jnp.int32)
        _ctx_512P = jax.random.normal(jax.random.fold_in(_rk, 11), (32, 16, 64), jnp.float32)
        _ctx_512c = jax.random.dirichlet(jax.random.fold_in(_rk, 511), 0.3 * jnp.ones((16,), jnp.float32), (32, 128))
        _ctx_512t = jnp.einsum('bsk,bkd->bsd', _ctx_512c, _ctx_512P)
        _ctx_512t = _ctx_512t * jax.lax.rsqrt(jnp.mean(jnp.square(_ctx_512t)) + 1e-12) * 0.953939
        ctx_512 = -1.39393e-06 + 0.999914 * (_ctx_512t + 0.3 * jax.random.normal(jax.random.fold_in(_rk, 611), (32, 128, 64), jnp.float32))
        _g = jax.random.normal(jax.random.fold_in(_rk, 9001), (2, 4), jnp.float32)
        _g = jnp.sign(_g) * jnp.maximum(jnp.abs(_g), 1.0) + (_g == 0) * 1.0
        g_xattn = _g[0]
        g_ffn = _g[1]
        return (x, ctx_512, g_xattn, g_ffn)
    x, ctx_512, g_xattn, g_ffn = _rec_inputs()

    def _L0_xattn_setup():
        import jax, jax.numpy as jnp
        import numpy as np
        HEADS = 16
        D_MODEL = 128
        IMG_MODEL = 64
        D_K = D_MODEL // HEADS
        key = jax.random.key(seed)
        ks = jax.random.split(key, 12)
        B, LQ, LKV = (8, 256, 128)
        s_dm = 1.0 / np.sqrt(D_MODEL)
        s_im = 1.0 / np.sqrt(IMG_MODEL)
        return {'q': jax.random.normal(ks[0], (B, LQ, D_MODEL), jnp.float32), 'k': jax.random.normal(ks[1], (B, LKV, IMG_MODEL), jnp.float32), 'v': jax.random.normal(ks[2], (B, LKV, IMG_MODEL), jnp.float32), 'Wq': jax.random.normal(ks[3], (D_MODEL, D_MODEL), jnp.float32) * s_dm, 'bq': jnp.zeros((D_MODEL,), jnp.float32), 'Wk': jax.random.normal(ks[4], (IMG_MODEL, D_MODEL), jnp.float32) * s_im, 'bk': jnp.zeros((D_MODEL,), jnp.float32), 'Wv': jax.random.normal(ks[5], (IMG_MODEL, D_MODEL), jnp.float32) * s_im, 'bv': jnp.zeros((D_MODEL,), jnp.float32), 'Wo': jax.random.normal(ks[6], (D_MODEL, D_MODEL), jnp.float32) * s_dm, 'bo': jnp.zeros((D_MODEL,), jnp.float32)}
    _L0_xattn_all = _L0_xattn_setup()
    _L0_xattn_in = {k: v for k, v in _L0_xattn_all.items() if k in ('Wq', 'bq', 'Wk', 'bk', 'Wv', 'bv', 'Wo', 'bo')}
    del _L0_xattn_all

    def _L0_ffn_setup():
        import jax, jax.numpy as jnp
        import numpy as np
        H = 128
        E = 32
        I = 64
        TOP_K = 6
        IS = 128
        NORM_MIN = 1e-12
        B, S = (2, 128)
        key = jax.random.key(seed)
        ks = jax.random.split(key, 8)
        sc = 0.02
        return {'hidden_states': jax.random.normal(ks[0], (B, S, H), jnp.float32), 'router_weight': jax.random.normal(ks[1], (E, H), jnp.float32) * sc, 'e_score_bias': jnp.zeros((E,), jnp.float32), 'gate_up_proj': jax.random.normal(ks[2], (E, 2 * I, H), jnp.float32) * sc, 'down_proj': jax.random.normal(ks[3], (E, H, I), jnp.float32) * sc, 'shared_gate_w': jax.random.normal(ks[4], (IS, H), jnp.float32) * sc, 'shared_up_w': jax.random.normal(ks[5], (IS, H), jnp.float32) * sc, 'shared_down_w': jax.random.normal(ks[6], (H, IS), jnp.float32) * sc}
    _L0_ffn_all = _L0_ffn_setup()
    _L0_ffn_in = {k: v for k, v in _L0_ffn_all.items() if k in ('router_weight', 'e_score_bias', 'gate_up_proj', 'down_proj', 'shared_gate_w', 'shared_up_w', 'shared_down_w')}
    del _L0_ffn_all

    def _L1_xattn_setup():
        import jax, jax.numpy as jnp
        import numpy as np
        H, D, C1, C2, S, M, B, W = (16, 32, 128, 64, 256, 64, 2, 4)

        def _ln(x, g, b):
            m = jnp.mean(x, -1, keepdims=True)
            v = jnp.var(x, -1, keepdims=True)
            return (x - m) * jax.lax.rsqrt(v + 1e-05) * g + b

        def _mha(x, y, wq, wk, wv, li1_w, li1_b, lnx_g, lnx_b, lny_g, lny_b, ln3_g, ln3_b, li2_w, li2_b, li3_w, li3_b, causal):
            xn = _ln(x, lnx_g, lnx_b)
            yn = _ln(y, lny_g, lny_b)
            q = jnp.einsum('bsc,hcd->bhsd', xn, wq)
            k = jnp.einsum('btc,hcd->bhtd', yn, wk)
            v = jnp.einsum('btc,hcd->bhtd', yn, wv)
            a = jax.nn.softmax(jnp.einsum('bhsd,bhtd->bhst', q, k) * D ** (-0.5), axis=-1)
            if causal:
                s, t = (a.shape[-2], a.shape[-1])
                mask = (jnp.arange(t)[None, :] > jnp.arange(s)[:, None]).astype(a.dtype)
                a = a * mask
            o = jnp.einsum('bhst,bhtd->bhsd', a, v)
            o = o.transpose(0, 2, 1, 3).reshape(x.shape[0], x.shape[1], H * D)
            x_out = x + o @ li1_w + li1_b
            h = jax.nn.gelu(_ln(x_out, ln3_g, ln3_b) @ li2_w + li2_b, approximate=False)
            return x_out + h @ li3_w + li3_b
        key = jax.random.key(seed)
        ks = iter(jax.random.split(key, 64))

        def w(shape, scale=0.02):
            return jax.random.normal(next(ks), shape, jnp.float32) * scale
        inp = {'xx': jax.random.normal(next(ks), (B, S, C1), jnp.float32), 'ee': jax.random.normal(next(ks), (B, M, C2), jnp.float32), 'ln1_g': jnp.ones(C1, jnp.float32), 'ln1_b': jnp.zeros(C1, jnp.float32), 'ln2_g': jnp.ones(C1, jnp.float32), 'ln2_b': jnp.zeros(C1, jnp.float32)}
        for pfx, cy in (('a1', C1), ('a2', C2)):
            inp[pfx + '_wq'] = w((H, C1, D))
            inp[pfx + '_wk'] = w((H, cy, D))
            inp[pfx + '_wv'] = w((H, cy, D))
            inp[pfx + '_li1_w'] = w((H * D, C1))
            inp[pfx + '_li1_b'] = jnp.zeros(C1, jnp.float32)
            inp[pfx + '_lnx_g'] = jnp.ones(C1, jnp.float32)
            inp[pfx + '_lnx_b'] = jnp.zeros(C1, jnp.float32)
            inp[pfx + '_lny_g'] = jnp.ones(cy, jnp.float32)
            inp[pfx + '_lny_b'] = jnp.zeros(cy, jnp.float32)
            inp[pfx + '_ln3_g'] = jnp.ones(C1, jnp.float32)
            inp[pfx + '_ln3_b'] = jnp.zeros(C1, jnp.float32)
            inp[pfx + '_li2_w'] = w((C1, C1 * W))
            inp[pfx + '_li2_b'] = jnp.zeros(C1 * W, jnp.float32)
            inp[pfx + '_li3_w'] = w((C1 * W, C1))
            inp[pfx + '_li3_b'] = jnp.zeros(C1, jnp.float32)
        inp['training'] = 0
        return inp
    _L1_xattn_all = _L1_xattn_setup()
    _L1_xattn_in = {k: v for k, v in _L1_xattn_all.items() if k in ('ln1_g', 'ln1_b', 'ln2_g', 'ln2_b', 'a1_wq', 'a1_wk', 'a1_wv', 'a1_li1_w', 'a1_li1_b', 'a1_lnx_g', 'a1_lnx_b', 'a1_lny_g', 'a1_lny_b', 'a1_ln3_g', 'a1_ln3_b', 'a1_li2_w', 'a1_li2_b', 'a1_li3_w', 'a1_li3_b', 'a2_wq', 'a2_wk', 'a2_wv', 'a2_li1_w', 'a2_li1_b', 'a2_lnx_g', 'a2_lnx_b', 'a2_lny_g', 'a2_lny_b', 'a2_ln3_g', 'a2_ln3_b', 'a2_li2_w', 'a2_li2_b', 'a2_li3_w', 'a2_li3_b')}
    del _L1_xattn_all

    def _L1_ffn_setup():
        import jax, jax.numpy as jnp
        import numpy as np
        B, S, H = (4, 256, 128)
        E = 8
        GS = 2
        NG = E // GS
        F = int(H * 4 * (2.0 / 3.0))
        key = jax.random.key(seed)
        ks = jax.random.split(key, 7)
        sc_h = 1.0 / np.sqrt(H)
        sc_f = 1.0 / np.sqrt(F)
        return {'x': jax.random.normal(ks[0], (B, S, H), dtype=jnp.float32), 'Wr': jax.random.normal(ks[1], (H, E), dtype=jnp.float32) * sc_h, 'br': jnp.zeros((E,), dtype=jnp.float32), 'W_up': jax.random.normal(ks[2], (NG, H, F), dtype=jnp.float32) * sc_h, 'b_up': jax.random.normal(ks[3], (NG, F), dtype=jnp.float32) * 0.01, 'W_down': jax.random.normal(ks[4], (E, F, H), dtype=jnp.float32) * sc_f, 'b_down': jax.random.normal(ks[5], (E, H), dtype=jnp.float32) * 0.01}
    _L1_ffn_all = _L1_ffn_setup()
    _L1_ffn_in = {k: v for k, v in _L1_ffn_all.items() if k in ('Wr', 'br', 'W_up', 'b_up', 'W_down', 'b_down')}
    del _L1_ffn_all

    def _L2_xattn_setup():
        import jax, jax.numpy as jnp
        import numpy as np
        DIM = 128
        LATENT_DIM = 64
        NUM_HEADS = 16
        HEAD_DIM = DIM // NUM_HEADS
        SCALE = HEAD_DIM ** (-0.5)
        key = jax.random.key(seed)
        k1, k2, k3, k4, k5 = jax.random.split(key, 5)
        B, xN, zN = (2, 256, 256)
        x = jax.random.normal(k1, (B, xN, DIM), dtype=jnp.float32)
        z = jax.random.normal(k2, (B, zN, LATENT_DIM), dtype=jnp.float32)
        Wq = jax.random.normal(k3, (DIM, DIM), dtype=jnp.float32) * DIM ** (-0.5)
        Wkv = jax.random.normal(k4, (2 * DIM, LATENT_DIM), dtype=jnp.float32) * LATENT_DIM ** (-0.5)
        Wo = jax.random.normal(k5, (DIM, DIM), dtype=jnp.float32) * DIM ** (-0.5)
        return {'x': x, 'z': z, 'Wq': Wq, 'Wkv': Wkv, 'Wo': Wo}
    _L2_xattn_all = _L2_xattn_setup()
    _L2_xattn_in = {k: v for k, v in _L2_xattn_all.items() if k in ('Wq', 'Wkv', 'Wo')}
    del _L2_xattn_all

    def _L2_ffn_setup():
        import jax, jax.numpy as jnp
        import numpy as np
        DIM = 128
        DEPTH = 2
        HEADS = 8
        DIM_HEAD = 64
        WINDOW = 64
        INNER = HEADS * DIM_HEAD
        HID = int(DIM * 4 * 2 / 3)
        B, N = (2, 1024)
        QK_SCALE = 8.0

        def shift_token(t):
            t1, t2 = jnp.split(t, 2, axis=-1)
            t2 = jnp.pad(t2, ((0, 0), (1, 0), (0, 0)))[:, :-1]
            return jnp.concatenate([t1, t2], axis=-1)

        def l2norm(t):
            return t / jnp.clip(jnp.linalg.norm(t, axis=-1, keepdims=True), 1e-12)

        def rotate_half(x):
            x1, x2 = jnp.split(x, 2, axis=-1)
            return jnp.concatenate([-x2, x1], axis=-1)

        def rotary_xpos(q, k):
            n = q.shape[-2]
            half_idx = jnp.arange(0, DIM_HEAD, 2, dtype=jnp.float32)
            inv_freq = 1.0 / 10000.0 ** (half_idx / DIM_HEAD)
            t = jnp.arange(n, dtype=jnp.float32)
            freqs = t[:, None] * inv_freq[None, :]
            freqs = jnp.concatenate([freqs, freqs], axis=-1)
            base = (half_idx + 0.4 * DIM_HEAD) / (1.4 * DIM_HEAD)
            power = (t - n // 2) / float(WINDOW // 2)
            scale = base[None, :] ** power[:, None]
            scale = jnp.concatenate([scale, scale], axis=-1)
            cos, sin = (jnp.cos(freqs), jnp.sin(freqs))
            q = q * cos * scale + rotate_half(q) * sin * scale
            k = k * cos / scale + rotate_half(k) * sin / scale
            return (q, k)

        def local_attention(q, k, v):
            b, h, n, d = q.shape
            w = n // WINDOW
            bq = q.reshape(b, h, w, WINDOW, d) * QK_SCALE
            bk = k.reshape(b, h, w, WINDOW, d)
            bv = v.reshape(b, h, w, WINDOW, d)

            def look_around(t):
                p = jnp.pad(t, ((0, 0), (0, 0), (1, 0), (0, 0), (0, 0)))
                return jnp.concatenate([p[:, :, :w], p[:, :, 1:]], axis=3)
            bk, bv = (look_around(bk), look_around(bv))
            bt = jnp.arange(n).reshape(w, WINDOW)
            btp = jnp.pad(bt, ((1, 0), (0, 0)), constant_values=-1)
            btk = jnp.concatenate([btp[:w], btp[1:]], axis=1)
            sim = jnp.einsum('bhwid,bhwjd->bhwij', bq, bk)
            i = bt[:, :, None]
            j = btk[:, None, :]
            mask = (i < j) | (i > j + WINDOW) | (j == -1)
            sim = jnp.where(mask, -jnp.finfo(sim.dtype).max, sim)
            attn = jax.nn.softmax(sim, axis=-1)
            out = jnp.einsum('bhwij,bhwjd->bhwid', attn, bv)
            return out.reshape(b, h, n, d)

        def _layer(x, wqkv, qs, ksc, wo, lg, lb, w1, b1, w2, b2):
            b, n, _ = x.shape
            h = shift_token(x)
            qkv = h @ wqkv
            q, k, v = jnp.split(qkv, 3, axis=-1)
            to_heads = lambda t: t.reshape(b, n, HEADS, DIM_HEAD).transpose(0, 2, 1, 3)
            q, k, v = (to_heads(q), to_heads(k), to_heads(v))
            q = l2norm(q) * qs
            k = l2norm(k) * ksc
            q, k = rotary_xpos(q, k)
            o = local_attention(q, k, v)
            o = o.transpose(0, 2, 1, 3).reshape(b, n, INNER)
            x = x + o @ wo
            h = shift_token(x)
            mu = h.mean(-1, keepdims=True)
            var = h.var(-1, keepdims=True)
            h = (h - mu) / jnp.sqrt(var + 1e-05) * lg + lb
            h = h @ w1 + b1
            a, g = jnp.split(h, 2, axis=-1)
            h = a * jax.nn.gelu(g, approximate=False)
            x = x + h @ w2 + b2
            return x
        key = jax.random.key(seed)
        ks = jax.random.split(key, 6)
        return {'x': jax.random.normal(ks[0], (B, N, DIM), jnp.float32), 'wqkv': jax.random.normal(ks[1], (DEPTH, DIM, 3 * INNER), jnp.float32) * 0.02, 'q_scale': jnp.ones((DEPTH, DIM_HEAD), jnp.float32), 'k_scale': jnp.ones((DEPTH, DIM_HEAD), jnp.float32), 'wo': jax.random.normal(ks[2], (DEPTH, INNER, DIM), jnp.float32) * 0.02, 'ln_g': jnp.ones((DEPTH, DIM), jnp.float32), 'ln_b': jnp.zeros((DEPTH, DIM), jnp.float32), 'w1': jax.random.normal(ks[3], (DEPTH, DIM, 2 * HID), jnp.float32) * 0.02, 'b1': jnp.zeros((DEPTH, 2 * HID), jnp.float32), 'w2': jax.random.normal(ks[4], (DEPTH, HID, DIM), jnp.float32) * 0.02, 'b2': jnp.zeros((DEPTH, DIM), jnp.float32)}
    _L2_ffn_all = _L2_ffn_setup()
    _L2_ffn_in = {k: v for k, v in _L2_ffn_all.items() if k in ('wqkv', 'q_scale', 'k_scale', 'wo', 'ln_g', 'ln_b', 'w1', 'b1', 'w2', 'b2')}
    del _L2_ffn_all

    def _L3_xattn_setup():
        import jax, jax.numpy as jnp
        import numpy as np
        HEADS = 16
        D_MODEL = 128
        IMG_MODEL = 64
        D_K = D_MODEL // HEADS
        key = jax.random.key(seed)
        ks = jax.random.split(key, 12)
        B, LQ, LKV = (8, 256, 128)
        s_dm = 1.0 / np.sqrt(D_MODEL)
        s_im = 1.0 / np.sqrt(IMG_MODEL)
        return {'q': jax.random.normal(ks[0], (B, LQ, D_MODEL), jnp.float32), 'k': jax.random.normal(ks[1], (B, LKV, IMG_MODEL), jnp.float32), 'v': jax.random.normal(ks[2], (B, LKV, IMG_MODEL), jnp.float32), 'Wq': jax.random.normal(ks[3], (D_MODEL, D_MODEL), jnp.float32) * s_dm, 'bq': jnp.zeros((D_MODEL,), jnp.float32), 'Wk': jax.random.normal(ks[4], (IMG_MODEL, D_MODEL), jnp.float32) * s_im, 'bk': jnp.zeros((D_MODEL,), jnp.float32), 'Wv': jax.random.normal(ks[5], (IMG_MODEL, D_MODEL), jnp.float32) * s_im, 'bv': jnp.zeros((D_MODEL,), jnp.float32), 'Wo': jax.random.normal(ks[6], (D_MODEL, D_MODEL), jnp.float32) * s_dm, 'bo': jnp.zeros((D_MODEL,), jnp.float32)}
    _L3_xattn_all = _L3_xattn_setup()
    _L3_xattn_in = {k: v for k, v in _L3_xattn_all.items() if k in ('Wq', 'bq', 'Wk', 'bk', 'Wv', 'bv', 'Wo', 'bo')}
    del _L3_xattn_all

    def _L3_ffn_setup():
        import jax, jax.numpy as jnp
        import numpy as np
        D = 128
        H = 4
        HD = D // H
        E = 8
        FF = 512
        CAP_FACTOR = 1.0

        def _ln(x, g, b, eps=1e-05):
            mu = jnp.mean(x, -1, keepdims=True)
            v = jnp.mean((x - mu) ** 2, -1, keepdims=True)
            return (x - mu) * jax.lax.rsqrt(v + eps) * g + b

        def _mha(x, w, b, ow, ob):
            L, N, _ = x.shape
            qkv = x @ w.T + b
            q, k, v = jnp.split(qkv, 3, axis=-1)
            rh = lambda t: t.reshape(L, N, H, HD).transpose(1, 2, 0, 3)
            q, k, v = (rh(q), rh(k), rh(v))
            scores = jnp.einsum('nhld,nhmd->nhlm', q, k) / np.float32(np.sqrt(HD))
            attn = jax.nn.softmax(scores, axis=-1)
            o = jnp.einsum('nhlm,nhmd->nhld', attn, v).transpose(2, 0, 1, 3).reshape(L, N, D)
            return o @ ow.T + ob

        def _moe(x, wg, w1, b1, w2, b2):
            L, N, _ = x.shape
            S = L * N
            cap = int(CAP_FACTOR * S) // E
            xf = x.reshape(S, D)
            gates = jax.nn.softmax(xf @ wg, axis=-1)
            idx = jnp.argmax(gates, axis=-1)
            mask1 = jax.nn.one_hot(idx, E, dtype=x.dtype)
            loc = jnp.sum((jnp.cumsum(mask1, 0) - 1.0) * mask1, -1).astype(jnp.int32)
            keep = loc < cap
            gate_val = jnp.take_along_axis(gates, idx[:, None], -1)[:, 0]
            slot = jnp.where(keep, idx.astype(jnp.int32) * cap + loc, E * cap)
            disp = jnp.zeros((E * cap, D), x.dtype).at[slot].set(xf, mode='drop')
            disp = disp.reshape(E, cap, D)
            h = jnp.einsum('ecd,edf->ecf', disp, w1) + b1[:, None, :]
            y = (jnp.einsum('ecf,efd->ecd', h, w2) + b2[:, None, :]).reshape(E * cap, D)
            out = jnp.where(keep[:, None], gate_val[:, None] * y[jnp.minimum(slot, E * cap - 1)], 0.0)
            return out.reshape(L, N, D)
        key = jax.random.key(seed)
        ks = jax.random.split(key, 8)
        L, N = (128, 16)
        s = 0.02
        return {'x': jax.random.normal(ks[0], (L, N, D), jnp.float32), 'in_proj_w': jax.random.normal(ks[1], (3 * D, D), jnp.float32) * s, 'in_proj_b': jnp.zeros((3 * D,), jnp.float32), 'out_proj_w': jax.random.normal(ks[2], (D, D), jnp.float32) * s, 'out_proj_b': jnp.zeros((D,), jnp.float32), 'ln1_g': jnp.ones((D,), jnp.float32), 'ln1_b': jnp.zeros((D,), jnp.float32), 'ln2_g': jnp.ones((D,), jnp.float32), 'ln2_b': jnp.zeros((D,), jnp.float32), 'wg': jax.random.normal(ks[3], (D, E), jnp.float32) * s, 'w1': jax.random.normal(ks[4], (E, D, FF), jnp.float32) * s, 'b1': jnp.zeros((E, FF), jnp.float32), 'w2': jax.random.normal(ks[5], (E, FF, D), jnp.float32) * s, 'b2': jnp.zeros((E, D), jnp.float32)}
    _L3_ffn_all = _L3_ffn_setup()
    _L3_ffn_in = {k: v for k, v in _L3_ffn_all.items() if k in ('in_proj_w', 'in_proj_b', 'out_proj_w', 'out_proj_b', 'ln1_g', 'ln1_b', 'ln2_g', 'ln2_b', 'wg', 'w1', 'b1', 'w2', 'b2')}
    del _L3_ffn_all
    return {'x': x, 'ctx_512': ctx_512, 'g_xattn': g_xattn, 'g_ffn': g_ffn, 'L0_xattn_Wq': _L0_xattn_in['Wq'], 'L0_xattn_bq': _L0_xattn_in['bq'], 'L0_xattn_Wk': _L0_xattn_in['Wk'], 'L0_xattn_bk': _L0_xattn_in['bk'], 'L0_xattn_Wv': _L0_xattn_in['Wv'], 'L0_xattn_bv': _L0_xattn_in['bv'], 'L0_xattn_Wo': _L0_xattn_in['Wo'], 'L0_xattn_bo': _L0_xattn_in['bo'], 'L0_ffn_router_weight': _L0_ffn_in['router_weight'], 'L0_ffn_e_score_bias': _L0_ffn_in['e_score_bias'], 'L0_ffn_gate_up_proj': _L0_ffn_in['gate_up_proj'], 'L0_ffn_down_proj': _L0_ffn_in['down_proj'], 'L0_ffn_shared_gate_w': _L0_ffn_in['shared_gate_w'], 'L0_ffn_shared_up_w': _L0_ffn_in['shared_up_w'], 'L0_ffn_shared_down_w': _L0_ffn_in['shared_down_w'], 'L1_xattn_ln1_g': _L1_xattn_in['ln1_g'], 'L1_xattn_ln1_b': _L1_xattn_in['ln1_b'], 'L1_xattn_ln2_g': _L1_xattn_in['ln2_g'], 'L1_xattn_ln2_b': _L1_xattn_in['ln2_b'], 'L1_xattn_a1_wq': _L1_xattn_in['a1_wq'], 'L1_xattn_a1_wk': _L1_xattn_in['a1_wk'], 'L1_xattn_a1_wv': _L1_xattn_in['a1_wv'], 'L1_xattn_a1_li1_w': _L1_xattn_in['a1_li1_w'], 'L1_xattn_a1_li1_b': _L1_xattn_in['a1_li1_b'], 'L1_xattn_a1_lnx_g': _L1_xattn_in['a1_lnx_g'], 'L1_xattn_a1_lnx_b': _L1_xattn_in['a1_lnx_b'], 'L1_xattn_a1_lny_g': _L1_xattn_in['a1_lny_g'], 'L1_xattn_a1_lny_b': _L1_xattn_in['a1_lny_b'], 'L1_xattn_a1_ln3_g': _L1_xattn_in['a1_ln3_g'], 'L1_xattn_a1_ln3_b': _L1_xattn_in['a1_ln3_b'], 'L1_xattn_a1_li2_w': _L1_xattn_in['a1_li2_w'], 'L1_xattn_a1_li2_b': _L1_xattn_in['a1_li2_b'], 'L1_xattn_a1_li3_w': _L1_xattn_in['a1_li3_w'], 'L1_xattn_a1_li3_b': _L1_xattn_in['a1_li3_b'], 'L1_xattn_a2_wq': _L1_xattn_in['a2_wq'], 'L1_xattn_a2_wk': _L1_xattn_in['a2_wk'], 'L1_xattn_a2_wv': _L1_xattn_in['a2_wv'], 'L1_xattn_a2_li1_w': _L1_xattn_in['a2_li1_w'], 'L1_xattn_a2_li1_b': _L1_xattn_in['a2_li1_b'], 'L1_xattn_a2_lnx_g': _L1_xattn_in['a2_lnx_g'], 'L1_xattn_a2_lnx_b': _L1_xattn_in['a2_lnx_b'], 'L1_xattn_a2_lny_g': _L1_xattn_in['a2_lny_g'], 'L1_xattn_a2_lny_b': _L1_xattn_in['a2_lny_b'], 'L1_xattn_a2_ln3_g': _L1_xattn_in['a2_ln3_g'], 'L1_xattn_a2_ln3_b': _L1_xattn_in['a2_ln3_b'], 'L1_xattn_a2_li2_w': _L1_xattn_in['a2_li2_w'], 'L1_xattn_a2_li2_b': _L1_xattn_in['a2_li2_b'], 'L1_xattn_a2_li3_w': _L1_xattn_in['a2_li3_w'], 'L1_xattn_a2_li3_b': _L1_xattn_in['a2_li3_b'], 'L1_ffn_Wr': _L1_ffn_in['Wr'], 'L1_ffn_br': _L1_ffn_in['br'], 'L1_ffn_W_up': _L1_ffn_in['W_up'], 'L1_ffn_b_up': _L1_ffn_in['b_up'], 'L1_ffn_W_down': _L1_ffn_in['W_down'], 'L1_ffn_b_down': _L1_ffn_in['b_down'], 'L2_xattn_Wq': _L2_xattn_in['Wq'], 'L2_xattn_Wkv': _L2_xattn_in['Wkv'], 'L2_xattn_Wo': _L2_xattn_in['Wo'], 'L2_ffn_wqkv': _L2_ffn_in['wqkv'], 'L2_ffn_q_scale': _L2_ffn_in['q_scale'], 'L2_ffn_k_scale': _L2_ffn_in['k_scale'], 'L2_ffn_wo': _L2_ffn_in['wo'], 'L2_ffn_ln_g': _L2_ffn_in['ln_g'], 'L2_ffn_ln_b': _L2_ffn_in['ln_b'], 'L2_ffn_w1': _L2_ffn_in['w1'], 'L2_ffn_b1': _L2_ffn_in['b1'], 'L2_ffn_w2': _L2_ffn_in['w2'], 'L2_ffn_b2': _L2_ffn_in['b2'], 'L3_xattn_Wq': _L3_xattn_in['Wq'], 'L3_xattn_bq': _L3_xattn_in['bq'], 'L3_xattn_Wk': _L3_xattn_in['Wk'], 'L3_xattn_bk': _L3_xattn_in['bk'], 'L3_xattn_Wv': _L3_xattn_in['Wv'], 'L3_xattn_bv': _L3_xattn_in['bv'], 'L3_xattn_Wo': _L3_xattn_in['Wo'], 'L3_xattn_bo': _L3_xattn_in['bo'], 'L3_ffn_in_proj_w': _L3_ffn_in['in_proj_w'], 'L3_ffn_in_proj_b': _L3_ffn_in['in_proj_b'], 'L3_ffn_out_proj_w': _L3_ffn_in['out_proj_w'], 'L3_ffn_out_proj_b': _L3_ffn_in['out_proj_b'], 'L3_ffn_ln1_g': _L3_ffn_in['ln1_g'], 'L3_ffn_ln1_b': _L3_ffn_in['ln1_b'], 'L3_ffn_ln2_g': _L3_ffn_in['ln2_g'], 'L3_ffn_ln2_b': _L3_ffn_in['ln2_b'], 'L3_ffn_wg': _L3_ffn_in['wg'], 'L3_ffn_w1': _L3_ffn_in['w1'], 'L3_ffn_b1': _L3_ffn_in['b1'], 'L3_ffn_w2': _L3_ffn_in['w2'], 'L3_ffn_b2': _L3_ffn_in['b2']}

def reference(x, ctx_512, g_xattn, g_ffn, L0_xattn_Wq, L0_xattn_bq, L0_xattn_Wk, L0_xattn_bk, L0_xattn_Wv, L0_xattn_bv, L0_xattn_Wo, L0_xattn_bo, L0_ffn_router_weight, L0_ffn_e_score_bias, L0_ffn_gate_up_proj, L0_ffn_down_proj, L0_ffn_shared_gate_w, L0_ffn_shared_up_w, L0_ffn_shared_down_w, L1_xattn_ln1_g, L1_xattn_ln1_b, L1_xattn_ln2_g, L1_xattn_ln2_b, L1_xattn_a1_wq, L1_xattn_a1_wk, L1_xattn_a1_wv, L1_xattn_a1_li1_w, L1_xattn_a1_li1_b, L1_xattn_a1_lnx_g, L1_xattn_a1_lnx_b, L1_xattn_a1_lny_g, L1_xattn_a1_lny_b, L1_xattn_a1_ln3_g, L1_xattn_a1_ln3_b, L1_xattn_a1_li2_w, L1_xattn_a1_li2_b, L1_xattn_a1_li3_w, L1_xattn_a1_li3_b, L1_xattn_a2_wq, L1_xattn_a2_wk, L1_xattn_a2_wv, L1_xattn_a2_li1_w, L1_xattn_a2_li1_b, L1_xattn_a2_lnx_g, L1_xattn_a2_lnx_b, L1_xattn_a2_lny_g, L1_xattn_a2_lny_b, L1_xattn_a2_ln3_g, L1_xattn_a2_ln3_b, L1_xattn_a2_li2_w, L1_xattn_a2_li2_b, L1_xattn_a2_li3_w, L1_xattn_a2_li3_b, L1_ffn_Wr, L1_ffn_br, L1_ffn_W_up, L1_ffn_b_up, L1_ffn_W_down, L1_ffn_b_down, L2_xattn_Wq, L2_xattn_Wkv, L2_xattn_Wo, L2_ffn_wqkv, L2_ffn_q_scale, L2_ffn_k_scale, L2_ffn_wo, L2_ffn_ln_g, L2_ffn_ln_b, L2_ffn_w1, L2_ffn_b1, L2_ffn_w2, L2_ffn_b2, L3_xattn_Wq, L3_xattn_bq, L3_xattn_Wk, L3_xattn_bk, L3_xattn_Wv, L3_xattn_bv, L3_xattn_Wo, L3_xattn_bo, L3_ffn_in_proj_w, L3_ffn_in_proj_b, L3_ffn_out_proj_w, L3_ffn_out_proj_b, L3_ffn_ln1_g, L3_ffn_ln1_b, L3_ffn_ln2_g, L3_ffn_ln2_b, L3_ffn_wg, L3_ffn_w1, L3_ffn_b1, L3_ffn_w2, L3_ffn_b2):
    import jax
    import jax.numpy as jnp

    def _L0_xattn_ref(q, k, v, Wq, bq, Wk, bk, Wv, bv, Wo, bo):
        import jax, jax.numpy as jnp
        import numpy as np
        HEADS = 16
        D_MODEL = 128
        IMG_MODEL = 64
        D_K = D_MODEL // HEADS
        B, LQ, _ = q.shape
        LKV = k.shape[1]
        qh = (q @ Wq + bq).reshape(B, LQ, HEADS, D_K).transpose(0, 2, 1, 3)
        kh = (k @ Wk + bk).reshape(B, LKV, HEADS, D_K).transpose(0, 2, 1, 3)
        vh = (v @ Wv + bv).reshape(B, LKV, HEADS, D_K).transpose(0, 2, 1, 3)
        scale = 1.0 / np.sqrt(D_K)
        scores = jnp.einsum('bhqd,bhkd->bhqk', qh, kh) * scale
        attn = jax.nn.softmax(scores, axis=-1)
        out = jnp.einsum('bhqk,bhkd->bhqd', attn, vh)
        concat = out.transpose(0, 2, 1, 3).reshape(B, LQ, D_MODEL)
        return concat @ Wo + bo

    def _L0_ffn_ref(hidden_states, router_weight, e_score_bias, gate_up_proj, down_proj, shared_gate_w, shared_up_w, shared_down_w):
        import jax, jax.numpy as jnp
        import numpy as np
        H = 128
        E = 32
        I = 64
        TOP_K = 6
        IS = 128
        NORM_MIN = 1e-12
        B, S = (2, 128)
        b, s, h = hidden_states.shape
        x = hidden_states.reshape(-1, h)
        T = x.shape[0]
        shared_out = jax.nn.silu(x @ shared_gate_w.T) * (x @ shared_up_w.T) @ shared_down_w.T
        xf = x.astype(jnp.float32)
        router_logits = xf @ router_weight.T
        routing_weights = jax.nn.softmax(router_logits, axis=-1)
        corrected = routing_weights + e_score_bias
        _, top_idx = jax.lax.top_k(corrected, TOP_K)
        top_w = jnp.take_along_axis(routing_weights, top_idx, axis=-1)
        top_w = top_w / jnp.clip(top_w.sum(axis=-1, keepdims=True), NORM_MIN)
        top_w = top_w.astype(x.dtype)
        combine = jnp.zeros((T, E), x.dtype).at[jnp.arange(T)[:, None], top_idx].add(top_w)
        gu = jnp.einsum('th,eih->tei', x, gate_up_proj)
        gate, up = jnp.split(gu, 2, axis=-1)
        hmid = jax.nn.silu(gate) * up
        y = jnp.einsum('tei,ehi->teh', hmid, down_proj)
        out = jnp.einsum('teh,te->th', y, combine) + shared_out
        return out.reshape(b, s, h)

    def _L1_xattn_ref(xx, ee, ln1_g, ln1_b, ln2_g, ln2_b, a1_wq, a1_wk, a1_wv, a1_li1_w, a1_li1_b, a1_lnx_g, a1_lnx_b, a1_lny_g, a1_lny_b, a1_ln3_g, a1_ln3_b, a1_li2_w, a1_li2_b, a1_li3_w, a1_li3_b, a2_wq, a2_wk, a2_wv, a2_li1_w, a2_li1_b, a2_lnx_g, a2_lnx_b, a2_lny_g, a2_lny_b, a2_ln3_g, a2_ln3_b, a2_li2_w, a2_li2_b, a2_li3_w, a2_li3_b, training):
        import jax, jax.numpy as jnp
        import numpy as np
        H, D, C1, C2, S, M, B, W = (16, 32, 128, 64, 256, 64, 2, 4)

        def _ln(x, g, b):
            m = jnp.mean(x, -1, keepdims=True)
            v = jnp.var(x, -1, keepdims=True)
            return (x - m) * jax.lax.rsqrt(v + 1e-05) * g + b

        def _mha(x, y, wq, wk, wv, li1_w, li1_b, lnx_g, lnx_b, lny_g, lny_b, ln3_g, ln3_b, li2_w, li2_b, li3_w, li3_b, causal):
            xn = _ln(x, lnx_g, lnx_b)
            yn = _ln(y, lny_g, lny_b)
            q = jnp.einsum('bsc,hcd->bhsd', xn, wq)
            k = jnp.einsum('btc,hcd->bhtd', yn, wk)
            v = jnp.einsum('btc,hcd->bhtd', yn, wv)
            a = jax.nn.softmax(jnp.einsum('bhsd,bhtd->bhst', q, k) * D ** (-0.5), axis=-1)
            if causal:
                s, t = (a.shape[-2], a.shape[-1])
                mask = (jnp.arange(t)[None, :] > jnp.arange(s)[:, None]).astype(a.dtype)
                a = a * mask
            o = jnp.einsum('bhst,bhtd->bhsd', a, v)
            o = o.transpose(0, 2, 1, 3).reshape(x.shape[0], x.shape[1], H * D)
            x_out = x + o @ li1_w + li1_b
            h = jax.nn.gelu(_ln(x_out, ln3_g, ln3_b) @ li2_w + li2_b, approximate=False)
            return x_out + h @ li3_w + li3_b
        x = _ln(xx, ln1_g, ln1_b)
        x = x + _mha(x, x, a1_wq, a1_wk, a1_wv, a1_li1_w, a1_li1_b, a1_lnx_g, a1_lnx_b, a1_lny_g, a1_lny_b, a1_ln3_g, a1_ln3_b, a1_li2_w, a1_li2_b, a1_li3_w, a1_li3_b, causal=True)
        x = _ln(x, ln2_g, ln2_b)
        return x + _mha(x, ee, a2_wq, a2_wk, a2_wv, a2_li1_w, a2_li1_b, a2_lnx_g, a2_lnx_b, a2_lny_g, a2_lny_b, a2_ln3_g, a2_ln3_b, a2_li2_w, a2_li2_b, a2_li3_w, a2_li3_b, causal=False)

    def _L1_ffn_ref(x, Wr, br, W_up, b_up, W_down, b_down):
        import jax, jax.numpy as jnp
        import numpy as np
        B, S, H = (4, 256, 128)
        E = 8
        GS = 2
        NG = E // GS
        F = int(H * 4 * (2.0 / 3.0))
        b, s, h = x.shape
        n_tok = b * s
        k = n_tok // E
        xf = x.reshape(n_tok, h)
        logits = xf @ Wr + br
        Sm = jax.nn.softmax(logits, axis=-1)
        G_t, idx_t = jax.lax.top_k(Sm.T, k)
        G = G_t.T
        idx = idx_t.T
        tokens = xf[idx]
        group = jnp.arange(E) // GS
        Wu = W_up[group]
        bu = b_up[group]
        mid = jax.nn.silu(jnp.einsum('keh,ehf->kef', tokens, Wu) + bu)
        out = jnp.einsum('kef,efh->keh', mid, W_down) + b_down
        y = jnp.zeros_like(xf).at[idx].add(G[..., None] * out)
        return y.reshape(b, s, h)

    def _L2_xattn_ref(x, z, Wq, Wkv, Wo):
        import jax, jax.numpy as jnp
        import numpy as np
        DIM = 128
        LATENT_DIM = 64
        NUM_HEADS = 16
        HEAD_DIM = DIM // NUM_HEADS
        SCALE = HEAD_DIM ** (-0.5)
        B, xN, _ = x.shape
        _, zN, _ = z.shape
        Q = (x @ Wq.T).reshape(B, xN, NUM_HEADS, HEAD_DIM)
        KV = (z @ Wkv.T).reshape(B, zN, 2, NUM_HEADS, HEAD_DIM)
        K = KV[:, :, 0]
        V = KV[:, :, 1]
        attn = jnp.einsum('bqhd,bkhd->bhqk', Q, K) * SCALE
        attn = jax.nn.softmax(attn, axis=-1)
        O = jnp.einsum('bhqk,bkhd->bqhd', attn, V).reshape(B, xN, DIM)
        return O @ Wo.T

    def _L2_ffn_ref(x, wqkv, q_scale, k_scale, wo, ln_g, ln_b, w1, b1, w2, b2):
        import jax, jax.numpy as jnp
        import numpy as np
        DIM = 128
        DEPTH = 2
        HEADS = 8
        DIM_HEAD = 64
        WINDOW = 64
        INNER = HEADS * DIM_HEAD
        HID = int(DIM * 4 * 2 / 3)
        B, N = (2, 1024)
        QK_SCALE = 8.0

        def shift_token(t):
            t1, t2 = jnp.split(t, 2, axis=-1)
            t2 = jnp.pad(t2, ((0, 0), (1, 0), (0, 0)))[:, :-1]
            return jnp.concatenate([t1, t2], axis=-1)

        def l2norm(t):
            return t / jnp.clip(jnp.linalg.norm(t, axis=-1, keepdims=True), 1e-12)

        def rotate_half(x):
            x1, x2 = jnp.split(x, 2, axis=-1)
            return jnp.concatenate([-x2, x1], axis=-1)

        def rotary_xpos(q, k):
            n = q.shape[-2]
            half_idx = jnp.arange(0, DIM_HEAD, 2, dtype=jnp.float32)
            inv_freq = 1.0 / 10000.0 ** (half_idx / DIM_HEAD)
            t = jnp.arange(n, dtype=jnp.float32)
            freqs = t[:, None] * inv_freq[None, :]
            freqs = jnp.concatenate([freqs, freqs], axis=-1)
            base = (half_idx + 0.4 * DIM_HEAD) / (1.4 * DIM_HEAD)
            power = (t - n // 2) / float(WINDOW // 2)
            scale = base[None, :] ** power[:, None]
            scale = jnp.concatenate([scale, scale], axis=-1)
            cos, sin = (jnp.cos(freqs), jnp.sin(freqs))
            q = q * cos * scale + rotate_half(q) * sin * scale
            k = k * cos / scale + rotate_half(k) * sin / scale
            return (q, k)

        def local_attention(q, k, v):
            b, h, n, d = q.shape
            w = n // WINDOW
            bq = q.reshape(b, h, w, WINDOW, d) * QK_SCALE
            bk = k.reshape(b, h, w, WINDOW, d)
            bv = v.reshape(b, h, w, WINDOW, d)

            def look_around(t):
                p = jnp.pad(t, ((0, 0), (0, 0), (1, 0), (0, 0), (0, 0)))
                return jnp.concatenate([p[:, :, :w], p[:, :, 1:]], axis=3)
            bk, bv = (look_around(bk), look_around(bv))
            bt = jnp.arange(n).reshape(w, WINDOW)
            btp = jnp.pad(bt, ((1, 0), (0, 0)), constant_values=-1)
            btk = jnp.concatenate([btp[:w], btp[1:]], axis=1)
            sim = jnp.einsum('bhwid,bhwjd->bhwij', bq, bk)
            i = bt[:, :, None]
            j = btk[:, None, :]
            mask = (i < j) | (i > j + WINDOW) | (j == -1)
            sim = jnp.where(mask, -jnp.finfo(sim.dtype).max, sim)
            attn = jax.nn.softmax(sim, axis=-1)
            out = jnp.einsum('bhwij,bhwjd->bhwid', attn, bv)
            return out.reshape(b, h, n, d)

        def _layer(x, wqkv, qs, ksc, wo, lg, lb, w1, b1, w2, b2):
            b, n, _ = x.shape
            h = shift_token(x)
            qkv = h @ wqkv
            q, k, v = jnp.split(qkv, 3, axis=-1)
            to_heads = lambda t: t.reshape(b, n, HEADS, DIM_HEAD).transpose(0, 2, 1, 3)
            q, k, v = (to_heads(q), to_heads(k), to_heads(v))
            q = l2norm(q) * qs
            k = l2norm(k) * ksc
            q, k = rotary_xpos(q, k)
            o = local_attention(q, k, v)
            o = o.transpose(0, 2, 1, 3).reshape(b, n, INNER)
            x = x + o @ wo
            h = shift_token(x)
            mu = h.mean(-1, keepdims=True)
            var = h.var(-1, keepdims=True)
            h = (h - mu) / jnp.sqrt(var + 1e-05) * lg + lb
            h = h @ w1 + b1
            a, g = jnp.split(h, 2, axis=-1)
            h = a * jax.nn.gelu(g, approximate=False)
            x = x + h @ w2 + b2
            return x
        for l in range(DEPTH):
            x = _layer(x, wqkv[l], q_scale[l], k_scale[l], wo[l], ln_g[l], ln_b[l], w1[l], b1[l], w2[l], b2[l])
        return x

    def _L3_xattn_ref(q, k, v, Wq, bq, Wk, bk, Wv, bv, Wo, bo):
        import jax, jax.numpy as jnp
        import numpy as np
        HEADS = 16
        D_MODEL = 128
        IMG_MODEL = 64
        D_K = D_MODEL // HEADS
        B, LQ, _ = q.shape
        LKV = k.shape[1]
        qh = (q @ Wq + bq).reshape(B, LQ, HEADS, D_K).transpose(0, 2, 1, 3)
        kh = (k @ Wk + bk).reshape(B, LKV, HEADS, D_K).transpose(0, 2, 1, 3)
        vh = (v @ Wv + bv).reshape(B, LKV, HEADS, D_K).transpose(0, 2, 1, 3)
        scale = 1.0 / np.sqrt(D_K)
        scores = jnp.einsum('bhqd,bhkd->bhqk', qh, kh) * scale
        attn = jax.nn.softmax(scores, axis=-1)
        out = jnp.einsum('bhqk,bhkd->bhqd', attn, vh)
        concat = out.transpose(0, 2, 1, 3).reshape(B, LQ, D_MODEL)
        return concat @ Wo + bo

    def _L3_ffn_ref(x, in_proj_w, in_proj_b, out_proj_w, out_proj_b, ln1_g, ln1_b, ln2_g, ln2_b, wg, w1, b1, w2, b2):
        import jax, jax.numpy as jnp
        import numpy as np
        D = 128
        H = 4
        HD = D // H
        E = 8
        FF = 512
        CAP_FACTOR = 1.0

        def _ln(x, g, b, eps=1e-05):
            mu = jnp.mean(x, -1, keepdims=True)
            v = jnp.mean((x - mu) ** 2, -1, keepdims=True)
            return (x - mu) * jax.lax.rsqrt(v + eps) * g + b

        def _mha(x, w, b, ow, ob):
            L, N, _ = x.shape
            qkv = x @ w.T + b
            q, k, v = jnp.split(qkv, 3, axis=-1)
            rh = lambda t: t.reshape(L, N, H, HD).transpose(1, 2, 0, 3)
            q, k, v = (rh(q), rh(k), rh(v))
            scores = jnp.einsum('nhld,nhmd->nhlm', q, k) / np.float32(np.sqrt(HD))
            attn = jax.nn.softmax(scores, axis=-1)
            o = jnp.einsum('nhlm,nhmd->nhld', attn, v).transpose(2, 0, 1, 3).reshape(L, N, D)
            return o @ ow.T + ob

        def _moe(x, wg, w1, b1, w2, b2):
            L, N, _ = x.shape
            S = L * N
            cap = int(CAP_FACTOR * S) // E
            xf = x.reshape(S, D)
            gates = jax.nn.softmax(xf @ wg, axis=-1)
            idx = jnp.argmax(gates, axis=-1)
            mask1 = jax.nn.one_hot(idx, E, dtype=x.dtype)
            loc = jnp.sum((jnp.cumsum(mask1, 0) - 1.0) * mask1, -1).astype(jnp.int32)
            keep = loc < cap
            gate_val = jnp.take_along_axis(gates, idx[:, None], -1)[:, 0]
            slot = jnp.where(keep, idx.astype(jnp.int32) * cap + loc, E * cap)
            disp = jnp.zeros((E * cap, D), x.dtype).at[slot].set(xf, mode='drop')
            disp = disp.reshape(E, cap, D)
            h = jnp.einsum('ecd,edf->ecf', disp, w1) + b1[:, None, :]
            y = (jnp.einsum('ecf,efd->ecd', h, w2) + b2[:, None, :]).reshape(E * cap, D)
            out = jnp.where(keep[:, None], gate_val[:, None] * y[jnp.minimum(slot, E * cap - 1)], 0.0)
            return out.reshape(L, N, D)
        y1 = _ln(x + _mha(x, in_proj_w, in_proj_b, out_proj_w, out_proj_b), ln1_g, ln1_b)
        y2 = _ln(y1 + _moe(y1, wg, w1, b1, w2, b2), ln2_g, ln2_b)
        return y2
    x = x + jnp.tanh(g_xattn[0]) * _L0_xattn_ref(_layernorm(x, axis=-1), ctx_512, ctx_512, L0_xattn_Wq, L0_xattn_bq, L0_xattn_Wk, L0_xattn_bk, L0_xattn_Wv, L0_xattn_bv, L0_xattn_Wo, L0_xattn_bo)
    x = x + jnp.tanh(g_ffn[0]) * _L0_ffn_ref(_layernorm(x, axis=-1), L0_ffn_router_weight, L0_ffn_e_score_bias, L0_ffn_gate_up_proj, L0_ffn_down_proj, L0_ffn_shared_gate_w, L0_ffn_shared_up_w, L0_ffn_shared_down_w)
    x = x + jnp.tanh(g_xattn[1]) * _L1_xattn_ref(_layernorm(x, axis=-1), ctx_512, L1_xattn_ln1_g, L1_xattn_ln1_b, L1_xattn_ln2_g, L1_xattn_ln2_b, L1_xattn_a1_wq, L1_xattn_a1_wk, L1_xattn_a1_wv, L1_xattn_a1_li1_w, L1_xattn_a1_li1_b, L1_xattn_a1_lnx_g, L1_xattn_a1_lnx_b, L1_xattn_a1_lny_g, L1_xattn_a1_lny_b, L1_xattn_a1_ln3_g, L1_xattn_a1_ln3_b, L1_xattn_a1_li2_w, L1_xattn_a1_li2_b, L1_xattn_a1_li3_w, L1_xattn_a1_li3_b, L1_xattn_a2_wq, L1_xattn_a2_wk, L1_xattn_a2_wv, L1_xattn_a2_li1_w, L1_xattn_a2_li1_b, L1_xattn_a2_lnx_g, L1_xattn_a2_lnx_b, L1_xattn_a2_lny_g, L1_xattn_a2_lny_b, L1_xattn_a2_ln3_g, L1_xattn_a2_ln3_b, L1_xattn_a2_li2_w, L1_xattn_a2_li2_b, L1_xattn_a2_li3_w, L1_xattn_a2_li3_b, 0)
    x = x + jnp.tanh(g_ffn[1]) * _L1_ffn_ref(_layernorm(x, axis=-1), L1_ffn_Wr, L1_ffn_br, L1_ffn_W_up, L1_ffn_b_up, L1_ffn_W_down, L1_ffn_b_down)
    x = x + jnp.tanh(g_xattn[2]) * _L2_xattn_ref(_layernorm(x, axis=-1), ctx_512, L2_xattn_Wq, L2_xattn_Wkv, L2_xattn_Wo)
    x = x + jnp.tanh(g_ffn[2]) * _L2_ffn_ref(_layernorm(x, axis=-1), L2_ffn_wqkv, L2_ffn_q_scale, L2_ffn_k_scale, L2_ffn_wo, L2_ffn_ln_g, L2_ffn_ln_b, L2_ffn_w1, L2_ffn_b1, L2_ffn_w2, L2_ffn_b2)
    x = x + jnp.tanh(g_xattn[3]) * _L3_xattn_ref(_layernorm(x, axis=-1), ctx_512, ctx_512, L3_xattn_Wq, L3_xattn_bq, L3_xattn_Wk, L3_xattn_bk, L3_xattn_Wv, L3_xattn_bv, L3_xattn_Wo, L3_xattn_bo)
    x = x + jnp.tanh(g_ffn[3]) * _L3_ffn_ref(_layernorm(x, axis=-1), L3_ffn_in_proj_w, L3_ffn_in_proj_b, L3_ffn_out_proj_w, L3_ffn_out_proj_b, L3_ffn_ln1_g, L3_ffn_ln1_b, L3_ffn_ln2_g, L3_ffn_ln2_b, L3_ffn_wg, L3_ffn_w1, L3_ffn_b1, L3_ffn_w2, L3_ffn_b2)
    return x

_drawn_inputs = setup_inputs


def setup_inputs(seed=0):
    import zlib

    import numpy as np

    out = dict(_drawn_inputs(seed))
    spreads = {'L0_xattn_bq': (0.0, 0.448),
     'L0_xattn_bk': (0.0, 0.8),
     'L0_xattn_bv': (0.0, 0.1),
     'L0_xattn_bo': (0.0, 0.1),
     'L0_ffn_e_score_bias': (0.0, 0.8),
     'L1_xattn_ln1_g': (1.0, 0.2),
     'L1_xattn_ln1_b': (0.0, 0.1),
     'L1_xattn_ln2_g': (1.0, 0.2),
     'L1_xattn_ln2_b': (0.0, 0.1),
     'L1_xattn_a1_li1_b': (0.0, 0.1),
     'L1_xattn_a1_lnx_g': (1.0, 0.6),
     'L1_xattn_a1_lnx_b': (0.0, 0.8),
     'L1_xattn_a1_lny_g': (1.0, 0.6),
     'L1_xattn_a1_lny_b': (0.0, 0.8),
     'L1_xattn_a1_ln3_g': (1.0, 0.6),
     'L1_xattn_a1_ln3_b': (0.0, 0.8),
     'L1_xattn_a1_li2_b': (0.0, 0.472),
     'L1_xattn_a1_li3_b': (0.0, 0.1),
     'L1_xattn_a2_li1_b': (0.0, 0.1),
     'L1_xattn_a2_lnx_g': (1.0, 0.6),
     'L1_xattn_a2_lnx_b': (0.0, 0.8),
     'L1_xattn_a2_lny_g': (1.0, 0.6),
     'L1_xattn_a2_lny_b': (0.0, 0.8),
     'L1_xattn_a2_ln3_g': (1.0, 0.6),
     'L1_xattn_a2_ln3_b': (0.0, 0.8),
     'L1_xattn_a2_li2_b': (0.0, 0.451),
     'L1_xattn_a2_li3_b': (0.0, 0.1),
     'L1_ffn_br': (0.0, 0.449),
     'L2_ffn_q_scale': (1.0, 0.6),
     'L2_ffn_k_scale': (1.0, 0.6),
     'L2_ffn_ln_g': (1.0, 0.6),
     'L2_ffn_ln_b': (0.0, 0.8),
     'L2_ffn_b1': (0.0, 0.587),
     'L2_ffn_b2': (0.0, 0.1),
     'L3_xattn_bq': (0.0, 0.1),
     'L3_xattn_bk': (0.0, 0.8),
     'L3_xattn_bv': (0.0, 0.1),
     'L3_xattn_bo': (0.0, 0.1),
     'L3_ffn_in_proj_b': (0.0, 0.53),
     'L3_ffn_out_proj_b': (0.0, 0.1),
     'L3_ffn_ln1_g': (1.0, 0.2),
     'L3_ffn_ln1_b': (0.0, 0.1),
     'L3_ffn_ln2_g': (1.0, 0.2),
     'L3_ffn_ln2_b': (0.0, 0.1),
     'L3_ffn_b1': (0.0, 0.8),
     'L3_ffn_b2': (0.0, 0.8)}
    factors = {'L0_ffn_router_weight': 8.0,
     'L0_ffn_gate_up_proj': 8.0,
     'L0_ffn_down_proj': 8.0,
     'L0_ffn_shared_gate_w': 8.0,
     'L0_ffn_shared_up_w': 8.0,
     'L0_ffn_shared_down_w': 8.0,
     'L1_xattn_a1_wq': 8.0,
     'L1_xattn_a1_wk': 8.0,
     'L1_xattn_a1_wv': 3.146,
     'L1_xattn_a1_li1_w': 3.17,
     'L1_xattn_a2_wq': 8.0,
     'L1_xattn_a2_wk': 8.0,
     'L1_ffn_b_up': 8.0,
     'L1_ffn_b_down': 8.0,
     'L3_ffn_in_proj_w': 6.33,
     'L3_ffn_out_proj_w': 3.219,
     'L3_ffn_wg': 4.919,
     'L3_ffn_w1': 6.527,
     'L3_ffn_w2': 6.015}
    for name, (base, spread) in spreads.items():
        noise = np.random.default_rng([zlib.crc32(name.encode()), seed]).standard_normal(out[name].shape)
        drawn = base * np.exp(spread * noise) if base else spread * noise
        out[name] = jnp.asarray(drawn.astype(out[name].dtype))
    for name, factor in factors.items():
        out[name] = (out[name] * factor).astype(out[name].dtype)
    return out
```

```python
from contextlib import ExitStack, contextmanager

import numpy as np

import concourse.bass as bass
from concourse import mybir

ALU = mybir.AluOpType
ACT = mybir.ActivationFunctionType
AX = mybir.AxisListType
F32 = mybir.dt.float32
I32 = mybir.dt.int32

P = 128
TILES = 32
D = 128
CTX = 64
TOKENS = TILES * P
BANK = 512
EPS = 1e-5


@contextmanager
def stage(nc, names):
    semaphores = {name: nc.alloc_semaphore(nc.get_next_instruction_name() + name) for name in names.split()}
    with nc.Block() as block:
        yield block, semaphores
    nc.clear_and_free_semaphores(list(semaphores.values()))
    nc.all_engine_barrier()


@contextmanager
def memory(nc):
    with ExitStack() as held:
        def sb(name, shape, dtype=F32):
            return held.enter_context(nc.sbuf_tensor(nc.get_next_instruction_name() + name, shape, dtype))

        def ps(name, shape):
            return held.enter_context(nc.psum_tensor(nc.get_next_instruction_name() + name, shape, F32))

        yield sb, ps


def tile_cols(tensor, t, n=1):
    return tensor[:, bass.ds(t * P, n * P)]


def spread(ap, shape):
    return ap.to_broadcast(shape)



def layer_norm(nc, const, src, width=D, t_outs=(), row_out=None, row_affine=None, loads=(), normalize=True):
    second = len(t_outs) > 1
    turned_out = bool(t_outs)
    with memory(nc) as (sb, ps):
        stats = sb("stats", [P, TILES, 6])
        work = sb("work", [P, 4, TILES])
        std = sb("std", [P, TILES])
        mean = sb("mean", [P, TILES])
        rstd = sb("rstd", [P, TILES])
        xn = sb("xn", [P, 8, D])
        scaled = sb("scaled", [P, 8, width])
        bank = ps("turned", [P, 2, BANK])
        with stage(nc, "loaded stats_done chain std_ready xn_ready turned first_copied second_copied "
                       "row_scaled row_done padded") as (block, s):

            @block.sync
            def _(sp):
                for dst, source in loads:
                    sp.dma_start(dst, source).then_inc(s["loaded"], 16)
                if loads:
                    sp.wait_ge(s["loaded"], 16 * len(loads))

            @block.vector
            def _(dve):
                if normalize:
                    with dve.Fori(0, TILES // 8) as it:
                        for u in range(8):
                            nc.vector.bn_stats(stats[:, bass.ds(it * 8 + u, 1), :],
                                               src[:, bass.ds(it * 8 + u, 1), :]).then_inc(s["stats_done"], 1)
                    dve.wait_ge(s["stats_done"], TILES)
                    nc.vector.tensor_tensor(work[:, 0, :], stats[:, :, 1], stats[:, :, 4], ALU.add).then_inc(s["chain"], 1)
                    nc.vector.tensor_tensor(work[:, 1, :], stats[:, :, 1], stats[:, :, 4],
                                            ALU.subtract).then_inc(s["chain"], 1)
                    nc.vector.tensor_tensor(work[:, 2, :], stats[:, :, 2], stats[:, :, 5], ALU.add).then_inc(s["chain"], 1)
                    dve.wait_ge(s["chain"], 3)
                    nc.vector.tensor_scalar(mean[:], work[:, 0, :], 0.5, None, ALU.mult).then_inc(s["chain"], 1)
                    nc.vector.tensor_tensor(work[:, 3, :], work[:, 1, :], work[:, 1, :], ALU.mult).then_inc(s["chain"], 1)
                    dve.wait_ge(s["chain"], 5)
                    nc.vector.scalar_tensor_tensor(out=work[:, 0, :], in0=work[:, 3, :], scalar=width / 4.0,
                                                   in1=work[:, 2, :], op0=ALU.mult, op1=ALU.add).then_inc(s["chain"], 1)
                    dve.wait_ge(s["std_ready"], 1)
                    nc.vector.reciprocal(rstd[:], std[:]).then_inc(s["chain"], 1)
                    dve.wait_ge(s["chain"], 7)
                if width < D:
                    dve.wait_ge(s["padded"], 1)
                with dve.Fori(0, TILES // 8) as it:
                    for half in range(2):
                        bank_no = it * 2 + half
                        if turned_out:
                            dve.wait_ge(s["turned"], bank_no + 1)
                        if row_out is not None:
                            dve.wait_ge(s["row_done"], bank_no + 1)
                        for k in range(4):
                            u = half * 4 + k
                            t = it * 8 + u
                            if normalize:
                                ins = nc.vector.tensor_scalar(xn[:, u:u + 1, 0:width], src[:, bass.ds(t, 1), :],
                                                              mean[:, bass.ds(t, 1)], rstd[:, bass.ds(t, 1)],
                                                              ALU.subtract, ALU.mult)
                            else:
                                ins = nc.vector.tensor_copy(xn[:, u:u + 1, 0:width], src[:, bass.ds(t, 1), :])
                            ins.then_inc(s["xn_ready"], 1)
                    if second:
                        for half in range(2):
                            bank_no = it * 2 + half
                            dst, gain, shift = t_outs[1]
                            dve.wait_ge(s["first_copied"], bank_no + 3)
                            nc.vector.tensor_scalar(dst[0:width, bass.ds(bank_no * BANK, BANK)],
                                                    bank[0:width, half, :], gain, shift,
                                                    ALU.mult, ALU.add).then_inc(s["second_copied"], 1)

            @block.tensor
            def _(pe):
                if not turned_out:
                    return
                pe.sem_inc(s["turned"], 2)
                with pe.Fori(0, TILES // 8) as it:
                    for half in range(2):
                        bank_no = it * 2 + half
                        pe.wait_ge(s["first_copied"], bank_no + 1)
                        if second:
                            pe.wait_ge(s["second_copied"], bank_no + 1)
                        pe.wait_ge(s["xn_ready"], bank_no * 4 + 4)
                        for k in range(4):
                            last = nc.tensor.transpose(bank[:, half, k * P:(k + 1) * P],
                                                       xn[:, half * 4 + k, :], const["ident"][:])
                        last.then_inc(s["turned"], 1)

            @block.scalar
            def _(act):
                act.sem_inc(s["first_copied"], 2)
                act.sem_inc(s["second_copied"], 2)
                if normalize:
                    act.wait_ge(s["chain"], 6)
                    nc.scalar.activation(std[:], work[:, 0, :], ACT.Sqrt, bias=const["eps"][:, 0:1],
                                         scale=1.0 / width).then_inc(s["std_ready"], 1)
                if not turned_out:
                    return
                dst, gain, shift = t_outs[0]
                with act.Fori(0, TILES // 8) as it:
                    for half in range(2):
                        bank_no = it * 2 + half
                        act.wait_ge(s["turned"], bank_no + 3)
                        out = dst[0:width, bass.ds(bank_no * BANK, BANK)]
                        if gain is None:
                            ins = nc.scalar.activation(out, bank[0:width, half, :], ACT.Copy)
                        else:
                            ins = nc.scalar.activation(out, bank[0:width, half, :], ACT.Identity,
                                                       bias=shift, scale=gain)
                        ins.then_inc(s["first_copied"], 1)

            @block.gpsimd
            def _(pool):
                if width < D:
                    nc.gpsimd.memset(xn[:], 0.0).then_inc(s["padded"], 1)
                if row_out is None:
                    return
                pool.sem_inc(s["row_done"], 2)
                with pool.Fori(0, TILES // 8) as it:
                    for half in range(2):
                        bank_no = it * 2 + half
                        dst = row_out[:, bass.ds(bank_no * 4, 4), :]
                        xs, rs = xn[:, half * 4:half * 4 + 4, 0:width], scaled[:, half * 4:half * 4 + 4, :]
                        pool.wait_ge(s["xn_ready"], bank_no * 4 + 4)
                        if row_affine is None:
                            nc.gpsimd.tensor_copy(dst, xs).then_inc(s["row_done"], 1)
                        else:
                            gain, shift = row_affine
                            nc.gpsimd.tensor_tensor(rs, xs, spread(gain[:, None, :], [P, 4, width]),
                                                    ALU.mult).then_inc(s["row_scaled"], 1)
                            pool.wait_ge(s["row_scaled"], bank_no + 1)
                            nc.gpsimd.tensor_tensor(dst, rs, spread(shift[:, None, :], [P, 4, width]),
                                                    ALU.add).then_inc(s["row_done"], 1)



def attention(nc, const, *, heads, dk, groups, kv_rows, q_src, kv_src, wq, wk, wv, scale,
              q_bias=None, k_bias=None, v_bias=None, add_mask=None, keep_mask=None, rotary=None,
              wo=None, o_bias=None, gate=None, resid=None, out=None, turned_out=None):
    slots = heads // groups
    row_step = P // slots
    width = groups * P
    inner = heads * dk
    chunks = inner // P
    v_cols = dk if keep_mask is not None else dk + 1
    per_bank = heads // 2
    with memory(nc) as (sb, ps):
        qt = sb("qt", [P, width])
        kt = sb("kt", [P, width])
        kv_tile = sb("kv_tile", [kv_rows, 2, P])
        v = sb("v", [P, 2, heads, dk + 1])
        probs = sb("probs", [P, 2, width])
        kept = sb("kept", [P, 2, width]) if keep_mask is not None else probs
        probs_t = sb("probs_t", [P, 2, width])
        maxes = sb("maxes", [P, 2, groups])
        sums = sb("sums", [P, heads])
        inv = sb("inv", [P, heads])
        o = sb("o", [P, inner])
        ot = sb("ot", [P, inner])
        if rotary is not None:
            same = sb("same", [P, 2, heads, dk])
            swap = sb("swap", [P, 2, heads, dk])
            square = sb("square", [P, 2, heads, dk])
            length = sb("length", [P, 2, heads])
            length_c = sb("length_c", [P, 2, heads])
            inv_len = sb("inv_len", [P, 2, heads])
            minus_half = sb("minus_half", [P, heads])
            added = sb("added", [P, 2, heads, dk])
            turned_rows = sb("turned_rows", [P, 2, heads, dk])
        p0 = ps("p0", [P, BANK])
        p1 = ps("p1", [P, BANK])
        sc = ps("sc", [P, 2, BANK])
        tp = ps("tp", [P, 2, BANK])
        ov = ps("ov", [P, 2, BANK])
        ov_heads = ov[:, :, 0:per_bank * v_cols].rearrange("p a (h c) -> p a h c", c=v_cols)

        def v_out(h):
            return ov[:, h // per_bank, (h % per_bank) * v_cols:(h % per_bank + 1) * v_cols]

        with stage(nc, "const_ready kv_copied q_done k_done v_done q_copied k_copied v_copied scores_ready "
                       "max_ready scores_used probs_ready kept_ready probs_turned probs_t_ready weighed "
                       "inv_ready o_ready o_turned ot_copied y_done y_used sums_ready squared summed "
                       "clamped inv_len_ready rotated added_ready rows_ready") as (block, s):

            @block.tensor
            def _(pe):
                def project(t, u, first=False):
                    if wo is not None:
                        pe.wait_ge(s["y_used"], t + 1)
                    elif not first:
                        pe.wait_ge(s["v_copied"], t)
                    if rotary is None:
                        for g in range(groups):
                            last = nc.tensor.matmul(p0[:, g * P:(g + 1) * P], wq[:, g * P:(g + 1) * P], q_src(t),
                                                    start=True, stop=True)
                        last.then_inc(s["q_done"], 1)
                        pe.wait_ge(s["ot_copied"], t + 1)
                        for g in range(groups):
                            last = nc.tensor.matmul(p1[:, g * P:(g + 1) * P], wk[:, g * P:(g + 1) * P], kv_src(t),
                                                    start=True, stop=True)
                        last.then_inc(s["k_done"], 1)
                        pe.wait_ge(s["kv_copied"], t + 1)
                        pe.wait_ge(s["q_copied"], t + 1)
                    else:
                        pe.wait_ge(s["kv_copied"], t + 1)
                        nc.tensor.matmul(p0[:, 0:inner], kv_tile[:, u, :], wq, start=True,
                                         stop=True).then_inc(s["q_done"], 1)
                        pe.wait_ge(s["ot_copied"], t + 1)
                        nc.tensor.matmul(p1[:, 0:inner], kv_tile[:, u, :], wk, start=True,
                                         stop=True).then_inc(s["k_done"], 1)
                        pe.wait_ge(s["rotated"], 6 * t + 3)
                        pe.wait_ge(s["squared"], 2 * t + 1)
                    last = nc.tensor.matmul(p0[:, 0:inner], kv_tile[:, u, :], wv, start=True, stop=v_bias is None)
                    if v_bias is not None:
                        last = nc.tensor.matmul(p0[:, 0:inner], const["ones"][0:1, :], v_bias, start=False, stop=True)
                    last.then_inc(s["v_done"], 1)

                def turn_rows(t):
                    if rotary is None:
                        return
                    pe.wait_ge(s["rotated"], 6 * t + 6)
                    pe.wait_ge(s["squared"], 2 * t + 2)
                    pe.wait_ge(s["rows_ready"], 2 * t + 1)
                    flat = turned_rows[:, 0, :, :].rearrange("p h c -> p (h c)")
                    for g in range(groups):
                        last = nc.tensor.transpose(p1[:, g * P:(g + 1) * P], flat[:, g * P:(g + 1) * P], const["ident"][:])
                    last.then_inc(s["q_done"], 1)
                    pe.wait_ge(s["rows_ready"], 2 * t + 2)
                    pe.wait_ge(s["v_copied"], t + 1)
                    flat = turned_rows[:, 1, :, :].rearrange("p h c -> p (h c)")
                    for g in range(groups):
                        last = nc.tensor.transpose(p0[:, g * P:(g + 1) * P], flat[:, g * P:(g + 1) * P], const["ident"][:])
                    last.then_inc(s["k_done"], 1)

                def scores(t, j):
                    n = t * slots + j
                    if j == 0:
                        pe.wait_ge(s["q_copied"], t + 1)
                        pe.wait_ge(s["k_copied"], t + 1)
                    pe.wait_ge(s["scores_used"], n + 1)
                    if add_mask is not None:
                        nc.tensor.matmul(sc[:, j % 2, 0:width], const["ident"][:], add_mask, start=True, stop=False,
                                         skip_group_check=True)
                    rows = slice(j * row_step, j * row_step + dk)
                    for g in range(groups):
                        last = nc.tensor.matmul(sc[:, j % 2, g * P:(g + 1) * P], qt[rows, g * P:(g + 1) * P],
                                                kt[rows, g * P:(g + 1) * P], start=add_mask is None, stop=True,
                                                skip_group_check=add_mask is not None)
                    last.then_inc(s["scores_ready"], 1)

                def turn_probs(t, j):
                    n = t * slots + j
                    if keep_mask is None:
                        pe.wait_ge(s["probs_ready"], n + 1)
                    else:
                        pe.wait_ge(s["kept_ready"], n + 3)
                    pe.wait_ge(s["probs_t_ready"], n + 1)
                    for g in range(groups):
                        last = nc.tensor.transpose(tp[:, j % 2, g * P:(g + 1) * P],
                                                   kept[:, j % 2, g * P:(g + 1) * P], const["ident"][:])
                    last.then_inc(s["probs_turned"], 1)

                def weigh(t, u, j):
                    n = t * slots + j
                    pe.wait_ge(s["probs_t_ready"], n + 3)
                    if j == 0:
                        pe.wait_ge(s["v_copied"], t + 1)
                        pe.wait_ge(s["o_ready"], t + 1)
                    for g in range(groups):
                        h = g * slots + j
                        last = nc.tensor.matmul(v_out(h), probs_t[:, j % 2, g * P:(g + 1) * P],
                                                v[:, u, h, 0:v_cols], start=True, stop=True)
                    last.then_inc(s["weighed"], 1)

                def finish(t, following):
                    pe.wait_ge(s["o_ready"], t + 2)
                    if following:
                        pe.wait_ge(s["k_copied"] if rotary is None else s["q_copied"], t + 2)
                    for c in range(chunks):
                        last = nc.tensor.transpose(p1[:, c * P:(c + 1) * P], o[:, c * P:(c + 1) * P], const["ident"][:])
                    last.then_inc(s["o_turned"], 1)
                    if wo is None:
                        return
                    pe.wait_ge(s["ot_copied"], t + 3)
                    if following:
                        pe.wait_ge(s["v_copied"] if rotary is None else s["k_copied"], t + 2)
                    for c in range(chunks):
                        last = nc.tensor.matmul(p0[:, 0:D], ot[:, c * P:(c + 1) * P], wo[:, c, :], start=c == 0,
                                                stop=c == chunks - 1 and o_bias is None)
                    if o_bias is not None:
                        last = nc.tensor.matmul(p0[:, 0:D], const["ones"][0:1, :], o_bias, start=False, stop=True)
                    last.then_inc(s["y_done"], 1)

                def pair(it, first, end):
                    for u in range(2):
                        t = it * 2 + u
                        scores(t, 0)
                        scores(t, 1)
                        if not (first and u == 0):
                            finish(t - 1, True)
                        following = not (end and u == 1)
                        if slots == 4:
                            turn_probs(t, 0)
                            scores(t, 2)
                            turn_probs(t, 1)
                            weigh(t, u, 0)
                            scores(t, 3)
                            if following:
                                project(t + 1, 1 - u)
                            turn_probs(t, 2)
                            weigh(t, u, 1)
                            turn_probs(t, 3)
                            weigh(t, u, 2)
                            weigh(t, u, 3)
                        else:
                            if following:
                                project(t + 1, 1 - u)
                            turn_probs(t, 0)
                            turn_probs(t, 1)
                            weigh(t, u, 0)
                            weigh(t, u, 1)
                        if following:
                            turn_rows(t + 1)

                project(0, 0, True)
                turn_rows(0)
                pair(0, True, False)
                with pe.Fori(1, TILES // 2 - 1) as it:
                    pair(it, False, False)
                pair(TILES // 2 - 1, False, True)
                finish(TILES - 1, False)

            @block.vector
            def _(dve):
                def subtract_max(t, j):
                    n = t * slots + j
                    dve.wait_ge(s["scores_ready"], n + 1)
                    scores = sc[:, j % 2, 0:width].rearrange("p (g k) -> p g k", k=P)
                    nc.vector.tensor_reduce(maxes[:, j % 2, :], scores, AX.X, ALU.max).then_inc(s["max_ready"], 1)
                    dve.wait_ge(s["probs_turned"] if keep_mask is None else s["kept_ready"], n + 1)
                    if keep_mask is not None:
                        dve.wait_ge(s["sums_ready"], n + 1)
                    dve.wait_ge(s["max_ready"], n + 1)
                    nc.vector.tensor_tensor(probs[:, j % 2, :].rearrange("p (g k) -> p g k", k=P), scores,
                                            spread(maxes[:, j % 2, :, None], [P, groups, P]),
                                            ALU.subtract).then_inc(s["scores_used"], 1)

                def sum_probs(t, j):
                    if keep_mask is None:
                        return
                    dve.wait_ge(s["probs_ready"], t * slots + j + 1)
                    if j == 0:
                        dve.wait_ge(s["inv_ready"], t + 1)
                    nc.vector.tensor_reduce(sums[:].rearrange("p (g j) -> p g j", j=slots)[:, :, j:j + 1],
                                            probs[:, j % 2, :].rearrange("p (g k) -> p g k", k=P),
                                            AX.X, ALU.add).then_inc(s["sums_ready"], 1)

                def normalise(t):
                    dve.wait_ge(s["weighed"], (t + 1) * slots)
                    inv_heads = inv[:].rearrange("p (a h) -> p a h", a=2)
                    if keep_mask is None:
                        nc.vector.reciprocal(inv_heads[:, :, :, None], ov_heads[:, :, :, dk:dk + 1]).then_inc(s["inv_ready"], 1)
                    else:
                        dve.wait_ge(s["sums_ready"], (t + 1) * slots + 2)
                        nc.vector.reciprocal(inv[:], sums[:]).then_inc(s["inv_ready"], 1)
                    dve.wait_ge(s["inv_ready"], t + 2)
                    dve.wait_ge(s["o_turned"], t + 1)
                    nc.vector.tensor_tensor(o[:].rearrange("p (a h c) -> p a h c", a=2, c=dk), ov_heads[:, :, :, 0:dk],
                                            spread(inv_heads[:, :, :, None], [P, 2, per_bank, dk]),
                                            ALU.mult).then_inc(s["o_ready"], 1)

                def add_residual(t):
                    if wo is None:
                        return
                    dve.wait_ge(s["y_done"], t + 1)
                    rows = resid[:, bass.ds(t, 1), :]
                    if gate is None:
                        ins = nc.vector.tensor_tensor(out[:, bass.ds(t, 1), :], p0[:, None, 0:D], rows, ALU.add)
                    else:
                        ins = nc.vector.scalar_tensor_tensor(out=out[:, bass.ds(t, 1), :], in0=p0[:, None, 0:D],
                                                             scalar=gate, in1=rows, op0=ALU.mult, op1=ALU.add)
                    ins.then_inc(s["y_used"], 1)

                def copy_queries(t):
                    if rotary is not None:
                        return
                    dve.wait_ge(s["q_done"], t + 1)
                    if q_bias is None:
                        ins = nc.vector.tensor_copy(qt[:], p0[:, 0:width])
                    else:
                        ins = nc.vector.tensor_tensor(qt[:].rearrange("p (g n) -> p g n", n=P),
                                                      p0[:, 0:width].rearrange("p (g n) -> p g n", n=P),
                                                      spread(q_bias[:, :, None], [P, groups, P]), ALU.add)
                    ins.then_inc(s["q_copied"], 1)

                def rotate(t):
                    if rotary is None:
                        return
                    half = dk // 2
                    for i, rows, done in ((0, p0, s["q_done"]), (1, p1, s["k_done"])):
                        rows = rows[:, 0:inner].rearrange("p (h c) -> p h c", c=dk)
                        c_same, c_swap = rotary[2 * i], rotary[2 * i + 1]
                        dve.wait_ge(done, 2 * t + 1)
                        dve.wait_ge(s["squared"], 2 * t + i + 1)
                        dve.wait_ge(s["added_ready"], 2 * t + i + 1)
                        nc.vector.tensor_tensor(same[:, i, :, :], rows, spread(c_same[:, None, :], [P, heads, dk]),
                                                ALU.mult).then_inc(s["rotated"], 1)
                        nc.vector.tensor_tensor(swap[:, i, :, 0:half], rows[:, :, half:dk],
                                                spread(c_swap[:, None, 0:half], [P, heads, half]),
                                                ALU.mult).then_inc(s["rotated"], 1)
                        nc.vector.tensor_tensor(swap[:, i, :, half:dk], rows[:, :, 0:half],
                                                spread(c_swap[:, None, half:dk], [P, heads, half]),
                                                ALU.mult).then_inc(s["rotated"], 1)
                        nc.vector.tensor_reduce(length[:, i, :], square[:, i, :, :], AX.X, ALU.add).then_inc(s["summed"], 1)
                        dve.wait_ge(s["summed"], 2 * t + i + 1)
                        dve.wait_ge(s["inv_len_ready"], 2 * t + i + 1)
                        nc.vector.tensor_scalar(length_c[:, i, :], length[:, i, :], 1e-24, None,
                                                ALU.max).then_inc(s["clamped"], 1)

                def pair(it, first, end):
                    for u in range(2):
                        t = it * 2 + u
                        following = not (end and u == 1)
                        if not (first and u == 0):
                            normalise(t - 1)
                        subtract_max(t, 0)
                        subtract_max(t, 1)
                        if not (first and u == 0):
                            add_residual(t - 1)
                        sum_probs(t, 0)
                        if slots == 4:
                            subtract_max(t, 2)
                            sum_probs(t, 1)
                            subtract_max(t, 3)
                            if following:
                                copy_queries(t + 1)
                            sum_probs(t, 2)
                            sum_probs(t, 3)
                        else:
                            sum_probs(t, 1)
                            if following:
                                copy_queries(t + 1)
                                rotate(t + 1)

                dve.sem_inc(s["y_used"], 2)
                dve.sem_inc(s["scores_used"], 2)
                dve.sem_inc(s["o_ready"], 1)
                dve.sem_inc(s["inv_ready"], 1)
                dve.sem_inc(s["sums_ready"], 2)
                copy_queries(0)
                rotate(0)
                pair(0, True, False)
                with dve.Fori(1, TILES // 2 - 1) as it:
                    pair(it, False, False)
                pair(TILES // 2 - 1, False, True)
                normalise(TILES - 1)
                add_residual(TILES - 1)

            @block.scalar
            def _(act):
                def exponentials(t, j):
                    act.wait_ge(s["scores_used"], t * slots + j + 3)
                    nc.scalar.activation(probs[:, j % 2, :], probs[:, j % 2, :], ACT.Exp,
                                         scale=scale).then_inc(s["probs_ready"], 1)

                def copy_probs(t, j):
                    n = t * slots + j
                    act.wait_ge(s["probs_turned"], n + 3)
                    nc.scalar.activation(probs_t[:, j % 2, :], tp[:, j % 2, 0:width], ACT.Copy).then_inc(s["probs_t_ready"], 1)

                def copy_turned(t):
                    act.wait_ge(s["o_turned"], t + 2)
                    if wo is None:
                        ins = nc.scalar.activation(turned_out(t), p1[:, 0:inner].rearrange("p (c l) -> p c l", c=4),
                                                   ACT.Copy)
                    else:
                        ins = nc.scalar.activation(ot[:], p1[:, 0:inner], ACT.Copy)
                    ins.then_inc(s["ot_copied"], 1)

                def copy_keys_values(t, u):
                    if rotary is None:
                        act.wait_ge(s["k_done"], t + 1)
                        for g in range(groups):
                            if k_bias is None:
                                last = nc.scalar.activation(kt[:], p1[:, 0:width], ACT.Copy)
                                break
                            last = nc.scalar.activation(kt[:, g * P:(g + 1) * P], p1[:, g * P:(g + 1) * P],
                                                        ACT.Identity, bias=k_bias[:, g:g + 1])
                        last.then_inc(s["k_copied"], 1)
                    act.wait_ge(s["v_done"], t + 1)
                    nc.scalar.activation(v[:, u, :, 0:dk], p0[:, 0:inner].rearrange("p (h c) -> p h c", c=dk),
                                         ACT.Copy).then_inc(s["v_copied"], 1)

                def square_rows(t):
                    if rotary is None:
                        return
                    for i, rows, done in ((0, p0, s["q_done"]), (1, p1, s["k_done"])):
                        act.wait_ge(done, 2 * t + 1)
                        nc.scalar.activation(square[:, i, :, :].rearrange("p h c -> p (h c)"), rows[:, 0:inner],
                                             ACT.Square).then_inc(s["squared"], 1)

                def copy_rotated(t):
                    if rotary is None:
                        return
                    act.wait_ge(s["q_done"], 2 * t + 2)
                    nc.scalar.activation(qt[:], p1[:, 0:width], ACT.Copy).then_inc(s["q_copied"], 1)
                    act.wait_ge(s["k_done"], 2 * t + 2)
                    nc.scalar.activation(kt[:], p0[:, 0:width], ACT.Copy).then_inc(s["k_copied"], 1)

                def pair(it, first, end):
                    for u in range(2):
                        t = it * 2 + u
                        following = not (end and u == 1)
                        exponentials(t, 0)
                        if not (first and u == 0):
                            copy_turned(t - 1)
                        exponentials(t, 1)
                        if slots == 4:
                            copy_probs(t, 0)
                            exponentials(t, 2)
                            copy_probs(t, 1)
                            exponentials(t, 3)
                            if following:
                                copy_keys_values(t + 1, 1 - u)
                            copy_probs(t, 2)
                            copy_probs(t, 3)
                        else:
                            if following:
                                square_rows(t + 1)
                                copy_keys_values(t + 1, 1 - u)
                            copy_probs(t, 0)
                            copy_probs(t, 1)
                            if following:
                                copy_rotated(t + 1)

                act.sem_inc(s["ot_copied"], 2)
                act.sem_inc(s["probs_t_ready"], 2)
                act.wait_ge(s["const_ready"], 1)
                square_rows(0)
                copy_keys_values(0, 0)
                copy_rotated(0)
                pair(0, True, False)
                with act.Fori(1, TILES // 2 - 1) as it:
                    pair(it, False, False)
                pair(TILES // 2 - 1, False, True)
                copy_turned(TILES - 1)

            @block.gpsimd
            def _(pool):
                def copy_kv(t, u):
                    pool.wait_ge(s["v_done"], t - 1)
                    view = kv_tile[:, u, :]
                    source = kv_src(t)
                    if len(source.shape) == 3:
                        view = view.rearrange("p (c l) -> p c l", c=4)
                    nc.gpsimd.tensor_copy(view, source).then_inc(s["kv_copied"], 1)

                def mask(t, j):
                    if keep_mask is None:
                        return
                    n = t * slots + j
                    pool.wait_ge(s["probs_ready"], n + 1)
                    pool.wait_ge(s["probs_turned"], n + 1)
                    nc.gpsimd.tensor_tensor(kept[:, j % 2, :].rearrange("p (g k) -> p g k", k=P),
                                            probs[:, j % 2, :].rearrange("p (g k) -> p g k", k=P),
                                            spread(keep_mask[:, None, :], [P, groups, P]),
                                            ALU.mult).then_inc(s["kept_ready"], 1)

                def rotate(t):
                    if rotary is None:
                        return
                    for i in range(2):
                        pool.wait_ge(s["rotated"], 6 * t + 3 * i + 3)
                        nc.gpsimd.tensor_tensor(added[:, i, :, :], same[:, i, :, :], swap[:, i, :, :],
                                                ALU.add).then_inc(s["added_ready"], 1)
                        pool.wait_ge(s["clamped"], 2 * t + i + 1)
                        nc.gpsimd.tensor_tensor(inv_len[:, i, :], length_c[:, i, :], minus_half[:],
                                                ALU.pow).then_inc(s["inv_len_ready"], 1)
                        pool.wait_ge(s["added_ready"], 2 * t + i + 3)
                        pool.wait_ge(s["inv_len_ready"], 2 * t + i + 3)
                        nc.gpsimd.tensor_tensor(turned_rows[:, i, :, :], added[:, i, :, :],
                                                spread(inv_len[:, i, :, None], [P, heads, dk]),
                                                ALU.mult).then_inc(s["rows_ready"], 1)

                def pair(it, first, end):
                    for u in range(2):
                        t = it * 2 + u
                        following = not (end and u == 1)
                        if following and not (first and u == 0):
                            copy_kv(t + 1, 1 - u)
                        for j in range(slots):
                            mask(t, j)
                        if following:
                            rotate(t + 1)

                pool.sem_inc(s["probs_turned"], 2)
                pool.sem_inc(s["kept_ready"], 2)
                pool.sem_inc(s["o_turned"], 1)
                pool.sem_inc(s["added_ready"], 2)
                pool.sem_inc(s["inv_len_ready"], 2)
                nc.gpsimd.memset(v[:], 1.0).then_inc(s["const_ready"], 1)
                if rotary is not None:
                    nc.gpsimd.memset(minus_half[:], -0.5).then_inc(s["const_ready"], 1)
                    pool.wait_ge(s["const_ready"], 2)
                for t in range(2):
                    source = kv_src(t)
                    view = kv_tile[:, t, :]
                    if len(source.shape) == 3:
                        view = view.rearrange("p (c l) -> p c l", c=4)
                    nc.gpsimd.tensor_copy(view, source).then_inc(s["kv_copied"], 1)
                rotate(0)
                pair(0, True, False)
                with pool.Fori(1, TILES // 2 - 1) as it:
                    pair(it, False, False)
                pair(TILES // 2 - 1, False, True)



def feed_forward(nc, const, *, src_t, up, up_bias, down, down_bias, rows, chunks, act_func, resid,
                 value=None, value_bias=None):
    gated = value is not None
    with memory(nc) as (sb, ps):
        hidden = sb("hidden", [rows, 2, chunks, BANK])
        acted = sb("acted", [rows, 2, BANK])
        up_ps = ps("up_ps", [P, 2, BANK])
        value_ps = ps("value_ps", [P, 2, BANK])
        down_ps = ps("down_ps", [P, 2, BANK])
        with stage(nc, "up_done value_done acted_ready hidden_ready down_done y_used") as (block, s):

            @block.tensor
            def _(pe):
                def expand(i, b):
                    for c in range(chunks):
                        n = i * chunks + c
                        slot = (b * chunks + c) % 2
                        cols = slice(c * rows, (c + 1) * rows)
                        pe.wait_ge(s["acted_ready"], n + 1)
                        nc.tensor.matmul(up_ps[0:rows, slot, :], up[:, cols], src_t[:, bass.ds(i * BANK, BANK)],
                                         start=True, stop=True).then_inc(s["up_done"], 1)
                        if gated:
                            pe.wait_ge(s["hidden_ready"], n + 1)
                            nc.tensor.matmul(value_ps[0:rows, slot, :], value[:, cols],
                                             src_t[:, bass.ds(i * BANK, BANK)],
                                             start=True, stop=True).then_inc(s["value_done"], 1)

                def contract(i, b):
                    if gated:
                        pe.wait_ge(s["hidden_ready"], (i + 1) * chunks + 2)
                    else:
                        pe.wait_ge(s["acted_ready"], (i + 1) * chunks + 2)
                    pe.wait_ge(s["y_used"], i + 1)
                    for k in range(4):
                        for c in range(chunks):
                            nc.tensor.matmul(down_ps[:, b, k * P:(k + 1) * P], hidden[:, b, c, k * P:(k + 1) * P],
                                             down[:, c, :], start=c == 0, stop=False)
                        last = nc.tensor.matmul(down_ps[:, b, k * P:(k + 1) * P], const["ones"][0:1, :], down_bias,
                                                start=False, stop=True)
                    last.then_inc(s["down_done"], 1)

                expand(0, 0)
                with pe.Fori(0, TILES // 8 - 1) as it:
                    expand(it * 2 + 1, 1)
                    contract(it * 2, 0)
                    expand(it * 2 + 2, 0)
                    contract(it * 2 + 1, 1)
                expand(TILES // 4 - 1, 1)
                contract(TILES // 4 - 2, 0)
                contract(TILES // 4 - 1, 1)

            @block.scalar
            def _(act):
                act.sem_inc(s["acted_ready"], 2)
                with act.Fori(0, TILES // 8) as it:
                    for b in range(2):
                        i = it * 2 + b
                        for c in range(chunks):
                            n = i * chunks + c
                            slot = (b * chunks + c) % 2
                            act.wait_ge(s["up_done"], n + 1)
                            if gated:
                                act.wait_ge(s["hidden_ready"], n + 1)
                                dst = acted[:, slot, :]
                            else:
                                if c == 0:
                                    act.wait_ge(s["down_done"], i + 1)
                                dst = hidden[:, b, c, :]
                            nc.scalar.activation(dst, up_ps[0:rows, slot, :], act_func,
                                                 bias=up_bias[0:rows, c:c + 1]).then_inc(s["acted_ready"], 1)

            @block.vector
            def _(dve):
                dve.sem_inc(s["hidden_ready"], 2)
                dve.sem_inc(s["y_used"], 2)
                dve.sem_inc(s["down_done"], 2)

                def multiply(i, b):
                    if not gated:
                        return
                    for c in range(chunks):
                        n = i * chunks + c
                        slot = (b * chunks + c) % 2
                        dve.wait_ge(s["value_done"], n + 1)
                        dve.wait_ge(s["acted_ready"], n + 3)
                        if c == 0:
                            dve.wait_ge(s["down_done"], i + 1)
                        nc.vector.scalar_tensor_tensor(out=hidden[:, b, c, :], in0=value_ps[0:rows, slot, :],
                                                       scalar=value_bias[0:rows, c:c + 1], in1=acted[:, slot, :],
                                                       op0=ALU.add, op1=ALU.mult).then_inc(s["hidden_ready"], 1)

                def add(i, b):
                    dve.wait_ge(s["down_done"], i + 3)
                    rows_ = resid[:, bass.ds(i * 4, 4), :]
                    nc.vector.tensor_tensor(rows_, down_ps[:, b, :].rearrange("p (k d) -> p k d", d=D), rows_,
                                            ALU.add).then_inc(s["y_used"], 1)

                multiply(0, 0)
                with dve.Fori(0, TILES // 8 - 1) as it:
                    multiply(it * 2 + 1, 1)
                    add(it * 2, 0)
                    multiply(it * 2 + 2, 0)
                    add(it * 2 + 1, 1)
                multiply(TILES // 4 - 1, 1)
                add(TILES // 4 - 2, 0)
                add(TILES // 4 - 1, 1)



def router(nc, const, src_t, weight, bias, probs, experts):
    with memory(nc) as (sb, ps):
        tile = sb("tile", [P, 4, P])
        shifted = sb("shifted", [P, TILES, experts])
        most = sb("most", [P, TILES])
        total = sb("total", [P, TILES])
        inv = sb("inv", [P, TILES])
        logits = ps("logits", [P, 2, BANK])
        with stage(nc, "tile_copied logits_done logits_used chain exp_done") as (block, s):

            @block.gpsimd
            def _(pool):
                pool.sem_inc(s["logits_done"], 1)
                with pool.Fori(0, TILES // 4) as it:
                    pool.wait_ge(s["logits_done"], it + 1)
                    nc.gpsimd.tensor_copy(tile[:].rearrange("p k n -> p (k n)"),
                                          src_t[:, bass.ds(it * BANK, BANK)]).then_inc(s["tile_copied"], 1)

            @block.tensor
            def _(pe):
                with pe.Fori(0, TILES // 4) as it:
                    pe.wait_ge(s["tile_copied"], it + 1)
                    pe.wait_ge(s["logits_used"], it + 1)
                    for k in range(4):
                        last = nc.tensor.matmul(logits[:, 0, k * experts:(k + 1) * experts], tile[:, k, :], weight,
                                                start=True, stop=True)
                    last.then_inc(s["logits_done"], 1)

            @block.vector
            def _(dve):
                dve.sem_inc(s["logits_used"], 1)
                with dve.Fori(0, TILES // 4) as it:
                    dve.wait_ge(s["logits_done"], it + 2)
                    src = logits[:, 0, 0:4 * experts].rearrange("p (k e) -> p k e", e=experts)
                    dst = shifted[:, bass.ds(it * 4, 4), :]
                    if bias is None:
                        ins = nc.vector.tensor_copy(dst, src)
                    else:
                        ins = nc.vector.tensor_tensor(dst, src, spread(bias[:, None, :], [P, 4, experts]), ALU.add)
                    ins.then_inc(s["logits_used"], 1)
                dve.wait_ge(s["logits_used"], TILES // 4 + 1)
                nc.vector.tensor_reduce(most[:], shifted[:], AX.X, ALU.max).then_inc(s["chain"], 1)
                dve.wait_ge(s["chain"], 1)
                nc.vector.tensor_tensor(shifted[:], shifted[:], spread(most[:, :, None], [P, TILES, experts]),
                                        ALU.subtract).then_inc(s["chain"], 1)
                dve.wait_ge(s["exp_done"], 1)
                nc.vector.tensor_reduce(total[:], shifted[:], AX.X, ALU.add).then_inc(s["chain"], 1)
                dve.wait_ge(s["chain"], 3)
                nc.vector.reciprocal(inv[:], total[:]).then_inc(s["chain"], 1)
                dve.wait_ge(s["chain"], 4)
                nc.vector.tensor_tensor(probs[:], shifted[:], spread(inv[:, :, None], [P, TILES, experts]),
                                        ALU.mult).then_inc(s["chain"], 1)

            @block.scalar
            def _(act):
                act.wait_ge(s["chain"], 2)
                nc.scalar.activation(shifted[:], shifted[:], ACT.Exp).then_inc(s["exp_done"], 1)


def pick_first(nc, values, threshold, quota, picked, experts):
    with memory(nc) as (sb, ps):
        above = sb("above", [P, TILES, experts])
        equal = sb("equal", [P, TILES, experts])
        ones = sb("ones", [P, TILES * experts])
        upto = sb("upto", [P, TILES, experts])
        before = sb("before", [P, TILES])
        count = sb("count", [P, TILES])
        with stage(nc, "chain") as (block, s):

            @block.vector
            def _(dve):
                wide = [P, TILES, experts]
                nc.vector.memset(ones[:], 1.0).then_inc(s["chain"], 1)
                nc.vector.memset(before[:], 0.0).then_inc(s["chain"], 1)
                nc.vector.tensor_tensor(above[:], values, spread(threshold[:, :, None], wide),
                                        ALU.is_gt).then_inc(s["chain"], 1)
                nc.vector.tensor_tensor(equal[:], values, spread(threshold[:, :, None], wide),
                                        ALU.is_equal).then_inc(s["chain"], 1)
                dve.wait_ge(s["chain"], 4)
                nc.vector.tensor_reduce(count[:], above[:], AX.X, ALU.add).then_inc(s["chain"], 1)
                nc.vector.tensor_tensor_scan(upto[:].rearrange("p t e -> p (t e)"), ones[:],
                                             equal[:].rearrange("p t e -> p (t e)"), 0.0, ALU.mult,
                                             ALU.add).then_inc(s["chain"], 1)
                dve.wait_ge(s["chain"], 6)
                nc.vector.tensor_copy(before[:, 1:TILES], upto[:, 0:TILES - 1, experts - 1]).then_inc(s["chain"], 1)
                dve.wait_ge(s["chain"], 7)
                nc.vector.tensor_tensor(before[:], before[:], count[:], ALU.subtract).then_inc(s["chain"], 1)
                dve.wait_ge(s["chain"], 8)
                nc.vector.tensor_tensor(upto[:], upto[:], spread(before[:, :, None], wide),
                                        ALU.subtract).then_inc(s["chain"], 1)
                dve.wait_ge(s["chain"], 9)
                nc.vector.scalar_tensor_tensor(out=equal[:], in0=upto[:], scalar=float(quota), in1=equal[:],
                                               op0=ALU.is_le, op1=ALU.mult).then_inc(s["chain"], 1)
                dve.wait_ge(s["chain"], 10)
                nc.vector.tensor_tensor(picked[:], above[:], equal[:], ALU.add).then_inc(s["chain"], 1)


def rank_largest(nc, values, threshold, experts, rank):
    with memory(nc) as (sb, ps):
        rows = sb("rows", [P, 8, experts])
        largest = sb("largest", [P, 8, 8])
        scratch = sb("scratch", [P, 1])
        with stage(nc, "rows_copied found taken") as (block, s):

            @block.vector
            def _(dve):
                dve.sem_inc(s["found"], 8)
                dve.sem_inc(s["taken"], 1)
                with dve.Fori(0, TILES // 8) as it:
                    dve.wait_ge(s["found"], it * 8 + 8)
                    nc.vector.tensor_copy(rows[:], values[:, bass.ds(it * 8, 8), :]).then_inc(s["rows_copied"], 1)
                    dve.wait_ge(s["taken"], it + 1)
                    dve.wait_ge(s["rows_copied"], it * 2 + 1)
                    nc.vector.memset(scratch[:], 0.0).then_inc(s["rows_copied"], 1)
                    for k in range(8):
                        nc.vector.max(largest[:, k, :], rows[:, k, :]).then_inc(s["found"], 1)
                    dve.wait_ge(s["found"], it * 8 + 16)
                    nc.vector.tensor_copy(threshold[:, bass.ds(it * 8, 8)],
                                          largest[:, :, rank - 1]).then_inc(s["taken"], 1)


def ranks_over_tokens(nc, const, mask, ranks, experts):
    with memory(nc) as (sb, ps):
        ones = sb("ones", [P, TILES])
        upto = sb("upto", [P, TILES, experts])
        counts = ps("counts", [P, BANK])
        with stage(nc, "ones_set scanned counted copied") as (block, s):

            @block.vector
            def _(dve):
                nc.vector.memset(ones[:], 1.0).then_inc(s["ones_set"], 1)
                dve.wait_ge(s["ones_set"], 1)
                for e in range(experts):
                    nc.vector.tensor_tensor_scan(upto[:, :, e], ones[:], mask[:, :, e], 0.0, ALU.mult,
                                                 ALU.add).then_inc(s["scanned"], 1)
                dve.wait_ge(s["scanned"], experts)
                nc.vector.tensor_tensor(upto[:], upto[:], mask[:], ALU.subtract).then_inc(s["scanned"], 1)
                dve.wait_ge(s["counted"], 1)
                nc.vector.tensor_copy(ranks[:], counts[:, 0:TILES * experts].rearrange("p (t e) -> p t e", e=experts)
                                      ).then_inc(s["copied"], 1)

            @block.tensor
            def _(pe):
                pe.wait_ge(s["scanned"], experts + 1)
                nc.tensor.matmul(counts[:, 0:TILES * experts], const["ones"][:], upto[:].rearrange("p t e -> p (t e)"),
                                 start=True, stop=False)
                nc.tensor.matmul(counts[:, 0:TILES * experts], const["earlier"][:], mask[:].rearrange("p t e -> p (t e)"),
                                 start=False, stop=True).then_inc(s["counted"], 1)


def expert_thresholds(nc, const, probs, threshold, missing, equal, above, experts, capacity):
    with memory(nc) as (sb, ps):
        bit = sb("bit", [P, experts], I32)
        trial = sb("trial", [P, experts])
        passed = sb("passed", [P, TILES, experts])
        count = sb("count", [P, experts])
        kept = sb("kept", [P, experts])
        totals = ps("totals", [P, BANK])
        wide = [P, TILES, experts]
        with stage(nc, "ready tried passed_ready counted summed decided lowered") as (block, s):

            @block.vector
            def _(dve):
                nc.vector.memset(bit[:], 1 << 30).then_inc(s["ready"], 1)
                nc.vector.memset(threshold[:], 0.0).then_inc(s["ready"], 1)
                dve.wait_ge(s["ready"], 2)
                dve.sem_inc(s["lowered"], 2)
                with dve.Fori(0, 31) as i:
                    dve.wait_ge(s["lowered"], i * 2 + 2)
                    nc.vector.tensor_tensor(trial[:].bitcast(I32), threshold[:].bitcast(I32), bit[:],
                                            ALU.bitwise_or).then_inc(s["tried"], 1)
                    dve.wait_ge(s["tried"], i + 1)
                    nc.vector.tensor_tensor(passed[:], probs[:], spread(trial[:, None, :], wide),
                                            ALU.is_ge).then_inc(s["passed_ready"], 1)
                    dve.wait_ge(s["passed_ready"], i + 1)
                    nc.vector.tensor_reduce(count[:], passed[:].rearrange("p t e -> p e t"), AX.X,
                                            ALU.add).then_inc(s["counted"], 1)
                    nc.vector.tensor_single_scalar(bit[:], bit[:], 1, ALU.logical_shift_right).then_inc(s["lowered"], 1)
                    dve.wait_ge(s["summed"], i + 1)
                    nc.vector.scalar_tensor_tensor(out=kept[:], in0=totals[:, 0:experts], scalar=float(capacity),
                                                   in1=trial[:], op0=ALU.is_ge, op1=ALU.mult).then_inc(s["decided"], 1)
                    dve.wait_ge(s["decided"], i + 1)
                    nc.vector.tensor_tensor(threshold[:], threshold[:], kept[:], ALU.max).then_inc(s["lowered"], 1)
                dve.wait_ge(s["lowered"], 64)
                nc.vector.tensor_tensor(above[:], probs[:], spread(threshold[:, None, :], wide),
                                        ALU.is_gt).then_inc(s["ready"], 1)
                nc.vector.tensor_tensor(equal[:], probs[:], spread(threshold[:, None, :], wide),
                                        ALU.is_equal).then_inc(s["ready"], 1)
                dve.wait_ge(s["ready"], 3)
                nc.vector.tensor_reduce(count[:], above[:].rearrange("p t e -> p e t"), AX.X,
                                        ALU.add).then_inc(s["counted"], 1)
                dve.wait_ge(s["summed"], 32)
                nc.vector.tensor_scalar(missing[:], totals[:, 0:experts], -1.0, float(capacity), ALU.mult,
                                        ALU.add).then_inc(s["ready"], 1)

            @block.tensor
            def _(pe):
                with pe.Fori(0, 32) as i:
                    pe.wait_ge(s["counted"], i + 1)
                    nc.tensor.matmul(totals[:, 0:experts], const["ones"][:], count[:], start=True,
                                     stop=True).then_inc(s["summed"], 1)



def mix_top_experts(nc, const, *, src_t, gate_w, up_w, down_w, combine, resid, gate):
    widths = [BANK] * 4 + [P]
    chunks = len(widths)
    with memory(nc) as (sb, ps):
        tile = sb("tile", [P, 2, P])
        acted = sb("acted", [P, 2, BANK])
        product = sb("product", [P, 2, BANK])
        weighted = sb("weighted", [P, 2, BANK])
        hidden_t = sb("hidden_t", [P, 2, BANK])
        gate_ps = ps("gate_ps", [P, 2, BANK])
        up_ps = ps("up_ps", [P, 2, BANK])
        turned_ps = ps("turned_ps", [P, 2, BANK])
        y_ps = ps("y_ps", [P, 2, BANK])
        with stage(nc, "tile_copied projected acted_ready product_ready weighted_ready turned t_copied y_done "
                       "y_used") as (block, s):

            def steps(it, first, end):
                def at(k):
                    if k < 0:
                        return None if first else (it * 2 - 1, 1, k + chunks, (k + 2 * chunks) % 2)
                    u, c = divmod(k, chunks)
                    return (it * 2 + u, u, c, k % 2)

                return [(at(k), at(k - 1), at(k - 2)) for k in range(2 * chunks)]

            @block.tensor
            def _(pe):
                def project(t, u, c, slot):
                    n = t * chunks + c
                    if c == 0:
                        pe.wait_ge(s["tile_copied"], t + 1)
                    pe.wait_ge(s["product_ready"], n + 1)
                    cols = slice(c * BANK, c * BANK + widths[c])
                    nc.tensor.matmul(gate_ps[:, slot, 0:widths[c]], tile[:, u, :], gate_w[:, cols], start=True,
                                     stop=True)
                    nc.tensor.matmul(up_ps[:, slot, 0:widths[c]], tile[:, u, :], up_w[:, cols], start=True,
                                     stop=True).then_inc(s["projected"], 1)

                def turn(t, u, c, slot):
                    n = t * chunks + c
                    pe.wait_ge(s["weighted_ready"], n + 3)
                    pe.wait_ge(s["t_copied"], n + 1)
                    for q in range(widths[c] // P):
                        last = nc.tensor.transpose(turned_ps[:, slot, q * P:(q + 1) * P],
                                                   weighted[:, slot, q * P:(q + 1) * P], const["ident"][:])
                    last.then_inc(s["turned"], 1)

                def contract(t, u, c, slot):
                    n = t * chunks + c
                    pe.wait_ge(s["t_copied"], n + 3)
                    if c == 0:
                        pe.wait_ge(s["y_used"], t + 1)
                    for q in range(widths[c] // P):
                        last = nc.tensor.matmul(y_ps[:, u, 0:D], hidden_t[:, slot, q * P:(q + 1) * P],
                                                down_w[:, 4 * c + q, :], start=c == 0 and q == 0,
                                                stop=c == chunks - 1)
                    if c == chunks - 1:
                        last.then_inc(s["y_done"], 1)

                def pair(it, first, end):
                    for now, before, two_before in steps(it, first, end):
                        project(*now)
                        if before:
                            turn(*before)
                        if two_before:
                            contract(*two_before)

                pair(0, True, False)
                with pe.Fori(1, TILES // 2) as it:
                    pair(it, False, False)
                turn(TILES - 1, 1, chunks - 1, 1)
                contract(TILES - 1, 1, chunks - 2, 0)
                contract(TILES - 1, 1, chunks - 1, 1)

            @block.scalar
            def _(act):
                def activate(t, u, c, slot):
                    act.wait_ge(s["projected"], t * chunks + c + 1)
                    nc.scalar.activation(acted[:, slot, 0:widths[c]], gate_ps[:, slot, 0:widths[c]],
                                         ACT.Silu).then_inc(s["acted_ready"], 1)

                def copy_turned(t, u, c, slot):
                    act.wait_ge(s["turned"], t * chunks + c + 3)
                    nc.scalar.activation(hidden_t[:, slot, 0:widths[c]], turned_ps[:, slot, 0:widths[c]],
                                         ACT.Copy).then_inc(s["t_copied"], 1)

                def pair(it, first, end):
                    for now, before, _ in steps(it, first, end):
                        activate(*now)
                        if before:
                            copy_turned(*before)

                act.sem_inc(s["t_copied"], 2)
                pair(0, True, False)
                with act.Fori(1, TILES // 2) as it:
                    pair(it, False, False)
                copy_turned(TILES - 1, 1, chunks - 1, 1)

            @block.vector
            def _(dve):
                def multiply(t, u, c, slot):
                    n = t * chunks + c
                    dve.wait_ge(s["acted_ready"], n + 1)
                    dve.wait_ge(s["weighted_ready"], n + 1)
                    nc.vector.tensor_tensor(product[:, slot, 0:widths[c]], up_ps[:, slot, 0:widths[c]],
                                            acted[:, slot, 0:widths[c]], ALU.mult).then_inc(s["product_ready"], 1)

                def add(t, u):
                    dve.wait_ge(s["y_done"], t + 1)
                    rows = resid[:, bass.ds(t, 1), :]
                    nc.vector.scalar_tensor_tensor(out=rows, in0=y_ps[:, u:u + 1, 0:D], scalar=gate, in1=rows,
                                                   op0=ALU.mult, op1=ALU.add).then_inc(s["y_used"], 1)

                def pair(it, first, end):
                    for k, (now, _, _) in enumerate(steps(it, first, end)):
                        multiply(*now)
                        if k % chunks == 2 and not (first and k < chunks):
                            add(now[0] - 1, 1 - now[1])

                dve.sem_inc(s["product_ready"], 2)
                dve.sem_inc(s["y_used"], 2)
                pair(0, True, False)
                with dve.Fori(1, TILES // 2) as it:
                    pair(it, False, False)
                add(TILES - 1, 1)

            @block.gpsimd
            def _(pool):
                def copy_tile(t, u):
                    nc.gpsimd.tensor_copy(tile[:, u, :], tile_cols(src_t, t)).then_inc(s["tile_copied"], 1)

                def weight(t, u, c, slot):
                    n = t * chunks + c
                    pool.wait_ge(s["product_ready"], n + 3)
                    pool.wait_ge(s["turned"], n + 1)
                    experts = widths[c] // 64
                    nc.gpsimd.tensor_tensor(
                        weighted[:, slot, 0:widths[c]].rearrange("p (e i) -> p e i", i=64),
                        product[:, slot, 0:widths[c]].rearrange("p (e i) -> p e i", i=64),
                        spread(combine[:, bass.ds(t, 1), c * 8:c * 8 + experts].rearrange("p t e -> p (t e)")[:, :, None],
                               [P, experts, 64]), ALU.mult).then_inc(s["weighted_ready"], 1)

                def pair(it, first, end):
                    for k, (now, _, _) in enumerate(steps(it, first, end)):
                        t, u, c, _slot = now
                        if c == 1 and not (end and u == 1):
                            if not (first and u == 0):
                                pool.wait_ge(s["projected"], t * chunks)
                            copy_tile(t + 1, 1 - u)
                        weight(*now)

                pool.sem_inc(s["weighted_ready"], 2)
                pool.sem_inc(s["turned"], 2)
                copy_tile(0, 0)
                pair(0, True, False)
                with pool.Fori(1, TILES // 2 - 1) as it:
                    pair(it, False, False)
                pair(TILES // 2 - 1, False, True)


def mix_chosen_tokens(nc, const, *, src_t, up_w, up_b, down_w, down_b, weights, resid):
    groups, chunks, rows = 4, 3, 114
    steps = TOKENS // BANK
    with memory(nc) as (sb, ps):
        hidden = sb("hidden", [rows, 2, chunks, BANK])
        up_ps = ps("up_ps", [P, 2, BANK])
        down_ps = ps("down_ps", [P, 2, BANK])
        with stage(nc, "up_done acted_ready down_done added") as (block, s):

            @block.tensor
            def _(pe):
                def expand(it, g):
                    m = it * groups + g
                    for c in range(chunks):
                        slot = (g * chunks + c) % 2
                        pe.wait_ge(s["acted_ready"], m * chunks + c + 1)
                        nc.tensor.matmul(up_ps[0:rows, slot, :], up_w[:, (g * chunks + c) * rows:(g * chunks + c + 1) * rows],
                                         src_t[:, bass.ds(it * BANK, BANK)], start=True, stop=True).then_inc(s["up_done"], 1)

                def contract(it, g):
                    m = it * groups + g
                    pe.wait_ge(s["acted_ready"], (m + 1) * chunks + 2)
                    for k in range(4):
                        n = m * 4 + k
                        pe.wait_ge(s["added"], n * 2 + 6)
                        for c in range(chunks):
                            nc.tensor.matmul(down_ps[:, k % 2, 0:2 * D], hidden[:, g % 2, c, k * P:(k + 1) * P],
                                             down_w[:, c, g * 2 * D:(g + 1) * 2 * D], start=c == 0, stop=False)
                        nc.tensor.matmul(down_ps[:, k % 2, 0:2 * D], const["ones"][0:1, :],
                                         down_b[:, g * 2 * D:(g + 1) * 2 * D], start=False,
                                         stop=True).then_inc(s["down_done"], 1)

                def step(it, end):
                    for g in range(groups):
                        if g < groups - 1:
                            expand(it, g + 1)
                        elif not end:
                            expand(it + 1, 0)
                        contract(it, g)

                expand(0, 0)
                with pe.Fori(0, steps - 1) as it:
                    step(it, False)
                step(steps - 1, True)

            @block.scalar
            def _(act):
                act.sem_inc(s["acted_ready"], 2)
                with act.Fori(0, steps) as it:
                    for g in range(groups):
                        for c in range(chunks):
                            act.wait_ge(s["up_done"], (it * groups + g) * chunks + c + 1)
                            nc.scalar.activation(hidden[:, g % 2, c, :], up_ps[0:rows, (g * chunks + c) % 2, :],
                                                 ACT.Silu, bias=up_b[0:rows, g * chunks + c:g * chunks + c + 1]
                                                 ).then_inc(s["acted_ready"], 1)

            @block.vector
            def _(dve):
                dve.sem_inc(s["added"], 8)
                with dve.Fori(0, steps) as it:
                    for g in range(groups):
                        for k in range(4):
                            n = (it * groups + g) * 4 + k
                            dve.wait_ge(s["down_done"], n + 1)
                            row = resid[:, bass.ds(it * 4 + k, 1), :]
                            for e in range(2):
                                dve.wait_ge(s["added"], n * 2 + 2 if e == 0 else n * 2 + 9)
                                nc.vector.scalar_tensor_tensor(
                                    out=row, in0=down_ps[:, k % 2:k % 2 + 1, e * D:(e + 1) * D],
                                    scalar=weights[:, bass.ds((it * 4 + k) * 8 + g * 2 + e, 1)], in1=row,
                                    op0=ALU.mult, op1=ALU.add).then_inc(s["added"], 1)


def merge_linear_experts(nc, const, w1_t, w2, b1, b2, merged, merged_b, experts, chunks):
    with memory(nc) as (sb, ps):
        w_ps = ps("w_ps", [P, 2, BANK])
        b_ps = ps("b_ps", [P, 2, BANK])
        with stage(nc, "w_done b_done w_copied b_copied") as (block, s):

            @block.tensor
            def _(pe):
                for e in range(experts):
                    if e >= 2:
                        pe.wait_ge(s["w_copied"], e - 1)
                        pe.wait_ge(s["b_copied"], e - 1)
                    for c in range(chunks):
                        last = nc.tensor.matmul(w_ps[:, e % 2, 0:D], w1_t[:, c, e, :], w2[:, c, e, :], start=c == 0,
                                                stop=c == chunks - 1)
                    last.then_inc(s["w_done"], 1)
                    for c in range(chunks):
                        nc.tensor.matmul(b_ps[0:1, e % 2, 0:D], b1[:, c, e:e + 1], w2[:, c, e, :], start=c == 0,
                                         stop=False)
                    nc.tensor.matmul(b_ps[0:1, e % 2, 0:D], const["ones"][0:1, 0:1], b2[0:1, e * D:(e + 1) * D],
                                     start=False, stop=True).then_inc(s["b_done"], 1)

            @block.vector
            def _(dve):
                for e in range(experts):
                    dve.wait_ge(s["w_done"], e + 1)
                    nc.vector.tensor_copy(merged[:, e * D:(e + 1) * D], w_ps[:, e % 2, 0:D]).then_inc(s["w_copied"], 1)

            @block.scalar
            def _(act):
                for e in range(experts):
                    act.wait_ge(s["b_done"], e + 1)
                    nc.scalar.activation(merged_b[0:1, e * D:(e + 1) * D], b_ps[0:1, e % 2, 0:D],
                                         ACT.Copy).then_inc(s["b_copied"], 1)


def mix_merged_experts(nc, const, *, src_t, merged, merged_b, weights, resid, experts):
    halves = experts * D // BANK
    per_bank = experts // halves
    with memory(nc) as (sb, ps):
        tile = sb("tile", [P, 2, P])
        y_ps = ps("y_ps", [P, 2, halves, BANK])
        with stage(nc, "tile_copied y_done added") as (block, s):

            @block.gpsimd
            def _(pool):
                pool.sem_inc(s["y_done"], 2)
                with pool.Fori(0, TILES // 2) as it:
                    for u in range(2):
                        pool.wait_ge(s["y_done"], it * 2 + u + 1)
                        nc.gpsimd.tensor_copy(tile[:, u, :], tile_cols(src_t, it * 2 + u)).then_inc(s["tile_copied"], 1)

            @block.tensor
            def _(pe):
                with pe.Fori(0, TILES // 2) as it:
                    for u in range(2):
                        t = it * 2 + u
                        pe.wait_ge(s["tile_copied"], t + 1)
                        pe.wait_ge(s["added"], (t + 1) * experts)
                        for a in range(halves):
                            cols = slice(a * BANK, (a + 1) * BANK)
                            nc.tensor.matmul(y_ps[:, u, a, :], tile[:, u, :], merged[:, cols], start=True, stop=False)
                            last = nc.tensor.matmul(y_ps[:, u, a, :], const["ones"][0:1, :], merged_b[0:1, cols],
                                                    start=False, stop=True)
                        last.then_inc(s["y_done"], 1)

            @block.vector
            def _(dve):
                dve.sem_inc(s["added"], 2 * experts)
                with dve.Fori(0, TILES // 2) as it:
                    for u in range(2):
                        t = it * 2 + u
                        dve.wait_ge(s["y_done"], t + 3)
                        row = resid[:, bass.ds(t, 1), :]
                        for e in range(experts):
                            dve.wait_ge(s["added"], (t + 2) * experts + e)
                            nc.vector.scalar_tensor_tensor(
                                out=row, in0=y_ps[:, u, e // per_bank:e // per_bank + 1,
                                                  (e % per_bank) * D:(e % per_bank + 1) * D],
                                scalar=weights[:, bass.ds(t * experts + e, 1)], in1=row,
                                op0=ALU.mult, op1=ALU.add).then_inc(s["added"], 1)



def add_all(nc, out, a, b, scale=None):
    with stage(nc, "added") as (block, s):

        @block.vector
        def _(dve):
            if scale is None:
                nc.vector.tensor_tensor(out, a, b, ALU.add).then_inc(s["added"], 1)
            else:
                nc.vector.scalar_tensor_tensor(out=out, in0=a, scalar=scale, in1=b, op0=ALU.mult,
                                               op1=ALU.add).then_inc(s["added"], 1)


def most_probable(nc, probs, most):
    with stage(nc, "found") as (block, s):

        @block.vector
        def _(dve):
            nc.vector.tensor_reduce(most[:], probs[:], AX.X, ALU.max).then_inc(s["found"], 1)


def combine_weights(nc, probs, picked, total, combine, experts):
    with stage(nc, "ones_set weighted summed") as (block, s):

        @block.vector
        def _(dve):
            nc.vector.memset(combine[:], 1.0).then_inc(s["ones_set"], 1)
            nc.vector.tensor_tensor(picked[:], picked[:], probs[:], ALU.mult).then_inc(s["weighted"], 1)
            dve.wait_ge(s["weighted"], 1)
            nc.vector.tensor_reduce(total[:], picked[:], AX.X, ALU.add).then_inc(s["summed"], 1)
            dve.wait_ge(s["summed"], 1)
            nc.vector.tensor_scalar(total[:], total[:], 1e-12, None, ALU.max).then_inc(s["summed"], 1)
            dve.wait_ge(s["summed"], 2)
            nc.vector.reciprocal(total[:], total[:]).then_inc(s["summed"], 1)
            dve.wait_ge(s["summed"], 3)
            dve.wait_ge(s["ones_set"], 1)
            nc.vector.tensor_tensor(combine[:, :, 0:experts], picked[:], spread(total[:, :, None], [P, TILES, experts]),
                                    ALU.mult).then_inc(s["weighted"], 1)


def chosen_weights(nc, probs, above, equal, ranks, missing, gate, experts):
    with stage(nc, "within taken chosen weighted") as (block, s):

        @block.vector
        def _(dve):
            nc.vector.tensor_tensor(ranks[:], ranks[:], spread(missing[:, None, :], [P, TILES, experts]),
                                    ALU.is_lt).then_inc(s["within"], 1)
            dve.wait_ge(s["within"], 1)
            nc.vector.tensor_tensor(equal[:], equal[:], ranks[:], ALU.mult).then_inc(s["taken"], 1)
            dve.wait_ge(s["taken"], 1)
            nc.vector.tensor_tensor(above[:], above[:], equal[:], ALU.add).then_inc(s["chosen"], 1)
            dve.wait_ge(s["chosen"], 1)
            nc.vector.scalar_tensor_tensor(out=probs[:], in0=probs[:], scalar=gate, in1=above[:], op0=ALU.mult,
                                           op1=ALU.mult).then_inc(s["weighted"], 1)


def capped_weights(nc, probs, picked, ranks, capacity):
    with stage(nc, "kept weighted") as (block, s):

        @block.vector
        def _(dve):
            nc.vector.scalar_tensor_tensor(out=ranks[:], in0=ranks[:], scalar=float(capacity), in1=picked[:],
                                           op0=ALU.is_lt, op1=ALU.mult).then_inc(s["kept"], 1)
            dve.wait_ge(s["kept"], 1)
            nc.vector.tensor_tensor(probs[:], probs[:], ranks[:], ALU.mult).then_inc(s["weighted"], 1)


def scale_rotary_tables(nc, tables, scales):
    with stage(nc, "scaled") as (block, s):

        @block.vector
        def _(dve):
            for i, scale in enumerate(scales):
                nc.vector.tensor_tensor(tables[:, i, :], tables[:, i, :], scale[:], ALU.mult).then_inc(s["scaled"], 1)


def shift_tokens(nc, const, src, dst):
    half = D // 2
    with memory(nc) as (sb, ps):
        bank = ps("shifted", [P, BANK])
        with stage(nc, "copied shifted used") as (block, s):

            @block.gpsimd
            def _(pool):
                nc.gpsimd.tensor_copy(dst[:, :, 0:half], src[:, :, 0:half]).then_inc(s["copied"], 1)

            @block.tensor
            def _(pe):
                with pe.Fori(0, TILES // 8) as it:
                    pe.wait_ge(s["used"], it + 1)
                    nc.tensor.matmul(bank[:], const["previous"][:], src[:, bass.ds(it * 8, 8), half:D], start=True,
                                     stop=True).then_inc(s["shifted"], 1)

            @block.scalar
            def _(act):
                act.sem_inc(s["used"], 1)
                with act.Fori(0, TILES // 8) as it:
                    act.wait_ge(s["shifted"], it + 1)
                    nc.scalar.activation(dst[:, bass.ds(it * 8, 8), half:D],
                                         bank[:].rearrange("p (t d) -> p t d", d=half), ACT.Copy).then_inc(s["used"], 1)


def project_rows(nc, const, *, src_t, weight, bias, resid, out):
    with memory(nc) as (sb, ps):
        tile = sb("tile", [P, 2, P])
        y_ps = ps("y_ps", [P, 2, BANK])
        with stage(nc, "tile_copied y_done y_used") as (block, s):

            @block.gpsimd
            def _(pool):
                pool.sem_inc(s["y_done"], 2)
                with pool.Fori(0, TILES // 2) as it:
                    for u in range(2):
                        pool.wait_ge(s["y_done"], it * 2 + u + 1)
                        nc.gpsimd.tensor_copy(tile[:, u, :], tile_cols(src_t, it * 2 + u)).then_inc(s["tile_copied"], 1)

            @block.tensor
            def _(pe):
                with pe.Fori(0, TILES // 2) as it:
                    for u in range(2):
                        t = it * 2 + u
                        pe.wait_ge(s["tile_copied"], t + 1)
                        pe.wait_ge(s["y_used"], t + 1)
                        nc.tensor.matmul(y_ps[:, u, 0:D], tile[:, u, :], weight, start=True, stop=False)
                        nc.tensor.matmul(y_ps[:, u, 0:D], const["ones"][0:1, :], bias, start=False,
                                         stop=True).then_inc(s["y_done"], 1)

            @block.vector
            def _(dve):
                dve.sem_inc(s["y_used"], 2)
                with dve.Fori(0, TILES // 2) as it:
                    for u in range(2):
                        t = it * 2 + u
                        dve.wait_ge(s["y_done"], t + 3)
                        nc.vector.tensor_tensor(out[:, bass.ds(t, 1), :], y_ps[:, u:u + 1, 0:D],
                                                resid[:, bass.ds(t, 1), :], ALU.add).then_inc(s["y_used"], 1)



def program(nc, w, out, until=8, start=0):
    with memory(nc) as (sb, ps):
        const = dict(ident=sb("ident", [P, P]), ones=sb("ones", [P, P]), earlier=sb("earlier", [P, P]),
                                previous=sb("previous", [P, P]), eps=sb("eps", [P, 1]))
        gates = sb("gates", [P, 8])
        x = sb("x", [P, TILES, D])
        z = sb("z", [P, TILES, D])
        h = sb("h", [P, TILES, D])
        xt = sb("xt", [P, TOKENS])
        yt = sb("yt", [P, TOKENS])
        ctx_t = sb("ctx_t", [CTX, TOKENS])

        def buffers(sb, names):
            bufs = {}
            loads = []
            for name in names.split():
                shape = list(w[name].shape)
                buf = sb("w", shape)
                bufs[name.split(".")[-1]] = buf
                index = tuple(slice(None) for _ in shape)
                loads.append((buf[index], w[name][index]))
            return bufs, loads

        with stage(nc, "loaded eps_set gates_ready") as (block, s):

            @block.sync
            def _(sp):
                sp.dma_start(x[:], w["x"].rearrange("t p d -> p t d")).then_inc(s["loaded"], 16)
                sp.dma_start(gates[:], w["gates"]).then_inc(s["loaded"], 16)
                sp.dma_start(const["ident"][:], w["ident"]).then_inc(s["loaded"], 16)
                sp.dma_start(const["earlier"][:], w["earlier"]).then_inc(s["loaded"], 16)
                sp.dma_start(const["previous"][:], w["previous"]).then_inc(s["loaded"], 16)
                sp.dma_start(ctx_t[:], w["ctx_t"]).then_inc(s["loaded"], 16)
                sp.wait_ge(s["loaded"], 96)

            @block.gpsimd
            def _(pool):
                nc.gpsimd.memset(const["eps"][:], EPS)
                nc.gpsimd.memset(const["ones"][:], 1.0)

            @block.scalar
            def _(act):
                act.wait_ge(s["loaded"], 96)
                nc.scalar.activation(gates[:], gates[:], ACT.Tanh).then_inc(s["gates_ready"], 1)

        def cross_attention(layer, gate_col, biased):
            with memory(nc) as (sb, ps):
                names = "wq wk wv wo" + (" bq bk bv bo" if biased else "")
                b, loads = buffers(sb, " ".join(f"{layer}.{n}" for n in names.split()))
                layer_norm(nc, const, x, t_outs=[(xt, None, None)], loads=loads)
                attention(nc, const, heads=16, dk=8, groups=4, kv_rows=CTX,
                          q_src=lambda t: tile_cols(xt, t), kv_src=lambda t: tile_cols(ctx_t, t),
                          wq=b["wq"], wk=b["wk"], wv=b["wv"][:], wo=b["wo"], scale=8 ** -0.5,
                          q_bias=b["bq"] if biased else None, k_bias=b["bk"] if biased else None,
                          v_bias=b["bv"][:] if biased else None, o_bias=b["bo"][:] if biased else None,
                          gate=gates[:, gate_col:gate_col + 1], resid=x, out=x)

        def top_experts_layer():
            with memory(nc) as (sb, ps):
                b, loads = buffers(sb, "f0.router f0.score_bias f0.gate_w f0.up_w f0.down_w")
                probs = sb("probs", [P, TILES, 32])
                corrected = sb("corrected", [P, TILES, 32])
                threshold = sb("threshold", [P, TILES])
                total = sb("total", [P, TILES])
                combine = sb("combine", [P, TILES, 34])
                wide = [P, TILES, 32]
                layer_norm(nc, const, x, t_outs=[(xt, None, None)], loads=loads)
                router(nc, const, xt, b["router"][:], None, probs, 32)
                add_all(nc, corrected[:], probs[:], spread(b["score_bias"][:, None, :], wide))
                rank_largest(nc, corrected, threshold, 32, 6)
                pick_first(nc, corrected[:], threshold, 6, corrected, 32)
                combine_weights(nc, probs, corrected, total, combine, 32)
                mix_top_experts(nc, const, src_t=xt, gate_w=b["gate_w"], up_w=b["up_w"], down_w=b["down_w"],
                                combine=combine, resid=x, gate=gates[:, 4:5])

        def transformer_block_layer():
            with memory(nc) as (sb, ps):
                ctx = sb("ctx", [P, TILES, CTX])
                b, loads = buffers(sb, "x1.ln1_g x1.ln1_b x1.ln2_g x1.ln2_b")
                layer_norm(nc, const, x, row_out=h, loads=loads + [(ctx[:], w["ctx"].rearrange("t p d -> p t d"))])
                layer_norm(nc, const, h, row_out=z, row_affine=(b["ln1_g"], b["ln1_b"]))
                for a in ("a1", "a2"):
                    with memory(nc) as (sb2, _):
                        names = "wq wk wv li1_w li1_b lnx_g lnx_b lny_g lny_b ln3_g ln3_b li2_w li2_b li3_w li3_b"
                        v, loads = buffers(sb2, " ".join(f"{a}.{n}" for n in names.split()))
                        keep = sb2("keep", [P, P])
                        loads.append((keep[:], w["later"]))
                        load_weights(nc, loads)
                        if a == "a1":
                            layer_norm(nc, const, z, t_outs=[(xt, v["lnx_g"][:, 0:1], v["lnx_b"][:, 0:1]),
                                                             (yt, v["lny_g"][:, 0:1], v["lny_b"][:, 0:1])])
                        else:
                            layer_norm(nc, const, z, t_outs=[(xt, v["lnx_g"][:, 0:1], v["lnx_b"][:, 0:1])])
                            layer_norm(nc, const, ctx, width=CTX, t_outs=[(yt, v["lny_g"][:, 0:1], v["lny_b"][:, 0:1])])
                        kv_rows = D if a == "a1" else CTX
                        attention(nc, const, heads=16, dk=32, groups=4, kv_rows=kv_rows,
                                  q_src=lambda t: tile_cols(xt, t),
                                  kv_src=lambda t: yt[0:kv_rows, bass.ds(t * P, P)],
                                  wq=v["wq"], wk=v["wk"], wv=v["wv"][:], wo=v["li1_w"], o_bias=v["li1_b"][:], scale=32 ** -0.5,
                                  keep_mask=keep if a == "a1" else None, resid=z, out=h)
                        layer_norm(nc, const, h, t_outs=[(xt, v["ln3_g"][:, 0:1], v["ln3_b"][:, 0:1])])
                        feed_forward(nc, const, src_t=xt, up=v["li2_w"], up_bias=v["li2_b"], down=v["li3_w"],
                                     down_bias=v["li3_b"][:], rows=P, chunks=4, act_func=ACT.Gelu, resid=h)
                    add_all(nc, z[:], z[:], h[:])
                    if a == "a1":
                        layer_norm(nc, const, z, row_out=z, row_affine=(b["ln2_g"], b["ln2_b"]))
                add_all(nc, x[:], z[:], x[:], gates[:, 1:2])

        def chosen_tokens_layer():
            experts, capacity = 8, TOKENS // 8
            with memory(nc) as (sb, ps):
                b, loads = buffers(sb, "f1.router f1.router_b f1.up_w f1.up_b f1.down_w f1.down_b")
                probs = sb("probs", [P, TILES, experts])
                above = sb("above", [P, TILES, experts])
                equal = sb("equal", [P, TILES, experts])
                ranks = sb("ranks", [P, TILES, experts])
                threshold = sb("threshold", [P, experts])
                missing = sb("missing", [P, experts])
                wide = [P, TILES, experts]
                layer_norm(nc, const, x, t_outs=[(xt, None, None)], loads=loads)
                router(nc, const, xt, b["router"][:], b["router_b"], probs, experts)
                expert_thresholds(nc, const, probs, threshold, missing, equal, above, experts, capacity)
                ranks_over_tokens(nc, const, equal, ranks, experts)
                chosen_weights(nc, probs, above, equal, ranks, missing, gates[:, 5:6], experts)
                mix_chosen_tokens(nc, const, src_t=xt, up_w=b["up_w"], up_b=b["up_b"], down_w=b["down_w"], down_b=b["down_b"],
                                  weights=probs[:].rearrange("p t e -> p (t e)"), resid=x)

        def local_transformer_layer():
            layer_norm(nc, const, x, row_out=z)
            for layer in range(2):
                with memory(nc) as (sb, ps):
                    names = "wqkv q_scale k_scale q_scale_swap k_scale_swap wo ln_g ln_b wa wg ba bg w2 b2"
                    b, loads = buffers(sb, " ".join(f"f2.{layer}.{n}" for n in names.split()))
                    mask = sb("mask", [P, 4 * P])
                    tables = sb("tables", [P, 4, 64])
                    loads += [(mask[:], w["window_mask"]), (tables[:], w["rotary_tables"])]
                    shift_tokens(nc, const, z, h)
                    layer_norm(nc, const, h, t_outs=[(xt, None, None)], normalize=False, loads=loads)
                    scale_rotary_tables(nc, tables, (b["q_scale"], b["q_scale_swap"], b["k_scale"], b["k_scale_swap"]))
                    attention(nc, const, heads=8, dk=64, groups=4, kv_rows=D, q_src=None,
                              kv_src=lambda t: tile_cols(xt, t), wq=b["wqkv"][:, 0:512], wk=b["wqkv"][:, 512:1024],
                              wv=b["wqkv"][:, 1024:1536], wo=b["wo"], scale=8.0, add_mask=mask[:],
                              rotary=[tables[:, i, :] for i in range(4)], resid=z, out=z)
                    shift_tokens(nc, const, z, h)
                    layer_norm(nc, const, h, t_outs=[(xt, b["ln_g"][:, 0:1], b["ln_b"][:, 0:1])])
                    feed_forward(nc, const, src_t=xt, up=b["wg"], up_bias=b["bg"], value=b["wa"], value_bias=b["ba"], down=b["w2"],
                                 down_bias=b["b2"][:], rows=114, chunks=3, act_func=ACT.Gelu, resid=z)
            add_all(nc, x[:], z[:], x[:], gates[:, 6:7])

        def capacity_experts_layer():
            experts, capacity = 8, TOKENS // 8
            with memory(nc) as (sb, ps):
                names = "wq wk wv bq bk bv wo bo ln1_g ln1_b ln2_g ln2_b router"
                b, loads = buffers(sb, " ".join(f"f3.{n}" for n in names.split()))
                merged = sb("merged", [P, experts * D])
                merged_b = sb("merged_b", [1, experts * D])
                mask = sb("mask", [P, P])
                loads.append((mask[:], w["block_mask"]))
                with memory(nc) as (sb2, _):
                    e, e_loads = buffers(sb2, "f3.w1_t f3.w2 f3.b1 f3.b2")
                    layer_norm(nc, const, x, row_out=z, t_outs=[(xt, None, None)], loads=loads + e_loads)
                    merge_linear_experts(nc, const, e["w1_t"], e["w2"], e["b1"], e["b2"], merged, merged_b, experts, 4)
                by_token = xt[:].rearrange("p (l n c) -> p n c l", l=TILES, c=4)
                out_by_token = yt[:].rearrange("p (l n c) -> p n c l", l=TILES, c=4)
                attention(nc, const, heads=4, dk=32, groups=1, kv_rows=D,
                          q_src=lambda t: by_token[:, bass.ds(t, 1), :, :].rearrange("p n c l -> p (n c) l"),
                          kv_src=lambda t: by_token[:, bass.ds(t, 1), :, :].rearrange("p n c l -> p (n c) l"),
                          wq=b["wq"], wk=b["wk"], wv=b["wv"][:], q_bias=b["bq"], k_bias=b["bk"], v_bias=b["bv"][:],
                          scale=float(1.0 / np.float32(np.sqrt(32))), add_mask=mask[:],
                          turned_out=lambda t: out_by_token[:, bass.ds(t, 1), :, :].rearrange("p n c l -> p (n c) l"))
                project_rows(nc, const, src_t=yt, weight=b["wo"][:], bias=b["bo"][:], resid=z, out=h)
                layer_norm(nc, const, h, row_out=z, row_affine=(b["ln1_g"], b["ln1_b"]))
                layer_norm(nc, const, z, t_outs=[(xt, None, None)], normalize=False)
                probs = sb("probs", [P, TILES, experts])
                picked = sb("picked", [P, TILES, experts])
                ranks = sb("ranks", [P, TILES, experts])
                most = sb("most", [P, TILES])
                router(nc, const, xt, b["router"][:], None, probs, experts)
                most_probable(nc, probs, most)
                pick_first(nc, probs[:], most, 1, picked, experts)
                ranks_over_tokens(nc, const, picked, ranks, experts)
                capped_weights(nc, probs, picked, ranks, capacity)
                mix_merged_experts(nc, const, src_t=xt, merged=merged, merged_b=merged_b,
                                   weights=probs[:].rearrange("p t e -> p (t e)"), resid=z, experts=experts)
                layer_norm(nc, const, z, row_out=h, row_affine=(b["ln2_g"], b["ln2_b"]))
                add_all(nc, x[:], h[:], x[:], gates[:, 7:8])

        for n in range(start, until):
            if n in (0, 4, 6):
                cross_attention(f"x{n // 2}", n // 2, n != 4)
            elif n == 1:
                top_experts_layer()
            elif n == 2:
                transformer_block_layer()
            elif n == 3:
                chosen_tokens_layer()
            elif n == 5:
                local_transformer_layer()
            else:
                capacity_experts_layer()

        with stage(nc, "stored") as (block, s):

            @block.sync
            def _(sp):
                sp.dma_start(out.rearrange("t p d -> p t d"), x[:]).then_inc(s["stored"], 16)
                sp.wait_ge(s["stored"], 16)


def load_weights(nc, loads):
    with stage(nc, "loaded") as (block, s):

        @block.sync
        def _(sp):
            for dst, source in loads:
                sp.dma_start(dst, source).then_inc(s["loaded"], 16)
            sp.wait_ge(s["loaded"], 16 * len(loads))



def rotary_tables():
    half_idx = np.arange(0, 64, 2, dtype=np.float32)
    inv_freq = (1.0 / 10000.0 ** (half_idx / 64)).astype(np.float32)
    t = np.arange(P, dtype=np.float32)
    freqs = np.concatenate([t[:, None] * inv_freq[None, :]] * 2, axis=-1)
    base = (half_idx + np.float32(0.4 * 64)) / np.float32(1.4 * 64)
    power = (t - P // 2) / np.float32(32)
    scale = np.concatenate([base[None, :] ** power[:, None]] * 2, axis=-1)
    sign = np.concatenate([-np.ones(32), np.ones(32)]).astype(np.float32)
    cos, sin = np.cos(freqs), np.sin(freqs) * sign
    return np.stack([cos * scale, sin * scale, cos / scale, sin / scale], axis=1).astype(np.float32)


def layout(a):
    def rows(v):
        return np.repeat(np.asarray(v)[None, :], P, axis=0)

    def col(v):
        return np.asarray(v)[:, None]

    def slots(m, dk):
        m = np.asarray(m).reshape(-1, 16, dk)
        wide = np.zeros((m.shape[0], 16, 32), m.dtype)
        wide[:, :, :dk] = m
        return wide.reshape(m.shape[0], 512)

    def on_partitions(m, chunk):
        m = np.asarray(m)
        chunks = -(-m.shape[0] // chunk)
        wide = np.zeros((chunks * chunk,) + m.shape[1:], m.dtype)
        wide[:m.shape[0]] = m
        return np.moveaxis(wide.reshape((chunks, chunk) + m.shape[1:]), 0, 1)

    def padded_cols(m, n):
        m = np.asarray(m)
        wide = np.zeros(m.shape[:-1] + (n,), m.dtype)
        wide[..., :m.shape[-1]] = m
        return wide

    def swapped(v):
        return np.concatenate([v[32:], v[:32]])

    w = {}
    i, j = np.arange(P)[:, None], np.arange(P)[None, :]
    w["ident"] = (i == j).astype(np.float32)
    w["earlier"] = (i < j).astype(np.float32)
    w["previous"] = (i == j - 1).astype(np.float32)
    w["later"] = (j > i).astype(np.float32)
    w["window_mask"] = np.tile(np.where((j <= i) & (i - j <= 64), 0.0, -1e30).astype(np.float32), (1, 4))
    w["block_mask"] = np.where(i // 32 == j // 32, 0.0, -1e30).astype(np.float32)
    w["rotary_tables"] = rotary_tables()
    w["x"] = a["x"]
    w["ctx"] = a["ctx_512"]
    w["ctx_t"] = np.asarray(a["ctx_512"]).reshape(TOKENS, CTX).T
    w["gates"] = np.concatenate([rows(a["g_xattn"]), rows(a["g_ffn"])], axis=1)
    for k in (0, 3):
        p = f"L{k}_xattn_"
        w[f"x{k}.wq"] = slots(a[p + "Wq"], 8)
        w[f"x{k}.wk"] = slots(a[p + "Wk"], 8)
        w[f"x{k}.wv"] = a[p + "Wv"]
        w[f"x{k}.wo"] = np.asarray(a[p + "Wo"])[:, None, :]
        w[f"x{k}.bq"] = slots(a[p + "bq"], 8).reshape(4, P).T
        w[f"x{k}.bk"] = slots(a[p + "bk"], 8).reshape(4, P).T
        w[f"x{k}.bv"] = np.asarray(a[p + "bv"])[None, :]
        w[f"x{k}.bo"] = np.asarray(a[p + "bo"])[None, :]
    kv = np.asarray(a["L2_xattn_Wkv"])
    w["x2.wq"] = slots(np.asarray(a["L2_xattn_Wq"]).T, 8)
    w["x2.wk"] = slots(kv[:D].T, 8)
    w["x2.wv"] = kv[D:].T
    w["x2.wo"] = np.asarray(a["L2_xattn_Wo"]).T[:, None, :]

    gate_up = np.asarray(a["L0_ffn_gate_up_proj"])
    w["f0.router"] = np.asarray(a["L0_ffn_router_weight"]).T
    w["f0.score_bias"] = rows(a["L0_ffn_e_score_bias"])
    w["f0.gate_w"] = np.concatenate([gate_up[:, :64].reshape(2048, D), a["L0_ffn_shared_gate_w"]]).T
    w["f0.up_w"] = np.concatenate([gate_up[:, 64:].reshape(2048, D), a["L0_ffn_shared_up_w"]]).T
    down = np.concatenate([np.moveaxis(np.asarray(a["L0_ffn_down_proj"]), 2, 1).reshape(2048, D),
                           np.asarray(a["L0_ffn_shared_down_w"]).T])
    w["f0.down_w"] = on_partitions(down, P)

    for n in ("ln1_g", "ln1_b", "ln2_g", "ln2_b"):
        w[f"x1.{n}"] = rows(a[f"L1_xattn_{n}"])
    for k in ("a1", "a2"):
        p = f"L1_xattn_{k}_"
        for n in ("wq", "wk", "wv"):
            w[f"{k}.{n}"] = np.moveaxis(np.asarray(a[p + n]), 0, 1).reshape(-1, 512)
        w[f"{k}.li1_w"] = on_partitions(a[p + "li1_w"], P)
        w[f"{k}.li1_b"] = np.asarray(a[p + "li1_b"])[None, :]
        for n in ("lnx_g", "lnx_b", "lny_g", "lny_b", "ln3_g", "ln3_b"):
            w[f"{k}.{n}"] = col(a[p + n])
        w[f"{k}.li2_w"] = a[p + "li2_w"]
        w[f"{k}.li2_b"] = np.asarray(a[p + "li2_b"]).reshape(4, P).T
        w[f"{k}.li3_w"] = on_partitions(a[p + "li3_w"], P)
        w[f"{k}.li3_b"] = np.asarray(a[p + "li3_b"])[None, :]

    w["f1.router"] = a["L1_ffn_Wr"]
    w["f1.router_b"] = rows(a["L1_ffn_br"])
    w["f1.up_w"] = np.moveaxis(padded_cols(a["L1_ffn_W_up"], 342), 0, 1).reshape(D, 4 * 342)
    w["f1.up_b"] = padded_cols(a["L1_ffn_b_up"], 342).reshape(12, 114).T
    w["f1.down_w"] = on_partitions(np.moveaxis(np.asarray(a["L1_ffn_W_down"]), 0, 1).reshape(341, 8 * D), 114)
    w["f1.down_b"] = np.asarray(a["L1_ffn_b_down"]).reshape(1, 8 * D)

    for k in range(2):
        q, p = f"f2.{k}.", "L2_ffn_"
        w[q + "wqkv"] = np.asarray(a[p + "wqkv"])[k]
        for n in ("q_scale", "k_scale"):
            w[q + n] = rows(np.asarray(a[p + n])[k])
            w[q + n + "_swap"] = rows(swapped(np.asarray(a[p + n])[k]))
        w[q + "wo"] = on_partitions(np.asarray(a[p + "wo"])[k], P)
        w[q + "ln_g"] = col(np.asarray(a[p + "ln_g"])[k])
        w[q + "ln_b"] = col(np.asarray(a[p + "ln_b"])[k])
        w1, b1 = np.asarray(a[p + "w1"])[k], np.asarray(a[p + "b1"])[k]
        w[q + "wa"] = padded_cols(w1[:, :341], 342)
        w[q + "wg"] = padded_cols(w1[:, 341:], 342)
        w[q + "ba"] = padded_cols(b1[:341], 342).reshape(3, 114).T
        w[q + "bg"] = padded_cols(b1[341:], 342).reshape(3, 114).T
        w[q + "w2"] = on_partitions(np.asarray(a[p + "w2"])[k], 114)
        w[q + "b2"] = np.asarray(a[p + "b2"])[k][None, :]

    proj, proj_b = np.asarray(a["L3_ffn_in_proj_w"]), np.asarray(a["L3_ffn_in_proj_b"])
    for k, n in enumerate("qkv"):
        w[f"f3.w{n}"] = proj[k * D:(k + 1) * D].T
    w["f3.bq"], w["f3.bk"] = col(proj_b[:D]), col(proj_b[D:2 * D])
    w["f3.bv"] = proj_b[None, 2 * D:]
    w["f3.wo"] = np.asarray(a["L3_ffn_out_proj_w"]).T
    w["f3.bo"] = np.asarray(a["L3_ffn_out_proj_b"])[None, :]
    for n in ("ln1_g", "ln1_b", "ln2_g", "ln2_b"):
        w[f"f3.{n}"] = rows(a[f"L3_ffn_{n}"])
    w["f3.router"] = a["L3_ffn_wg"]
    w["f3.w1_t"] = np.transpose(np.asarray(a["L3_ffn_w1"]).reshape(8, D, 4, P), (3, 2, 0, 1))
    w["f3.w2"] = np.transpose(np.asarray(a["L3_ffn_w2"]).reshape(8, 4, P, D), (2, 1, 0, 3))
    w["f3.b1"] = np.transpose(np.asarray(a["L3_ffn_b1"]).reshape(8, 4, P), (2, 1, 0))
    w["f3.b2"] = np.asarray(a["L3_ffn_b2"]).reshape(1, 8 * D)
    return {name: np.ascontiguousarray(v) for name, v in w.items()}


def kernel(**inputs):
    from concourse import bacc
    from concourse.bass_utils import run_bass_kernel_spmd

    nc = bacc.Bacc("TRN2", target_bir_lowering=False, num_devices=1)
    laid_out = layout(inputs)
    arrays = {"in_" + name.replace(".", "_"): v for name, v in laid_out.items()}
    tensors = {name: nc.dram_tensor("in_" + name.replace(".", "_"), v.shape, F32, kind="ExternalInput").ap()
               for name, v in laid_out.items()}
    out = nc.dram_tensor("out", (TILES, P, D), F32, kind="ExternalOutput").ap()
    program(nc, tensors, out)
    result = run_bass_kernel_spmd(nc, [arrays], core_ids=[0])
    return np.asarray(result.results[0]["out"])
```

```python
from contextlib import ExitStack, contextmanager

import numpy as np

import concourse.bass as bass
from concourse import mybir

ALU = mybir.AluOpType
ACT = mybir.ActivationFunctionType
AX = mybir.AxisListType
F32 = mybir.dt.float32
I32 = mybir.dt.int32
BF16 = mybir.dt.bfloat16

P = 128
TILES = 32
D = 128
CTX = 64
TOKENS = TILES * P
BANK = 512
EPS = 1e-5


@contextmanager
def stage(nc, names):
    semaphores = {name: nc.alloc_semaphore(nc.get_next_instruction_name() + name) for name in names.split()}
    with nc.Block() as block:
        yield block, semaphores
    nc.clear_and_free_semaphores(list(semaphores.values()))
    nc.all_engine_barrier()


@contextmanager
def memory(nc):
    with ExitStack() as held:
        def sb(name, shape, dtype=F32):
            return held.enter_context(nc.sbuf_tensor(nc.get_next_instruction_name() + name, shape, dtype))

        def ps(name, shape):
            return held.enter_context(nc.psum_tensor(nc.get_next_instruction_name() + name, shape, F32))

        yield sb, ps


def tile_cols(tensor, t, n=1):
    return tensor[:, bass.ds(t * P, n * P)]


def spread(ap, shape):
    return ap.to_broadcast(shape)



def layer_norm(nc, const, src, width=D, t_outs=(), row_out=None, row_affine=None, loads=(), normalize=True):
    second = len(t_outs) > 1
    turned_out = bool(t_outs)
    with memory(nc) as (sb, ps):
        stats = sb("stats", [P, TILES, 6])
        work = sb("work", [P, 4, TILES])
        std = sb("std", [P, TILES])
        mean = sb("mean", [P, TILES])
        rstd = sb("rstd", [P, TILES])
        xn = sb("xn", [P, 8, D])
        scaled = sb("scaled", [P, 8, width])
        bank = ps("turned", [P, 2, BANK])
        with stage(nc, "loaded stats_done chain std_ready xn_ready turned first_copied second_copied "
                       "row_scaled row_done padded") as (block, s):

            @block.sync
            def _(sp):
                for dst, source in loads:
                    sp.dma_start(dst, source).then_inc(s["loaded"], 16)
                if loads:
                    sp.wait_ge(s["loaded"], 16 * len(loads))

            @block.vector
            def _(dve):
                if normalize:
                    with dve.Fori(0, TILES // 8) as it:
                        for u in range(8):
                            nc.vector.bn_stats(stats[:, bass.ds(it * 8 + u, 1), :],
                                               src[:, bass.ds(it * 8 + u, 1), :]).then_inc(s["stats_done"], 1)
                    dve.wait_ge(s["stats_done"], TILES)
                    nc.vector.tensor_tensor(work[:, 0, :], stats[:, :, 1], stats[:, :, 4], ALU.add).then_inc(s["chain"], 1)
                    nc.vector.tensor_tensor(work[:, 1, :], stats[:, :, 1], stats[:, :, 4],
                                            ALU.subtract).then_inc(s["chain"], 1)
                    nc.vector.tensor_tensor(work[:, 2, :], stats[:, :, 2], stats[:, :, 5], ALU.add).then_inc(s["chain"], 1)
                    dve.wait_ge(s["chain"], 3)
                    nc.vector.tensor_scalar(mean[:], work[:, 0, :], 0.5, None, ALU.mult).then_inc(s["chain"], 1)
                    nc.vector.tensor_tensor(work[:, 3, :], work[:, 1, :], work[:, 1, :], ALU.mult).then_inc(s["chain"], 1)
                    dve.wait_ge(s["chain"], 5)
                    nc.vector.scalar_tensor_tensor(out=work[:, 0, :], in0=work[:, 3, :], scalar=width / 4.0,
                                                   in1=work[:, 2, :], op0=ALU.mult, op1=ALU.add).then_inc(s["chain"], 1)
                    dve.wait_ge(s["std_ready"], 1)
                    nc.vector.reciprocal(rstd[:], std[:]).then_inc(s["chain"], 1)
                    dve.wait_ge(s["chain"], 7)
                if width < D:
                    dve.wait_ge(s["padded"], 1)
                with dve.Fori(0, TILES // 8) as it:
                    for half in range(2):
                        bank_no = it * 2 + half
                        if turned_out:
                            dve.wait_ge(s["turned"], bank_no + 1)
                        if row_out is not None:
                            dve.wait_ge(s["row_done"], bank_no + 1)
                        for k in range(4):
                            u = half * 4 + k
                            t = it * 8 + u
                            if normalize:
                                ins = nc.vector.tensor_scalar(xn[:, u:u + 1, 0:width], src[:, bass.ds(t, 1), :],
                                                              mean[:, bass.ds(t, 1)], rstd[:, bass.ds(t, 1)],
                                                              ALU.subtract, ALU.mult)
                            else:
                                ins = nc.vector.tensor_copy(xn[:, u:u + 1, 0:width], src[:, bass.ds(t, 1), :])
                            ins.then_inc(s["xn_ready"], 1)
                    if second:
                        for half in range(2):
                            bank_no = it * 2 + half
                            dst, gain, shift = t_outs[1]
                            dve.wait_ge(s["first_copied"], bank_no + 3)
                            nc.vector.tensor_scalar(dst[0:width, bass.ds(bank_no * BANK, BANK)],
                                                    bank[0:width, half, :], gain, shift,
                                                    ALU.mult, ALU.add).then_inc(s["second_copied"], 1)

            @block.tensor
            def _(pe):
                if not turned_out:
                    return
                pe.sem_inc(s["turned"], 2)
                with pe.Fori(0, TILES // 8) as it:
                    for half in range(2):
                        bank_no = it * 2 + half
                        pe.wait_ge(s["first_copied"], bank_no + 1)
                        if second:
                            pe.wait_ge(s["second_copied"], bank_no + 1)
                        pe.wait_ge(s["xn_ready"], bank_no * 4 + 4)
                        for k in range(4):
                            last = nc.tensor.transpose(bank[:, half, k * P:(k + 1) * P],
                                                       xn[:, half * 4 + k, :], const["ident"][:])
                        last.then_inc(s["turned"], 1)

            @block.scalar
            def _(act):
                act.sem_inc(s["first_copied"], 2)
                act.sem_inc(s["second_copied"], 2)
                if normalize:
                    act.wait_ge(s["chain"], 6)
                    nc.scalar.activation(std[:], work[:, 0, :], ACT.Sqrt, bias=const["eps"][:, 0:1],
                                         scale=1.0 / width).then_inc(s["std_ready"], 1)
                if not turned_out:
                    return
                dst, gain, shift = t_outs[0]
                with act.Fori(0, TILES // 8) as it:
                    for half in range(2):
                        bank_no = it * 2 + half
                        act.wait_ge(s["turned"], bank_no + 3)
                        out = dst[0:width, bass.ds(bank_no * BANK, BANK)]
                        if gain is None:
                            ins = nc.scalar.activation(out, bank[0:width, half, :], ACT.Copy)
                        else:
                            ins = nc.scalar.activation(out, bank[0:width, half, :], ACT.Identity,
                                                       bias=shift, scale=gain)
                        ins.then_inc(s["first_copied"], 1)

            @block.gpsimd
            def _(pool):
                if width < D:
                    nc.gpsimd.memset(xn[:], 0.0).then_inc(s["padded"], 1)
                if row_out is None:
                    return
                pool.sem_inc(s["row_done"], 2)
                with pool.Fori(0, TILES // 8) as it:
                    for half in range(2):
                        bank_no = it * 2 + half
                        dst = row_out[:, bass.ds(bank_no * 4, 4), :]
                        xs, rs = xn[:, half * 4:half * 4 + 4, 0:width], scaled[:, half * 4:half * 4 + 4, :]
                        pool.wait_ge(s["xn_ready"], bank_no * 4 + 4)
                        if row_affine is None:
                            nc.gpsimd.tensor_copy(dst, xs).then_inc(s["row_done"], 1)
                        else:
                            gain, shift = row_affine
                            nc.gpsimd.tensor_tensor(rs, xs, spread(gain[:, None, :], [P, 4, width]),
                                                    ALU.mult).then_inc(s["row_scaled"], 1)
                            pool.wait_ge(s["row_scaled"], bank_no + 1)
                            nc.gpsimd.tensor_tensor(dst, rs, spread(shift[:, None, :], [P, 4, width]),
                                                    ALU.add).then_inc(s["row_done"], 1)



def attention(nc, const, *, heads, dk, kv_rows, q_src, kv_src, wq, wk, wv, scale, head_mask,
              q_bias=None, k_bias=None, v_bias=None, add_mask=None, keep_mask=None, ready=None,
              wo=None, o_bias=None, gate=None, resid=None, out=None, turned_out=None, tiles=TILES):
    steps = heads // 4
    inner = heads * dk
    groups = inner // P
    per_group = heads // groups
    v_cols = dk if keep_mask is not None else dk + 1
    per_bank = heads // 2
    with memory(nc) as (sb, ps):
        qt = sb("qt", [P, 2, inner])
        kt = sb("kt", [P, 2, inner]) if ready is None else None
        masked_k = sb("masked_k", [P, 2, heads, P])
        kv_tile = sb("kv_tile", [kv_rows, 2, P])
        v = sb("v", [P, 2, heads, dk + 1])
        probs = sb("probs", [P, 2, BANK])
        probs_t = sb("probs_t", [P, 2, BANK])
        maxes = sb("maxes", [P, 2, 4])
        sums = sb("sums", [P, 2, heads])
        inv = sb("inv", [P, heads])
        o = sb("o", [P, inner])
        ot = sb("ot", [P, inner])
        p0 = ps("p0", [P, BANK])
        p1 = ps("p1", [P, BANK])
        sc = ps("sc", [P, 2, BANK])
        tp = ps("tp", [P, 2, BANK])
        ov = ps("ov", [P, 2, BANK])
        ov_heads = ov[:, :, 0:per_bank * v_cols].rearrange("p a (h c) -> p a h c", c=v_cols)

        def v_out(h):
            return ov[:, h // per_bank, (h % per_bank) * v_cols:(h % per_bank + 1) * v_cols]

        def slot(u, j):
            return (u * steps + j) % 2

        with stage(nc, "const_ready kv_copied v_done q_done k_done q_copied k_copied "
                       "v_copied keys_masked scores_ready max_ready scores_used probs_ready probs_turned "
                       "probs_t_ready weighed inv_ready o_ready o_turned ot_copied y_done y_used"
                   ) as (block, s):

            @block.tensor
            def _(pe):
                def project_queries(t):
                    if ready is not None:
                        return
                    pe.wait_ge(s["ot_copied"], t + 1)
                    for g in range(groups):
                        last = nc.tensor.matmul(p1[:, g * P:(g + 1) * P], wq[:, g * P:(g + 1) * P], q_src(t),
                                                start=True, stop=True)
                    last.then_inc(s["q_done"], 1)

                def project_keys(t, first=False):
                    if ready is not None:
                        return
                    if wo is not None:
                        pe.wait_ge(s["y_used"], t + 1)
                    elif not first:
                        pe.wait_ge(s["v_copied"], t)
                    for g in range(groups):
                        last = nc.tensor.matmul(p0[:, g * P:(g + 1) * P], wk[:, g * P:(g + 1) * P], kv_src(t),
                                                start=True, stop=True)
                    last.then_inc(s["k_done"], 1)

                def project_values(t, u):
                    pe.wait_ge(s["kv_copied"], t + 1)
                    if ready is None:
                        pe.wait_ge(s["k_copied"], t + 1)
                    else:
                        pe.wait_ge(s["y_used"], t + 1)
                    nc.tensor.matmul(p0[:, 0:inner], kv_tile[:, u, :], wv, start=True, stop=True
                                     ).then_inc(s["v_done"], 1)

                def scores(t, u, j):
                    n = t * steps + j
                    if j == 0:
                        pe.wait_ge(s["q_copied"], t + 1)
                    pe.wait_ge(s["keys_masked"], n + 1)
                    pe.wait_ge(s["scores_used"], n + 1)
                    bank = sc[:, slot(u, j), :]
                    if add_mask is not None:
                        nc.tensor.matmul(bank, const["ident_bf16"][:], add_mask, start=True, stop=False,
                                         skip_group_check=True)
                    h = 4 * j
                    while h < 4 * j + 4:
                        g, n_heads = h // per_group, min(4, per_group)
                        cols = slice((h - 4 * j) * P, (h - 4 * j + n_heads) * P)
                        last = nc.tensor.matmul(bank[:, cols], qt[:, u, g * P:(g + 1) * P],
                                                masked_k[:, u, h:h + n_heads, :].rearrange("p h k -> p (h k)"),
                                                start=add_mask is None, stop=True,
                                                skip_group_check=add_mask is not None)
                        h += n_heads
                    last.then_inc(s["scores_ready"], 1)

                def turn_probs(t, u, j):
                    n = t * steps + j
                    pe.wait_ge(s["probs_ready"], n + 1)
                    pe.wait_ge(s["probs_t_ready"], n + 1)
                    for i in range(4):
                        last = nc.tensor.transpose(tp[:, slot(u, j), i * P:(i + 1) * P],
                                                   probs[:, slot(u, j), i * P:(i + 1) * P], const["ident"][:])
                    last.then_inc(s["probs_turned"], 1)

                def weigh(t, u, j):
                    n = t * steps + j
                    pe.wait_ge(s["probs_t_ready"], n + 3)
                    if j == 0:
                        pe.wait_ge(s["v_copied"], t + 1)
                        pe.wait_ge(s["o_ready"], t + 1)
                    for i in range(4):
                        h = 4 * j + i
                        last = nc.tensor.matmul(v_out(h), probs_t[:, slot(u, j), i * P:(i + 1) * P],
                                                v[:, u, h, 0:v_cols], start=True, stop=True)
                    last.then_inc(s["weighed"], 1)

                def turn_outputs(t, following=False, last_tile=False):
                    pe.wait_ge(s["o_ready"], t + 2)
                    if steps == 1 and not following:
                        pe.wait_ge(s["ot_copied"], t + 3)
                    if ready is None:
                        if steps == 1 and following:
                            pe.wait_ge(s["q_copied"], t + 3)
                        elif not last_tile:
                            pe.wait_ge(s["q_copied"], t + 2)
                    for c in range(groups):
                        last = nc.tensor.transpose(p1[:, c * P:(c + 1) * P], o[:, c * P:(c + 1) * P],
                                                   const["ident"][:])
                    last.then_inc(s["o_turned"], 1)

                def project_outputs(t, following=False):
                    if wo is None:
                        return
                    pe.wait_ge(s["ot_copied"], t + 3)
                    if following:
                        pe.wait_ge(s["v_copied"], t + 3)
                    for c in range(groups):
                        last = nc.tensor.matmul(p0[:, 0:D], ot[:, c * P:(c + 1) * P], wo[:, c, :], start=c == 0,
                                                stop=c == groups - 1 and o_bias is None)
                    if o_bias is not None:
                        last = nc.tensor.matmul(p0[:, 0:D], const["ones"][0:1, :], o_bias, start=False, stop=True)
                    last.then_inc(s["y_done"], 1)

                def pair(it, first, end):
                    for u in range(2):
                        t = it * 2 + u
                        earlier = not (first and u == 0)
                        following = not (end and u == 1)
                        if steps == 4:
                            scores(t, u, 1)
                            turn_probs(t, u, 0)
                            if earlier:
                                weigh(t - 1, 1 - u, 3)
                            scores(t, u, 2)
                            if following:
                                project_keys(t + 1)
                            turn_probs(t, u, 1)
                            weigh(t, u, 0)
                            if earlier:
                                turn_outputs(t - 1, following)
                            scores(t, u, 3)
                            if following:
                                project_values(t + 1, 1 - u)
                            turn_probs(t, u, 2)
                            if following:
                                project_queries(t + 1)
                            weigh(t, u, 1)
                            if earlier:
                                project_outputs(t - 1, following)
                            if following:
                                scores(t + 1, 1 - u, 0)
                            turn_probs(t, u, 3)
                            weigh(t, u, 2)
                        elif steps == 2:
                            scores(t, u, 1)
                            turn_probs(t, u, 0)
                            if earlier:
                                weigh(t - 1, 1 - u, 1)
                            if following:
                                project_values(t + 1, 1 - u)
                                scores(t + 1, 1 - u, 0)
                            if earlier:
                                turn_outputs(t - 1, following)
                            turn_probs(t, u, 1)
                            weigh(t, u, 0)
                            if earlier:
                                project_outputs(t - 1, following)
                        else:
                            if following:
                                project_queries(t + 1)
                                project_keys(t + 1)
                            turn_probs(t, u, 0)
                            if earlier:
                                weigh(t - 1, 1 - u, 0)
                            if following:
                                project_values(t + 1, 1 - u)
                                scores(t + 1, 1 - u, 0)
                            if earlier:
                                turn_outputs(t - 1, following)

                project_queries(0)
                project_keys(0, True)
                project_values(0, 0)
                scores(0, 0, 0)
                pair(0, True, False)
                with pe.Fori(1, tiles // 2 - 1) as it:
                    pair(it, False, False)
                pair(tiles // 2 - 1, False, True)
                weigh(tiles - 1, 1, steps - 1)
                turn_outputs(tiles - 1, last_tile=True)
                project_outputs(tiles - 1)

            @block.vector
            def _(dve):
                def subtract_max(t, u, j):
                    n = t * steps + j
                    dve.wait_ge(s["scores_ready"], n + 1)
                    scores = sc[:, slot(u, j), :].rearrange("p (g k) -> p g k", k=P)
                    most = maxes[:, slot(u, j), :]
                    nc.vector.tensor_reduce(most, scores, AX.X, ALU.max).then_inc(s["max_ready"], 1)
                    dve.wait_ge(s["probs_turned"], n + 1)
                    dve.wait_ge(s["max_ready"], n + 1)
                    nc.vector.tensor_tensor(probs[:, slot(u, j), :].rearrange("p (g k) -> p g k", k=P), scores,
                                            spread(most[:, :, None], [P, 4, P]),
                                            ALU.subtract).then_inc(s["scores_used"], 1)

                def mask_probs(t, u, j):
                    if keep_mask is None:
                        return
                    dve.wait_ge(s["probs_turned"], t * steps + j + 3)
                    nc.vector.tensor_tensor(probs_t[:, slot(u, j), :].rearrange("p (g k) -> p g k", k=P),
                                            tp[:, slot(u, j), :].rearrange("p (g k) -> p g k", k=P),
                                            spread(keep_mask[:, None, :], [P, 4, P]),
                                            ALU.mult).then_inc(s["probs_t_ready"], 1)

                def normalise(t, u):
                    dve.wait_ge(s["weighed"], (t + 1) * steps)
                    inv_heads = inv[:].rearrange("p (a h) -> p a h", a=2)
                    if keep_mask is None:
                        nc.vector.reciprocal(inv_heads[:, :, :, None], ov_heads[:, :, :, dk:dk + 1]
                                             ).then_inc(s["inv_ready"], 1)
                    else:
                        dve.wait_ge(s["probs_ready"], (t + 1) * steps)
                        nc.vector.reciprocal(inv[:], sums[:, u, :]).then_inc(s["inv_ready"], 1)
                    dve.wait_ge(s["inv_ready"], t + 3)
                    dve.wait_ge(s["o_turned"], t + 1)
                    nc.vector.tensor_tensor(o[:].rearrange("p (a h c) -> p a h c", a=2, c=dk), ov_heads[:, :, :, 0:dk],
                                            spread(inv_heads[:, :, :, None], [P, 2, per_bank, dk]),
                                            ALU.mult).then_inc(s["o_ready"], 1)

                def add_residual(t):
                    if wo is None:
                        return
                    dve.wait_ge(s["y_done"], t + 1)
                    rows = resid[:, bass.ds(t, 1), :]
                    if gate is None:
                        ins = nc.vector.tensor_tensor(out[:, bass.ds(t, 1), :], p0[:, None, 0:D], rows, ALU.add)
                    else:
                        ins = nc.vector.scalar_tensor_tensor(out=out[:, bass.ds(t, 1), :], in0=p0[:, None, 0:D],
                                                             scalar=gate, in1=rows, op0=ALU.mult, op1=ALU.add)
                    ins.then_inc(s["y_used"], 1)

                def copy_queries(t, u):
                    if ready is not None:
                        return
                    dve.wait_ge(s["q_done"], t + 1)
                    if q_bias is None:
                        ins = nc.vector.tensor_copy(qt[:, u, :], p1[:, 0:inner])
                    else:
                        ins = nc.vector.tensor_scalar(qt[:, u, :], p1[:, 0:inner], q_bias[:, 0:1], None, ALU.add)
                    ins.then_inc(s["q_copied"], 1)

                def add_value_bias(t, u):
                    if v_bias is None:
                        return
                    dve.wait_ge(s["v_done"], t + 1)
                    nc.vector.tensor_tensor(v[:, u, :, 0:dk], p0[:, 0:inner].rearrange("p (h c) -> p h c", c=dk),
                                            v_bias.rearrange("p (h c) -> p h c", c=dk),
                                            ALU.add).then_inc(s["v_copied"], 1)

                def pair(it, first, end):
                    for u in range(2):
                        t = it * 2 + u
                        earlier = not (first and u == 0)
                        following = not (end and u == 1)
                        if steps == 4:
                            subtract_max(t, u, 1)
                            mask_probs(t, u, 0)
                            if earlier:
                                normalise(t - 1, 1 - u)
                            subtract_max(t, u, 2)
                            mask_probs(t, u, 1)
                            subtract_max(t, u, 3)
                            if following:
                                add_value_bias(t + 1, 1 - u)
                                copy_queries(t + 1, 1 - u)
                            mask_probs(t, u, 2)
                            if following:
                                subtract_max(t + 1, 1 - u, 0)
                            if earlier:
                                add_residual(t - 1)
                            mask_probs(t, u, 3)
                        elif steps == 2:
                            subtract_max(t, u, 1)
                            if earlier:
                                normalise(t - 1, 1 - u)
                            if following:
                                add_value_bias(t + 1, 1 - u)
                                subtract_max(t + 1, 1 - u, 0)
                            if earlier:
                                add_residual(t - 1)
                        else:
                            if following:
                                copy_queries(t + 1, 1 - u)
                            if earlier:
                                normalise(t - 1, 1 - u)
                            if following:
                                add_value_bias(t + 1, 1 - u)
                                subtract_max(t + 1, 1 - u, 0)

                dve.sem_inc(s["y_used"], 3)
                dve.sem_inc(s["scores_used"], 2)
                dve.sem_inc(s["o_ready"], 1)
                dve.sem_inc(s["inv_ready"], 2)
                dve.wait_ge(s["const_ready"], 1)
                copy_queries(0, 0)
                add_value_bias(0, 0)
                subtract_max(0, 0, 0)
                pair(0, True, False)
                with dve.Fori(1, tiles // 2 - 1) as it:
                    pair(it, False, False)
                pair(tiles // 2 - 1, False, True)
                normalise(tiles - 1, 1)
                add_residual(tiles - 1)

            @block.scalar
            def _(act):
                def exponentials(t, u, j):
                    act.wait_ge(s["scores_used"], t * steps + j + 3)
                    if keep_mask is None:
                        half = probs[:, slot(u, j), :]
                        nc.scalar.activation(half, half, ACT.Exp, scale=scale).then_inc(s["probs_ready"], 1)
                        return
                    if j == 0:
                        act.wait_ge(s["inv_ready"], t + 1)
                    for i in range(4):
                        head = probs[:, slot(u, j), i * P:(i + 1) * P]
                        last = nc.scalar.activation(head, head, ACT.Exp, scale=scale,
                                                    accum_out=sums[:, u, 4 * j + i:4 * j + i + 1])
                    last.then_inc(s["probs_ready"], 1)

                def copy_probs(t, u, j):
                    if keep_mask is not None:
                        return
                    act.wait_ge(s["probs_turned"], t * steps + j + 3)
                    nc.scalar.activation(probs_t[:, slot(u, j), :], tp[:, slot(u, j), :],
                                         ACT.Copy).then_inc(s["probs_t_ready"], 1)

                def copy_turned(t):
                    act.wait_ge(s["o_turned"], t + 2)
                    if wo is None:
                        ins = nc.scalar.activation(turned_out(t), p1[:, 0:inner].rearrange("p (c l) -> p c l", c=4),
                                                   ACT.Copy)
                    else:
                        ins = nc.scalar.activation(ot[:], p1[:, 0:inner], ACT.Copy)
                    ins.then_inc(s["ot_copied"], 1)

                def copy_keys(t, u):
                    if ready is not None:
                        nc.scalar.activation(qt[:, u:u + 1, :], ready[0][:, bass.ds(t, 1), :],
                                             ACT.Copy).then_inc(s["q_copied"], 1)
                        return
                    act.wait_ge(s["k_done"], t + 1)
                    if k_bias is None:
                        ins = nc.scalar.activation(kt[:, u, :], p0[:, 0:inner], ACT.Copy)
                    else:
                        ins = nc.scalar.activation(kt[:, u, :], p0[:, 0:inner], ACT.Identity, bias=k_bias[:, 0:1])
                    ins.then_inc(s["k_copied"], 1)

                def copy_values(t, u):
                    if v_bias is not None:
                        return
                    act.wait_ge(s["v_done"], t + 1)
                    nc.scalar.activation(v[:, u, :, 0:dk], p0[:, 0:inner].rearrange("p (h c) -> p h c", c=dk),
                                         ACT.Copy).then_inc(s["v_copied"], 1)

                def pair(it, first, end):
                    for u in range(2):
                        t = it * 2 + u
                        earlier = not (first and u == 0)
                        following = not (end and u == 1)
                        if steps == 4:
                            exponentials(t, u, 1)
                            copy_probs(t, u, 0)
                            exponentials(t, u, 2)
                            if following:
                                copy_keys(t + 1, 1 - u)
                            copy_probs(t, u, 1)
                            if earlier:
                                copy_turned(t - 1)
                            exponentials(t, u, 3)
                            if following:
                                copy_values(t + 1, 1 - u)
                            copy_probs(t, u, 2)
                            if following:
                                exponentials(t + 1, 1 - u, 0)
                            copy_probs(t, u, 3)
                        elif steps == 2:
                            if following:
                                copy_keys(t + 1, 1 - u)
                            exponentials(t, u, 1)
                            copy_probs(t, u, 0)
                            if following:
                                copy_values(t + 1, 1 - u)
                                exponentials(t + 1, 1 - u, 0)
                            if earlier:
                                copy_turned(t - 1)
                            copy_probs(t, u, 1)
                        else:
                            if following:
                                copy_keys(t + 1, 1 - u)
                            copy_probs(t, u, 0)
                            if following:
                                copy_values(t + 1, 1 - u)
                                exponentials(t + 1, 1 - u, 0)
                            if earlier:
                                copy_turned(t - 1)

                act.sem_inc(s["ot_copied"], 3 if steps == 1 else 2)
                act.sem_inc(s["probs_t_ready"], 2)
                act.wait_ge(s["const_ready"], 1)
                copy_keys(0, 0)
                copy_values(0, 0)
                exponentials(0, 0, 0)
                pair(0, True, False)
                with act.Fori(1, tiles // 2 - 1) as it:
                    pair(it, False, False)
                pair(tiles // 2 - 1, False, True)
                copy_turned(tiles - 1)

            @block.gpsimd
            def _(pool):
                def copy_kv(t, u, first=False):
                    if not first:
                        pool.wait_ge(s["v_done"], t - 1)
                    view = kv_tile[:, u, :]
                    source = kv_src(t)
                    if len(source.shape) == 3:
                        view = view.rearrange("p (c l) -> p c l", c=4)
                    nc.gpsimd.tensor_copy(view, source).then_inc(s["kv_copied"], 1)

                def mask_keys(t, u, j, first=False):
                    if j == 0 and ready is None:
                        pool.wait_ge(s["k_copied"], t + 1)
                    elif j == 0 and not first:
                        pool.wait_ge(s["scores_ready"], (t - 1) * steps)
                    g = 4 * j // per_group
                    n_groups = max(1, 4 // per_group)
                    n_heads = 4 // n_groups
                    wide = [P, n_groups, n_heads, P]
                    cols = slice(g * P, (g + n_groups) * P)
                    if ready is None:
                        keys = kt[:, u, cols].rearrange("p (g k) -> p g k", k=P)
                    else:
                        keys = ready[1][:, bass.ds(t, 1), cols].rearrange("p a (g k) -> p (a g) k", k=P)
                    i = 4 * j % per_group
                    nc.gpsimd.tensor_tensor(
                        masked_k[:, u, 4 * j:4 * j + 4, :].rearrange("p (g h) k -> p g h k", g=n_groups),
                        spread(keys[:, :, None, :], wide),
                        spread(head_mask[:, None, i:i + n_heads, None], wide), ALU.mult).then_inc(s["keys_masked"], 1)

                def pair(it, first, end):
                    for u in range(2):
                        t = it * 2 + u
                        following = not (end and u == 1)
                        second = first and u == 0
                        if following and not second:
                            copy_kv(t + 1, 1 - u)
                        if following:
                            for j in range(steps):
                                mask_keys(t + 1, 1 - u, j, second)

                pool.sem_inc(s["probs_turned"], 2)
                pool.sem_inc(s["o_turned"], 1)
                nc.gpsimd.memset(v[:], 1.0).then_inc(s["const_ready"], 1)
                copy_kv(0, 0, True)
                copy_kv(1, 1, True)
                for j in range(steps):
                    mask_keys(0, 0, j, True)
                pair(0, True, False)
                with pool.Fori(1, tiles // 2 - 1) as it:
                    pair(it, False, False)
                pair(tiles // 2 - 1, False, True)



def rotary_rows(nc, const, *, heads, dk, src_t, wq, wk, tables, turned, tiles):
    inner = heads * dk
    groups = inner // P
    half = dk // 2
    with memory(nc) as (sb, ps):
        x_tile = sb("x_tile", [P, 2, P])
        same = sb("same", [P, 4, heads, dk])
        swap = sb("swap", [P, 4, heads, dk])
        square = sb("square", [P, 4, inner])
        length = sb("length", [P, 4, heads])
        clamped = sb("clamped", [P, 4, heads])
        root = sb("root", [P, 4, heads])
        inv_len = sb("inv_len", [P, 4, heads])
        added = sb("added", [P, 4, heads, dk])
        unit_rows = sb("unit_rows", [P, 2, 2, heads, dk])
        rows = ps("rows", [P, 4, BANK])
        turned_ps = ps("turned_ps", [P, 4, BANK])
        with stage(nc, "x_copied rows_done squared rotated summed clamped rooted inv_ready added_ready "
                       "rows_ready turned_done turned_copied") as (block, s):

            def tile_pairs(engine, body, tail):
                body(0, 0, False, False, True)
                body(1, 1, True, False, True)
                with engine.Fori(1, tiles // 2 - 1) as it:
                    for u in range(2):
                        body(it * 2 + u, u, True, True, True)
                body(tiles - 2, 0, True, True, True)
                body(tiles - 1, 1, True, True, False)
                tail()

            @block.tensor
            def _(pe):
                def project(t, u):
                    pe.wait_ge(s["x_copied"], t + 1)
                    for i, weight in ((0, wq), (1, wk)):
                        pe.wait_ge(s["rotated"], 3 * (2 * t + i) + 3)
                        nc.tensor.matmul(rows[:, 2 * u + i, 0:inner], x_tile[:, u, :], weight, start=True,
                                         stop=True).then_inc(s["rows_done"], 1)

                def turn(t, u):
                    for i in range(2):
                        pe.wait_ge(s["rows_ready"], 2 * t + i + 5)
                        pe.wait_ge(s["turned_copied"], 2 * t + i + 1)
                        flat = unit_rows[:, u, i, :, :].rearrange("p h c -> p (h c)")
                        for g in range(groups):
                            last = nc.tensor.transpose(turned_ps[:, 2 * u + i, g * P:(g + 1) * P],
                                                       flat[:, g * P:(g + 1) * P], const["ident"][:])
                        last.then_inc(s["turned_done"], 1)

                def body(t, u, earlier, before, following):
                    if following:
                        project(t + 1, 1 - u)
                    if earlier:
                        turn(t - 1, 1 - u)

                project(0, 0)
                tile_pairs(pe, body, lambda: turn(tiles - 1, 1))

            @block.scalar
            def _(act):
                def copy_x(t, u):
                    nc.scalar.activation(x_tile[:, u, :], src_t(t), ACT.Copy).then_inc(s["x_copied"], 1)

                def square_rows(t, u):
                    for i in range(2):
                        act.wait_ge(s["rows_done"], 2 * t + i + 1)
                        act.wait_ge(s["summed"], 2 * t + i + 1)
                        nc.scalar.activation(square[:, 2 * u + i, :], rows[:, 2 * u + i, 0:inner],
                                             ACT.Square).then_inc(s["squared"], 1)

                def take_roots(t, u):
                    act.wait_ge(s["clamped"], t + 1)
                    nc.scalar.activation(root[:, 2 * u:2 * u + 2, :], clamped[:, 2 * u:2 * u + 2, :],
                                         ACT.Sqrt).then_inc(s["rooted"], 1)

                def copy_out(t, u):
                    for i in range(2):
                        act.wait_ge(s["turned_done"], 2 * t + i + 5)
                        nc.scalar.activation(turned[i][:, bass.ds(t, 1), :], turned_ps[:, 2 * u + i:2 * u + i + 1, 0:inner],
                                             ACT.Copy).then_inc(s["turned_copied"], 1)

                def body(t, u, earlier, before, following):
                    square_rows(t, u)
                    if following:
                        copy_x(t + 1, 1 - u)
                    if earlier:
                        take_roots(t - 1, 1 - u)
                    if before:
                        copy_out(t - 2, u)

                def tail():
                    take_roots(tiles - 1, 1)
                    copy_out(tiles - 2, 0)
                    copy_out(tiles - 1, 1)

                act.sem_inc(s["turned_copied"], 4)
                copy_x(0, 0)
                tile_pairs(act, body, tail)

            @block.vector
            def _(dve):
                def rotate(t, u, i):
                    n = 2 * t + i
                    bank = rows[:, 2 * u + i, 0:inner].rearrange("p (h c) -> p h c", c=dk)
                    c_same, c_swap = tables[2 * i], tables[2 * i + 1]
                    dve.wait_ge(s["squared"], n + 1)
                    dve.wait_ge(s["added_ready"], n + 1)
                    nc.vector.tensor_tensor(same[:, 2 * u + i, :, :], bank, spread(c_same[:, None, :], [P, heads, dk]),
                                            ALU.mult).then_inc(s["rotated"], 1)
                    nc.vector.tensor_tensor(swap[:, 2 * u + i, :, 0:half], bank[:, :, half:dk],
                                            spread(c_swap[:, None, 0:half], [P, heads, half]),
                                            ALU.mult).then_inc(s["rotated"], 1)
                    nc.vector.tensor_tensor(swap[:, 2 * u + i, :, half:dk], bank[:, :, 0:half],
                                            spread(c_swap[:, None, half:dk], [P, heads, half]),
                                            ALU.mult).then_inc(s["rotated"], 1)
                    nc.vector.tensor_reduce(length[:, 2 * u + i, :],
                                            square[:, 2 * u + i, :].rearrange("p (h c) -> p h c", c=dk),
                                            AX.X, ALU.add).then_inc(s["summed"], 1)

                def invert(t, u):
                    dve.wait_ge(s["rooted"], t + 1)
                    dve.wait_ge(s["rows_ready"], 2 * t + 2)
                    nc.vector.reciprocal(inv_len[:, 2 * u:2 * u + 2, :], root[:, 2 * u:2 * u + 2, :]
                                         ).then_inc(s["inv_ready"], 1)

                def body(t, u, earlier, before, following):
                    rotate(t, u, 0)
                    if earlier:
                        invert(t - 1, 1 - u)
                    rotate(t, u, 1)
                    dve.wait_ge(s["summed"], 2 * t + 6)
                    nc.vector.tensor_scalar(clamped[:, 2 * u:2 * u + 2, :], length[:, 2 * u:2 * u + 2, :], 1e-24, None,
                                            ALU.max).then_inc(s["clamped"], 1)

                dve.sem_inc(s["rotated"], 12)
                dve.sem_inc(s["summed"], 4)
                tile_pairs(dve, body, lambda: invert(tiles - 1, 1))

            @block.gpsimd
            def _(pool):
                def scale_rows(t, u):
                    pool.wait_ge(s["inv_ready"], t + 1)
                    for i in range(2):
                        pool.wait_ge(s["turned_done"], 2 * t + i + 1)
                        pool.wait_ge(s["added_ready"], 2 * t + i + 5)
                        nc.gpsimd.tensor_tensor(unit_rows[:, u, i, :, :], added[:, 2 * u + i, :, :],
                                                spread(inv_len[:, 2 * u + i, :, None], [P, heads, dk]),
                                                ALU.mult).then_inc(s["rows_ready"], 1)

                def body(t, u, earlier, before, following):
                    for i in range(2):
                        pool.wait_ge(s["rotated"], 12 + 3 * (2 * t + i) + 3)
                        pool.wait_ge(s["rows_ready"], 2 * t + i + 1)
                        nc.gpsimd.tensor_tensor(added[:, 2 * u + i, :, :], same[:, 2 * u + i, :, :],
                                                swap[:, 2 * u + i, :, :], ALU.add).then_inc(s["added_ready"], 1)
                    if earlier:
                        scale_rows(t - 1, 1 - u)

                pool.sem_inc(s["added_ready"], 4)
                pool.sem_inc(s["rows_ready"], 4)
                pool.sem_inc(s["turned_done"], 4)
                tile_pairs(pool, body, lambda: scale_rows(tiles - 1, 1))



def feed_forward(nc, const, *, src_t, up, up_bias, down, down_bias, rows, chunks, act_func, resid,
                 value=None, value_bias=None):
    gated = value is not None
    with memory(nc) as (sb, ps):
        hidden = sb("hidden", [rows, 2, chunks, BANK])
        acted = sb("acted", [rows, 2, BANK])
        up_ps = ps("up_ps", [P, 2, BANK])
        value_ps = ps("value_ps", [P, 2, BANK])
        down_ps = ps("down_ps", [P, 2, BANK])
        with stage(nc, "up_done value_done acted_ready hidden_ready down_done y_used") as (block, s):

            @block.tensor
            def _(pe):
                def expand(i, b):
                    for c in range(chunks):
                        n = i * chunks + c
                        slot = (b * chunks + c) % 2
                        cols = slice(c * rows, (c + 1) * rows)
                        pe.wait_ge(s["acted_ready"], n + 1)
                        nc.tensor.matmul(up_ps[0:rows, slot, :], up[:, cols], src_t[:, bass.ds(i * BANK, BANK)],
                                         start=True, stop=True).then_inc(s["up_done"], 1)
                        if gated:
                            pe.wait_ge(s["hidden_ready"], n + 1)
                            nc.tensor.matmul(value_ps[0:rows, slot, :], value[:, cols],
                                             src_t[:, bass.ds(i * BANK, BANK)],
                                             start=True, stop=True).then_inc(s["value_done"], 1)

                def contract(i, b):
                    if gated:
                        pe.wait_ge(s["hidden_ready"], (i + 1) * chunks + 2)
                    else:
                        pe.wait_ge(s["acted_ready"], (i + 1) * chunks + 2)
                    pe.wait_ge(s["y_used"], i + 1)
                    for k in range(4):
                        for c in range(chunks):
                            nc.tensor.matmul(down_ps[:, b, k * P:(k + 1) * P], hidden[:, b, c, k * P:(k + 1) * P],
                                             down[:, c, :], start=c == 0, stop=False)
                        last = nc.tensor.matmul(down_ps[:, b, k * P:(k + 1) * P], const["ones"][0:1, :], down_bias,
                                                start=False, stop=True)
                    last.then_inc(s["down_done"], 1)

                expand(0, 0)
                with pe.Fori(0, TILES // 8 - 1) as it:
                    expand(it * 2 + 1, 1)
                    contract(it * 2, 0)
                    expand(it * 2 + 2, 0)
                    contract(it * 2 + 1, 1)
                expand(TILES // 4 - 1, 1)
                contract(TILES // 4 - 2, 0)
                contract(TILES // 4 - 1, 1)

            @block.scalar
            def _(act):
                act.sem_inc(s["acted_ready"], 2)
                with act.Fori(0, TILES // 8) as it:
                    for b in range(2):
                        i = it * 2 + b
                        for c in range(chunks):
                            n = i * chunks + c
                            slot = (b * chunks + c) % 2
                            act.wait_ge(s["up_done"], n + 1)
                            if gated:
                                act.wait_ge(s["hidden_ready"], n + 1)
                                dst = acted[:, slot, :]
                            else:
                                if c == 0:
                                    act.wait_ge(s["down_done"], i + 1)
                                dst = hidden[:, b, c, :]
                            nc.scalar.activation(dst, up_ps[0:rows, slot, :], act_func,
                                                 bias=up_bias[0:rows, c:c + 1]).then_inc(s["acted_ready"], 1)

            @block.vector
            def _(dve):
                dve.sem_inc(s["hidden_ready"], 2)
                dve.sem_inc(s["y_used"], 2)
                dve.sem_inc(s["down_done"], 2)

                def multiply(i, b):
                    if not gated:
                        return
                    for c in range(chunks):
                        n = i * chunks + c
                        slot = (b * chunks + c) % 2
                        dve.wait_ge(s["value_done"], n + 1)
                        dve.wait_ge(s["acted_ready"], n + 3)
                        if c == 0:
                            dve.wait_ge(s["down_done"], i + 1)
                        nc.vector.scalar_tensor_tensor(out=hidden[:, b, c, :], in0=value_ps[0:rows, slot, :],
                                                       scalar=value_bias[0:rows, c:c + 1], in1=acted[:, slot, :],
                                                       op0=ALU.add, op1=ALU.mult).then_inc(s["hidden_ready"], 1)

                def add(i, b):
                    dve.wait_ge(s["down_done"], i + 3)
                    rows_ = resid[:, bass.ds(i * 4, 4), :]
                    nc.vector.tensor_tensor(rows_, down_ps[:, b, :].rearrange("p (k d) -> p k d", d=D), rows_,
                                            ALU.add).then_inc(s["y_used"], 1)

                multiply(0, 0)
                with dve.Fori(0, TILES // 8 - 1) as it:
                    multiply(it * 2 + 1, 1)
                    add(it * 2, 0)
                    multiply(it * 2 + 2, 0)
                    add(it * 2 + 1, 1)
                multiply(TILES // 4 - 1, 1)
                add(TILES // 4 - 2, 0)
                add(TILES // 4 - 1, 1)



def router(nc, const, src_t, weight, bias, probs, experts):
    with memory(nc) as (sb, ps):
        tile = sb("tile", [P, 4, P])
        shifted = sb("shifted", [P, TILES, experts])
        most = sb("most", [P, TILES])
        total = sb("total", [P, TILES])
        inv = sb("inv", [P, TILES])
        logits = ps("logits", [P, 2, BANK])
        with stage(nc, "tile_copied logits_done logits_used chain exp_done") as (block, s):

            @block.gpsimd
            def _(pool):
                pool.sem_inc(s["logits_done"], 1)
                with pool.Fori(0, TILES // 4) as it:
                    pool.wait_ge(s["logits_done"], it + 1)
                    nc.gpsimd.tensor_copy(tile[:].rearrange("p k n -> p (k n)"),
                                          src_t[:, bass.ds(it * BANK, BANK)]).then_inc(s["tile_copied"], 1)

            @block.tensor
            def _(pe):
                with pe.Fori(0, TILES // 4) as it:
                    pe.wait_ge(s["tile_copied"], it + 1)
                    pe.wait_ge(s["logits_used"], it + 1)
                    for k in range(4):
                        last = nc.tensor.matmul(logits[:, 0, k * experts:(k + 1) * experts], tile[:, k, :], weight,
                                                start=True, stop=True)
                    last.then_inc(s["logits_done"], 1)

            @block.vector
            def _(dve):
                dve.sem_inc(s["logits_used"], 1)
                with dve.Fori(0, TILES // 4) as it:
                    dve.wait_ge(s["logits_done"], it + 2)
                    src = logits[:, 0, 0:4 * experts].rearrange("p (k e) -> p k e", e=experts)
                    dst = shifted[:, bass.ds(it * 4, 4), :]
                    if bias is None:
                        ins = nc.vector.tensor_copy(dst, src)
                    else:
                        ins = nc.vector.tensor_tensor(dst, src, spread(bias[:, None, :], [P, 4, experts]), ALU.add)
                    ins.then_inc(s["logits_used"], 1)
                dve.wait_ge(s["logits_used"], TILES // 4 + 1)
                nc.vector.tensor_reduce(most[:], shifted[:], AX.X, ALU.max).then_inc(s["chain"], 1)
                dve.wait_ge(s["chain"], 1)
                nc.vector.tensor_tensor(shifted[:], shifted[:], spread(most[:, :, None], [P, TILES, experts]),
                                        ALU.subtract).then_inc(s["chain"], 1)
                dve.wait_ge(s["exp_done"], 1)
                nc.vector.tensor_reduce(total[:], shifted[:], AX.X, ALU.add).then_inc(s["chain"], 1)
                dve.wait_ge(s["chain"], 3)
                nc.vector.reciprocal(inv[:], total[:]).then_inc(s["chain"], 1)
                dve.wait_ge(s["chain"], 4)
                nc.vector.tensor_tensor(probs[:], shifted[:], spread(inv[:, :, None], [P, TILES, experts]),
                                        ALU.mult).then_inc(s["chain"], 1)

            @block.scalar
            def _(act):
                act.wait_ge(s["chain"], 2)
                nc.scalar.activation(shifted[:], shifted[:], ACT.Exp).then_inc(s["exp_done"], 1)


def pick_first(nc, values, threshold, quota, picked, experts):
    with memory(nc) as (sb, ps):
        above = sb("above", [P, TILES, experts])
        equal = sb("equal", [P, TILES, experts])
        ones = sb("ones", [P, TILES * experts])
        upto = sb("upto", [P, TILES, experts])
        before = sb("before", [P, TILES])
        count = sb("count", [P, TILES])
        with stage(nc, "chain") as (block, s):

            @block.vector
            def _(dve):
                wide = [P, TILES, experts]
                nc.vector.memset(ones[:], 1.0).then_inc(s["chain"], 1)
                nc.vector.memset(before[:], 0.0).then_inc(s["chain"], 1)
                nc.vector.tensor_tensor(above[:], values, spread(threshold[:, :, None], wide),
                                        ALU.is_gt).then_inc(s["chain"], 1)
                nc.vector.tensor_tensor(equal[:], values, spread(threshold[:, :, None], wide),
                                        ALU.is_equal).then_inc(s["chain"], 1)
                dve.wait_ge(s["chain"], 4)
                nc.vector.tensor_reduce(count[:], above[:], AX.X, ALU.add).then_inc(s["chain"], 1)
                nc.vector.tensor_tensor_scan(upto[:].rearrange("p t e -> p (t e)"), ones[:],
                                             equal[:].rearrange("p t e -> p (t e)"), 0.0, ALU.mult,
                                             ALU.add).then_inc(s["chain"], 1)
                dve.wait_ge(s["chain"], 6)
                nc.vector.tensor_copy(before[:, 1:TILES], upto[:, 0:TILES - 1, experts - 1]).then_inc(s["chain"], 1)
                dve.wait_ge(s["chain"], 7)
                nc.vector.tensor_tensor(before[:], before[:], count[:], ALU.subtract).then_inc(s["chain"], 1)
                dve.wait_ge(s["chain"], 8)
                nc.vector.tensor_tensor(upto[:], upto[:], spread(before[:, :, None], wide),
                                        ALU.subtract).then_inc(s["chain"], 1)
                dve.wait_ge(s["chain"], 9)
                nc.vector.scalar_tensor_tensor(out=equal[:], in0=upto[:], scalar=float(quota), in1=equal[:],
                                               op0=ALU.is_le, op1=ALU.mult).then_inc(s["chain"], 1)
                dve.wait_ge(s["chain"], 10)
                nc.vector.tensor_tensor(picked[:], above[:], equal[:], ALU.add).then_inc(s["chain"], 1)


def rank_largest(nc, values, threshold, experts, rank):
    with memory(nc) as (sb, ps):
        rows = sb("rows", [P, 8, experts])
        largest = sb("largest", [P, 8, 8])
        scratch = sb("scratch", [P, 1])
        with stage(nc, "rows_copied found taken") as (block, s):

            @block.vector
            def _(dve):
                dve.sem_inc(s["found"], 8)
                dve.sem_inc(s["taken"], 1)
                with dve.Fori(0, TILES // 8) as it:
                    dve.wait_ge(s["found"], it * 8 + 8)
                    nc.vector.tensor_copy(rows[:], values[:, bass.ds(it * 8, 8), :]).then_inc(s["rows_copied"], 1)
                    dve.wait_ge(s["taken"], it + 1)
                    dve.wait_ge(s["rows_copied"], it * 2 + 1)
                    nc.vector.memset(scratch[:], 0.0).then_inc(s["rows_copied"], 1)
                    for k in range(8):
                        nc.vector.max(largest[:, k, :], rows[:, k, :]).then_inc(s["found"], 1)
                    dve.wait_ge(s["found"], it * 8 + 16)
                    nc.vector.tensor_copy(threshold[:, bass.ds(it * 8, 8)],
                                          largest[:, :, rank - 1]).then_inc(s["taken"], 1)


def ranks_over_tokens(nc, const, mask, ranks, experts):
    with memory(nc) as (sb, ps):
        ones = sb("ones", [P, TILES])
        upto = sb("upto", [P, TILES, experts])
        counts = ps("counts", [P, BANK])
        with stage(nc, "ones_set scanned counted copied") as (block, s):

            @block.vector
            def _(dve):
                nc.vector.memset(ones[:], 1.0).then_inc(s["ones_set"], 1)
                dve.wait_ge(s["ones_set"], 1)
                for e in range(experts):
                    nc.vector.tensor_tensor_scan(upto[:, :, e], ones[:], mask[:, :, e], 0.0, ALU.mult,
                                                 ALU.add).then_inc(s["scanned"], 1)
                dve.wait_ge(s["scanned"], experts)
                nc.vector.tensor_tensor(upto[:], upto[:], mask[:], ALU.subtract).then_inc(s["scanned"], 1)
                dve.wait_ge(s["counted"], 1)
                nc.vector.tensor_copy(ranks[:], counts[:, 0:TILES * experts].rearrange("p (t e) -> p t e", e=experts)
                                      ).then_inc(s["copied"], 1)

            @block.tensor
            def _(pe):
                pe.wait_ge(s["scanned"], experts + 1)
                nc.tensor.matmul(counts[:, 0:TILES * experts], const["ones"][:], upto[:].rearrange("p t e -> p (t e)"),
                                 start=True, stop=False)
                nc.tensor.matmul(counts[:, 0:TILES * experts], const["earlier"][:], mask[:].rearrange("p t e -> p (t e)"),
                                 start=False, stop=True).then_inc(s["counted"], 1)


def expert_thresholds(nc, const, probs, threshold, missing, equal, above, experts, capacity):
    with memory(nc) as (sb, ps):
        bit = sb("bit", [P, experts], I32)
        trial = sb("trial", [P, experts])
        passed = sb("passed", [P, TILES, experts])
        count = sb("count", [P, experts])
        kept = sb("kept", [P, experts])
        totals = ps("totals", [P, BANK])
        wide = [P, TILES, experts]
        with stage(nc, "ready tried passed_ready counted summed decided lowered") as (block, s):

            @block.vector
            def _(dve):
                nc.vector.memset(bit[:], 1 << 30).then_inc(s["ready"], 1)
                nc.vector.memset(threshold[:], 0.0).then_inc(s["ready"], 1)
                dve.wait_ge(s["ready"], 2)
                dve.sem_inc(s["lowered"], 2)
                with dve.Fori(0, 31) as i:
                    dve.wait_ge(s["lowered"], i * 2 + 2)
                    nc.vector.tensor_tensor(trial[:].bitcast(I32), threshold[:].bitcast(I32), bit[:],
                                            ALU.bitwise_or).then_inc(s["tried"], 1)
                    dve.wait_ge(s["tried"], i + 1)
                    nc.vector.tensor_tensor(passed[:], probs[:], spread(trial[:, None, :], wide),
                                            ALU.is_ge).then_inc(s["passed_ready"], 1)
                    dve.wait_ge(s["passed_ready"], i + 1)
                    nc.vector.tensor_reduce(count[:], passed[:].rearrange("p t e -> p e t"), AX.X,
                                            ALU.add).then_inc(s["counted"], 1)
                    nc.vector.tensor_single_scalar(bit[:], bit[:], 1, ALU.logical_shift_right).then_inc(s["lowered"], 1)
                    dve.wait_ge(s["summed"], i + 1)
                    nc.vector.scalar_tensor_tensor(out=kept[:], in0=totals[:, 0:experts], scalar=float(capacity),
                                                   in1=trial[:], op0=ALU.is_ge, op1=ALU.mult).then_inc(s["decided"], 1)
                    dve.wait_ge(s["decided"], i + 1)
                    nc.vector.tensor_tensor(threshold[:], threshold[:], kept[:], ALU.max).then_inc(s["lowered"], 1)
                dve.wait_ge(s["lowered"], 64)
                nc.vector.tensor_tensor(above[:], probs[:], spread(threshold[:, None, :], wide),
                                        ALU.is_gt).then_inc(s["ready"], 1)
                nc.vector.tensor_tensor(equal[:], probs[:], spread(threshold[:, None, :], wide),
                                        ALU.is_equal).then_inc(s["ready"], 1)
                dve.wait_ge(s["ready"], 3)
                nc.vector.tensor_reduce(count[:], above[:].rearrange("p t e -> p e t"), AX.X,
                                        ALU.add).then_inc(s["counted"], 1)
                dve.wait_ge(s["summed"], 32)
                nc.vector.tensor_scalar(missing[:], totals[:, 0:experts], -1.0, float(capacity), ALU.mult,
                                        ALU.add).then_inc(s["ready"], 1)

            @block.tensor
            def _(pe):
                with pe.Fori(0, 32) as i:
                    pe.wait_ge(s["counted"], i + 1)
                    nc.tensor.matmul(totals[:, 0:experts], const["ones"][:], count[:], start=True,
                                     stop=True).then_inc(s["summed"], 1)



def mix_top_experts(nc, const, *, src_t, gate_w, up_w, down_w, combine, resid, gate):
    widths = [BANK] * 4 + [P]
    chunks = len(widths)
    with memory(nc) as (sb, ps):
        tile = sb("tile", [P, 2, P])
        acted = sb("acted", [P, 2, BANK])
        product = sb("product", [P, 2, BANK])
        weighted = sb("weighted", [P, 2, BANK])
        hidden_t = sb("hidden_t", [P, 2, BANK])
        gate_ps = ps("gate_ps", [P, 2, BANK])
        up_ps = ps("up_ps", [P, 2, BANK])
        turned_ps = ps("turned_ps", [P, 2, BANK])
        y_ps = ps("y_ps", [P, 2, BANK])
        with stage(nc, "tile_copied projected acted_ready product_ready weighted_ready turned t_copied y_done "
                       "y_used") as (block, s):

            def steps(it, first, end):
                def at(k):
                    if k < 0:
                        return None if first else (it * 2 - 1, 1, k + chunks, (k + 2 * chunks) % 2)
                    u, c = divmod(k, chunks)
                    return (it * 2 + u, u, c, k % 2)

                return [(at(k), at(k - 1), at(k - 2)) for k in range(2 * chunks)]

            @block.tensor
            def _(pe):
                def project(t, u, c, slot):
                    n = t * chunks + c
                    if c == 0:
                        pe.wait_ge(s["tile_copied"], t + 1)
                    pe.wait_ge(s["product_ready"], n + 1)
                    cols = slice(c * BANK, c * BANK + widths[c])
                    nc.tensor.matmul(gate_ps[:, slot, 0:widths[c]], tile[:, u, :], gate_w[:, cols], start=True,
                                     stop=True)
                    nc.tensor.matmul(up_ps[:, slot, 0:widths[c]], tile[:, u, :], up_w[:, cols], start=True,
                                     stop=True).then_inc(s["projected"], 1)

                def turn(t, u, c, slot):
                    n = t * chunks + c
                    pe.wait_ge(s["weighted_ready"], n + 3)
                    pe.wait_ge(s["t_copied"], n + 1)
                    for q in range(widths[c] // P):
                        last = nc.tensor.transpose(turned_ps[:, slot, q * P:(q + 1) * P],
                                                   weighted[:, slot, q * P:(q + 1) * P], const["ident"][:])
                    last.then_inc(s["turned"], 1)

                def contract(t, u, c, slot):
                    n = t * chunks + c
                    pe.wait_ge(s["t_copied"], n + 3)
                    if c == 0:
                        pe.wait_ge(s["y_used"], t + 1)
                    for q in range(widths[c] // P):
                        last = nc.tensor.matmul(y_ps[:, u, 0:D], hidden_t[:, slot, q * P:(q + 1) * P],
                                                down_w[:, 4 * c + q, :], start=c == 0 and q == 0,
                                                stop=c == chunks - 1)
                    if c == chunks - 1:
                        last.then_inc(s["y_done"], 1)

                def pair(it, first, end):
                    for now, before, two_before in steps(it, first, end):
                        project(*now)
                        if before:
                            turn(*before)
                        if two_before:
                            contract(*two_before)

                pair(0, True, False)
                with pe.Fori(1, TILES // 2) as it:
                    pair(it, False, False)
                turn(TILES - 1, 1, chunks - 1, 1)
                contract(TILES - 1, 1, chunks - 2, 0)
                contract(TILES - 1, 1, chunks - 1, 1)

            @block.scalar
            def _(act):
                def activate(t, u, c, slot):
                    act.wait_ge(s["projected"], t * chunks + c + 1)
                    nc.scalar.activation(acted[:, slot, 0:widths[c]], gate_ps[:, slot, 0:widths[c]],
                                         ACT.Silu).then_inc(s["acted_ready"], 1)

                def copy_turned(t, u, c, slot):
                    act.wait_ge(s["turned"], t * chunks + c + 3)
                    nc.scalar.activation(hidden_t[:, slot, 0:widths[c]], turned_ps[:, slot, 0:widths[c]],
                                         ACT.Copy).then_inc(s["t_copied"], 1)

                def pair(it, first, end):
                    for now, before, _ in steps(it, first, end):
                        activate(*now)
                        if before:
                            copy_turned(*before)

                act.sem_inc(s["t_copied"], 2)
                pair(0, True, False)
                with act.Fori(1, TILES // 2) as it:
                    pair(it, False, False)
                copy_turned(TILES - 1, 1, chunks - 1, 1)

            @block.vector
            def _(dve):
                def multiply(t, u, c, slot):
                    n = t * chunks + c
                    dve.wait_ge(s["acted_ready"], n + 1)
                    dve.wait_ge(s["weighted_ready"], n + 1)
                    nc.vector.tensor_tensor(product[:, slot, 0:widths[c]], up_ps[:, slot, 0:widths[c]],
                                            acted[:, slot, 0:widths[c]], ALU.mult).then_inc(s["product_ready"], 1)

                def add(t, u):
                    dve.wait_ge(s["y_done"], t + 1)
                    rows = resid[:, bass.ds(t, 1), :]
                    nc.vector.scalar_tensor_tensor(out=rows, in0=y_ps[:, u:u + 1, 0:D], scalar=gate, in1=rows,
                                                   op0=ALU.mult, op1=ALU.add).then_inc(s["y_used"], 1)

                def pair(it, first, end):
                    for k, (now, _, _) in enumerate(steps(it, first, end)):
                        multiply(*now)
                        if k % chunks == 2 and not (first and k < chunks):
                            add(now[0] - 1, 1 - now[1])

                dve.sem_inc(s["product_ready"], 2)
                dve.sem_inc(s["y_used"], 2)
                pair(0, True, False)
                with dve.Fori(1, TILES // 2) as it:
                    pair(it, False, False)
                add(TILES - 1, 1)

            @block.gpsimd
            def _(pool):
                def copy_tile(t, u):
                    nc.gpsimd.tensor_copy(tile[:, u, :], tile_cols(src_t, t)).then_inc(s["tile_copied"], 1)

                def weight(t, u, c, slot):
                    n = t * chunks + c
                    pool.wait_ge(s["product_ready"], n + 3)
                    pool.wait_ge(s["turned"], n + 1)
                    experts = widths[c] // 64
                    nc.gpsimd.tensor_tensor(
                        weighted[:, slot, 0:widths[c]].rearrange("p (e i) -> p e i", i=64),
                        product[:, slot, 0:widths[c]].rearrange("p (e i) -> p e i", i=64),
                        spread(combine[:, bass.ds(t, 1), c * 8:c * 8 + experts].rearrange("p t e -> p (t e)")[:, :, None],
                               [P, experts, 64]), ALU.mult).then_inc(s["weighted_ready"], 1)

                def pair(it, first, end):
                    for k, (now, _, _) in enumerate(steps(it, first, end)):
                        t, u, c, _slot = now
                        if c == 1 and not (end and u == 1):
                            if not (first and u == 0):
                                pool.wait_ge(s["projected"], t * chunks)
                            copy_tile(t + 1, 1 - u)
                        weight(*now)

                pool.sem_inc(s["weighted_ready"], 2)
                pool.sem_inc(s["turned"], 2)
                copy_tile(0, 0)
                pair(0, True, False)
                with pool.Fori(1, TILES // 2 - 1) as it:
                    pair(it, False, False)
                pair(TILES // 2 - 1, False, True)


def mix_chosen_tokens(nc, const, *, src_t, up_w, up_b, down_w, down_b, weights, resid):
    groups, chunks, rows = 4, 3, 114
    steps = TOKENS // BANK
    with memory(nc) as (sb, ps):
        hidden = sb("hidden", [rows, 2, chunks, BANK])
        up_ps = ps("up_ps", [P, 2, BANK])
        down_ps = ps("down_ps", [P, 2, BANK])
        with stage(nc, "up_done acted_ready down_done added") as (block, s):

            @block.tensor
            def _(pe):
                def expand(it, g):
                    m = it * groups + g
                    for c in range(chunks):
                        slot = (g * chunks + c) % 2
                        pe.wait_ge(s["acted_ready"], m * chunks + c + 1)
                        nc.tensor.matmul(up_ps[0:rows, slot, :], up_w[:, (g * chunks + c) * rows:(g * chunks + c + 1) * rows],
                                         src_t[:, bass.ds(it * BANK, BANK)], start=True, stop=True).then_inc(s["up_done"], 1)

                def contract(it, g):
                    m = it * groups + g
                    pe.wait_ge(s["acted_ready"], (m + 1) * chunks + 2)
                    for k in range(4):
                        n = m * 4 + k
                        pe.wait_ge(s["added"], n * 2 + 6)
                        for c in range(chunks):
                            nc.tensor.matmul(down_ps[:, k % 2, 0:2 * D], hidden[:, g % 2, c, k * P:(k + 1) * P],
                                             down_w[:, c, g * 2 * D:(g + 1) * 2 * D], start=c == 0, stop=False)
                        nc.tensor.matmul(down_ps[:, k % 2, 0:2 * D], const["ones"][0:1, :],
                                         down_b[:, g * 2 * D:(g + 1) * 2 * D], start=False,
                                         stop=True).then_inc(s["down_done"], 1)

                def step(it, end):
                    for g in range(groups):
                        if g < groups - 1:
                            expand(it, g + 1)
                        elif not end:
                            expand(it + 1, 0)
                        contract(it, g)

                expand(0, 0)
                with pe.Fori(0, steps - 1) as it:
                    step(it, False)
                step(steps - 1, True)

            @block.scalar
            def _(act):
                act.sem_inc(s["acted_ready"], 2)
                with act.Fori(0, steps) as it:
                    for g in range(groups):
                        for c in range(chunks):
                            act.wait_ge(s["up_done"], (it * groups + g) * chunks + c + 1)
                            nc.scalar.activation(hidden[:, g % 2, c, :], up_ps[0:rows, (g * chunks + c) % 2, :],
                                                 ACT.Silu, bias=up_b[0:rows, g * chunks + c:g * chunks + c + 1]
                                                 ).then_inc(s["acted_ready"], 1)

            @block.vector
            def _(dve):
                dve.sem_inc(s["added"], 8)
                with dve.Fori(0, steps) as it:
                    for g in range(groups):
                        for k in range(4):
                            n = (it * groups + g) * 4 + k
                            dve.wait_ge(s["down_done"], n + 1)
                            row = resid[:, bass.ds(it * 4 + k, 1), :]
                            for e in range(2):
                                dve.wait_ge(s["added"], n * 2 + 2 if e == 0 else n * 2 + 9)
                                nc.vector.scalar_tensor_tensor(
                                    out=row, in0=down_ps[:, k % 2:k % 2 + 1, e * D:(e + 1) * D],
                                    scalar=weights[:, bass.ds((it * 4 + k) * 8 + g * 2 + e, 1)], in1=row,
                                    op0=ALU.mult, op1=ALU.add).then_inc(s["added"], 1)


def merge_linear_experts(nc, const, w1_t, w2, b1, b2, merged, merged_b, experts, chunks):
    with memory(nc) as (sb, ps):
        w_ps = ps("w_ps", [P, 2, BANK])
        b_ps = ps("b_ps", [P, 2, BANK])
        with stage(nc, "w_done b_done w_copied b_copied") as (block, s):

            @block.tensor
            def _(pe):
                for e in range(experts):
                    if e >= 2:
                        pe.wait_ge(s["w_copied"], e - 1)
                        pe.wait_ge(s["b_copied"], e - 1)
                    for c in range(chunks):
                        last = nc.tensor.matmul(w_ps[:, e % 2, 0:D], w1_t[:, c, e, :], w2[:, c, e, :], start=c == 0,
                                                stop=c == chunks - 1)
                    last.then_inc(s["w_done"], 1)
                    for c in range(chunks):
                        nc.tensor.matmul(b_ps[0:1, e % 2, 0:D], b1[:, c, e:e + 1], w2[:, c, e, :], start=c == 0,
                                         stop=False)
                    nc.tensor.matmul(b_ps[0:1, e % 2, 0:D], const["ones"][0:1, 0:1], b2[0:1, e * D:(e + 1) * D],
                                     start=False, stop=True).then_inc(s["b_done"], 1)

            @block.vector
            def _(dve):
                for e in range(experts):
                    dve.wait_ge(s["w_done"], e + 1)
                    nc.vector.tensor_copy(merged[:, e * D:(e + 1) * D], w_ps[:, e % 2, 0:D]).then_inc(s["w_copied"], 1)

            @block.scalar
            def _(act):
                for e in range(experts):
                    act.wait_ge(s["b_done"], e + 1)
                    nc.scalar.activation(merged_b[0:1, e * D:(e + 1) * D], b_ps[0:1, e % 2, 0:D],
                                         ACT.Copy).then_inc(s["b_copied"], 1)


def mix_merged_experts(nc, const, *, src_t, merged, merged_b, weights, resid, experts):
    halves = experts * D // BANK
    per_bank = experts // halves
    with memory(nc) as (sb, ps):
        tile = sb("tile", [P, 2, P])
        y_ps = ps("y_ps", [P, 2, halves, BANK])
        with stage(nc, "tile_copied y_done added") as (block, s):

            @block.gpsimd
            def _(pool):
                pool.sem_inc(s["y_done"], 2)
                with pool.Fori(0, TILES // 2) as it:
                    for u in range(2):
                        pool.wait_ge(s["y_done"], it * 2 + u + 1)
                        nc.gpsimd.tensor_copy(tile[:, u, :], tile_cols(src_t, it * 2 + u)).then_inc(s["tile_copied"], 1)

            @block.tensor
            def _(pe):
                with pe.Fori(0, TILES // 2) as it:
                    for u in range(2):
                        t = it * 2 + u
                        pe.wait_ge(s["tile_copied"], t + 1)
                        pe.wait_ge(s["added"], (t + 1) * experts)
                        for a in range(halves):
                            cols = slice(a * BANK, (a + 1) * BANK)
                            nc.tensor.matmul(y_ps[:, u, a, :], tile[:, u, :], merged[:, cols], start=True, stop=False)
                            last = nc.tensor.matmul(y_ps[:, u, a, :], const["ones"][0:1, :], merged_b[0:1, cols],
                                                    start=False, stop=True)
                        last.then_inc(s["y_done"], 1)

            @block.vector
            def _(dve):
                dve.sem_inc(s["added"], 2 * experts)
                with dve.Fori(0, TILES // 2) as it:
                    for u in range(2):
                        t = it * 2 + u
                        dve.wait_ge(s["y_done"], t + 3)
                        row = resid[:, bass.ds(t, 1), :]
                        for e in range(experts):
                            dve.wait_ge(s["added"], (t + 2) * experts + e)
                            nc.vector.scalar_tensor_tensor(
                                out=row, in0=y_ps[:, u, e // per_bank:e // per_bank + 1,
                                                  (e % per_bank) * D:(e % per_bank + 1) * D],
                                scalar=weights[:, bass.ds(t * experts + e, 1)], in1=row,
                                op0=ALU.mult, op1=ALU.add).then_inc(s["added"], 1)



def add_all(nc, out, a, b, scale=None):
    with stage(nc, "added") as (block, s):

        @block.vector
        def _(dve):
            if scale is None:
                nc.vector.tensor_tensor(out, a, b, ALU.add).then_inc(s["added"], 1)
            else:
                nc.vector.scalar_tensor_tensor(out=out, in0=a, scalar=scale, in1=b, op0=ALU.mult,
                                               op1=ALU.add).then_inc(s["added"], 1)


def most_probable(nc, probs, most):
    with stage(nc, "found") as (block, s):

        @block.vector
        def _(dve):
            nc.vector.tensor_reduce(most[:], probs[:], AX.X, ALU.max).then_inc(s["found"], 1)


def combine_weights(nc, probs, picked, total, combine, experts):
    with stage(nc, "ones_set weighted summed") as (block, s):

        @block.vector
        def _(dve):
            nc.vector.memset(combine[:], 1.0).then_inc(s["ones_set"], 1)
            nc.vector.tensor_tensor(picked[:], picked[:], probs[:], ALU.mult).then_inc(s["weighted"], 1)
            dve.wait_ge(s["weighted"], 1)
            nc.vector.tensor_reduce(total[:], picked[:], AX.X, ALU.add).then_inc(s["summed"], 1)
            dve.wait_ge(s["summed"], 1)
            nc.vector.tensor_scalar(total[:], total[:], 1e-12, None, ALU.max).then_inc(s["summed"], 1)
            dve.wait_ge(s["summed"], 2)
            nc.vector.reciprocal(total[:], total[:]).then_inc(s["summed"], 1)
            dve.wait_ge(s["summed"], 3)
            dve.wait_ge(s["ones_set"], 1)
            nc.vector.tensor_tensor(combine[:, :, 0:experts], picked[:], spread(total[:, :, None], [P, TILES, experts]),
                                    ALU.mult).then_inc(s["weighted"], 1)


def chosen_weights(nc, probs, above, equal, ranks, missing, gate, experts):
    with stage(nc, "within taken chosen weighted") as (block, s):

        @block.vector
        def _(dve):
            nc.vector.tensor_tensor(ranks[:], ranks[:], spread(missing[:, None, :], [P, TILES, experts]),
                                    ALU.is_lt).then_inc(s["within"], 1)
            dve.wait_ge(s["within"], 1)
            nc.vector.tensor_tensor(equal[:], equal[:], ranks[:], ALU.mult).then_inc(s["taken"], 1)
            dve.wait_ge(s["taken"], 1)
            nc.vector.tensor_tensor(above[:], above[:], equal[:], ALU.add).then_inc(s["chosen"], 1)
            dve.wait_ge(s["chosen"], 1)
            nc.vector.scalar_tensor_tensor(out=probs[:], in0=probs[:], scalar=gate, in1=above[:], op0=ALU.mult,
                                           op1=ALU.mult).then_inc(s["weighted"], 1)


def capped_weights(nc, probs, picked, ranks, capacity):
    with stage(nc, "kept weighted") as (block, s):

        @block.vector
        def _(dve):
            nc.vector.scalar_tensor_tensor(out=ranks[:], in0=ranks[:], scalar=float(capacity), in1=picked[:],
                                           op0=ALU.is_lt, op1=ALU.mult).then_inc(s["kept"], 1)
            dve.wait_ge(s["kept"], 1)
            nc.vector.tensor_tensor(probs[:], probs[:], ranks[:], ALU.mult).then_inc(s["weighted"], 1)


def prepare_window(nc, tables, scales, mask, mask_bf16):
    with stage(nc, "scaled copied") as (block, s):

        @block.gpsimd
        def _(pool):
            nc.gpsimd.tensor_copy(mask_bf16[:], mask[:]).then_inc(s["copied"], 1)

        @block.vector
        def _(dve):
            for i, scale in enumerate(scales):
                nc.vector.tensor_tensor(tables[:, i, :], tables[:, i, :], scale[:], ALU.mult).then_inc(s["scaled"], 1)


def shift_tokens(nc, const, src, dst):
    half = D // 2
    with memory(nc) as (sb, ps):
        bank = ps("shifted", [P, BANK])
        with stage(nc, "copied shifted used") as (block, s):

            @block.gpsimd
            def _(pool):
                nc.gpsimd.tensor_copy(dst[:, :, 0:half], src[:, :, 0:half]).then_inc(s["copied"], 1)

            @block.tensor
            def _(pe):
                with pe.Fori(0, TILES // 8) as it:
                    pe.wait_ge(s["used"], it + 1)
                    nc.tensor.matmul(bank[:], const["previous"][:], src[:, bass.ds(it * 8, 8), half:D], start=True,
                                     stop=True).then_inc(s["shifted"], 1)

            @block.scalar
            def _(act):
                act.sem_inc(s["used"], 1)
                with act.Fori(0, TILES // 8) as it:
                    act.wait_ge(s["shifted"], it + 1)
                    nc.scalar.activation(dst[:, bass.ds(it * 8, 8), half:D],
                                         bank[:].rearrange("p (t d) -> p t d", d=half), ACT.Copy).then_inc(s["used"], 1)


def project_rows(nc, const, *, src_t, weight, bias, resid, out):
    with memory(nc) as (sb, ps):
        tile = sb("tile", [P, 2, P])
        y_ps = ps("y_ps", [P, 2, BANK])
        with stage(nc, "tile_copied y_done y_used") as (block, s):

            @block.gpsimd
            def _(pool):
                pool.sem_inc(s["y_done"], 2)
                with pool.Fori(0, TILES // 2) as it:
                    for u in range(2):
                        pool.wait_ge(s["y_done"], it * 2 + u + 1)
                        nc.gpsimd.tensor_copy(tile[:, u, :], tile_cols(src_t, it * 2 + u)).then_inc(s["tile_copied"], 1)

            @block.tensor
            def _(pe):
                with pe.Fori(0, TILES // 2) as it:
                    for u in range(2):
                        t = it * 2 + u
                        pe.wait_ge(s["tile_copied"], t + 1)
                        pe.wait_ge(s["y_used"], t + 1)
                        nc.tensor.matmul(y_ps[:, u, 0:D], tile[:, u, :], weight, start=True, stop=False)
                        nc.tensor.matmul(y_ps[:, u, 0:D], const["ones"][0:1, :], bias, start=False,
                                         stop=True).then_inc(s["y_done"], 1)

            @block.vector
            def _(dve):
                dve.sem_inc(s["y_used"], 2)
                with dve.Fori(0, TILES // 2) as it:
                    for u in range(2):
                        t = it * 2 + u
                        dve.wait_ge(s["y_done"], t + 3)
                        nc.vector.tensor_tensor(out[:, bass.ds(t, 1), :], y_ps[:, u:u + 1, 0:D],
                                                resid[:, bass.ds(t, 1), :], ALU.add).then_inc(s["y_used"], 1)



def program(nc, w, out, until=8, start=0):
    with memory(nc) as (sb, ps):
        const = dict(ident=sb("ident", [P, P]), ones=sb("ones", [P, P]), ident_bf16=sb("ident_bf16", [P, P], BF16),
                     earlier=sb("earlier", [P, P]), previous=sb("previous", [P, P]), eps=sb("eps", [P, 1]))
        gates = sb("gates", [P, 8])
        head_mask = sb("head_mask", [P, 22])
        x = sb("x", [P, TILES, D])
        z = sb("z", [P, TILES, D])
        spare = sb("spare", [P, 2, TILES * D])
        h = spare[:, 0, :].rearrange("p (t d) -> p t d", d=D)
        xt = sb("xt", [P, TOKENS])
        yt = spare[:, 1, :]
        ctx_t = sb("ctx_t", [CTX, TOKENS])

        def buffers(sb, names):
            bufs = {}
            loads = []
            for name in names.split():
                shape = list(w[name].shape)
                buf = sb("w", shape)
                bufs[name.split(".")[-1]] = buf
                index = tuple(slice(None) for _ in shape)
                loads.append((buf[index], w[name][index]))
            return bufs, loads

        with stage(nc, "loaded eps_set gates_ready") as (block, s):

            @block.sync
            def _(sp):
                sp.dma_start(x[:], w["x"].rearrange("t p d -> p t d")).then_inc(s["loaded"], 16)
                sp.dma_start(gates[:], w["gates"]).then_inc(s["loaded"], 16)
                sp.dma_start(const["ident"][:], w["ident"]).then_inc(s["loaded"], 16)
                sp.dma_start(const["earlier"][:], w["earlier"]).then_inc(s["loaded"], 16)
                sp.dma_start(const["previous"][:], w["previous"]).then_inc(s["loaded"], 16)
                sp.dma_start(ctx_t[:], w["ctx_t"]).then_inc(s["loaded"], 16)
                sp.dma_start(head_mask[:], w["head_masks"]).then_inc(s["loaded"], 16)
                sp.wait_ge(s["loaded"], 112)

            @block.gpsimd
            def _(pool):
                pool.wait_ge(s["loaded"], 112)
                nc.gpsimd.tensor_copy(const["ident_bf16"][:], const["ident"][:])
                nc.gpsimd.memset(const["eps"][:], EPS)
                nc.gpsimd.memset(const["ones"][:], 1.0)

            @block.scalar
            def _(act):
                act.wait_ge(s["loaded"], 112)
                nc.scalar.activation(gates[:], gates[:], ACT.Tanh).then_inc(s["gates_ready"], 1)

        def cross_attention(layer, gate_col, biased):
            with memory(nc) as (sb, ps):
                names = "wq wk wv wo" + (" bq bk bv bo" if biased else "")
                b, loads = buffers(sb, " ".join(f"{layer}.{n}" for n in names.split()))
                layer_norm(nc, const, x, t_outs=[(xt, None, None)], loads=loads)
                attention(nc, const, heads=16, dk=8, kv_rows=CTX, head_mask=head_mask[:, 0:16],
                          q_src=lambda t: tile_cols(xt, t), kv_src=lambda t: tile_cols(ctx_t, t),
                          wq=b["wq"], wk=b["wk"], wv=b["wv"][:], wo=b["wo"], scale=8 ** -0.5,
                          q_bias=b["bq"] if biased else None, k_bias=b["bk"] if biased else None,
                          v_bias=b["bv"][:] if biased else None, o_bias=b["bo"][:] if biased else None,
                          gate=gates[:, gate_col:gate_col + 1], resid=x, out=x)

        def top_experts_layer():
            with memory(nc) as (sb, ps):
                b, loads = buffers(sb, "f0.router f0.score_bias f0.gate_w f0.up_w f0.down_w")
                probs = sb("probs", [P, TILES, 32])
                corrected = sb("corrected", [P, TILES, 32])
                threshold = sb("threshold", [P, TILES])
                total = sb("total", [P, TILES])
                combine = sb("combine", [P, TILES, 34])
                wide = [P, TILES, 32]
                layer_norm(nc, const, x, t_outs=[(xt, None, None)], loads=loads)
                router(nc, const, xt, b["router"][:], None, probs, 32)
                add_all(nc, corrected[:], probs[:], spread(b["score_bias"][:, None, :], wide))
                rank_largest(nc, corrected, threshold, 32, 6)
                pick_first(nc, corrected[:], threshold, 6, corrected, 32)
                combine_weights(nc, probs, corrected, total, combine, 32)
                mix_top_experts(nc, const, src_t=xt, gate_w=b["gate_w"], up_w=b["up_w"], down_w=b["down_w"],
                                combine=combine, resid=x, gate=gates[:, 4:5])

        def transformer_block_layer():
            with memory(nc) as (sb, ps):
                ctx = sb("ctx", [P, TILES, CTX])
                b, loads = buffers(sb, "x1.ln1_g x1.ln1_b x1.ln2_g x1.ln2_b")
                layer_norm(nc, const, x, row_out=h, loads=loads + [(ctx[:], w["ctx"].rearrange("t p d -> p t d"))])
                layer_norm(nc, const, h, row_out=z, row_affine=(b["ln1_g"], b["ln1_b"]))
                for a in ("a1", "a2"):
                    with memory(nc) as (sb2, _):
                        names = "wq wk wv li1_w li1_b lnx_g lnx_b lny_g lny_b ln3_g ln3_b li2_w li2_b li3_w li3_b"
                        v, loads = buffers(sb2, " ".join(f"{a}.{n}" for n in names.split()))
                        keep = sb2("keep", [P, P])
                        loads.append((keep[:], w["keys_kept"]))
                        load_weights(nc, loads)
                        if a == "a1":
                            layer_norm(nc, const, z, t_outs=[(xt, v["lnx_g"][:, 0:1], v["lnx_b"][:, 0:1]),
                                                             (yt, v["lny_g"][:, 0:1], v["lny_b"][:, 0:1])])
                        else:
                            layer_norm(nc, const, z, t_outs=[(xt, v["lnx_g"][:, 0:1], v["lnx_b"][:, 0:1])])
                            layer_norm(nc, const, ctx, width=CTX, t_outs=[(yt, v["lny_g"][:, 0:1], v["lny_b"][:, 0:1])])
                        kv_rows = D if a == "a1" else CTX
                        attention(nc, const, heads=16, dk=32, kv_rows=kv_rows, head_mask=head_mask[:, 16:20],
                                  q_src=lambda t: tile_cols(xt, t),
                                  kv_src=lambda t: yt[0:kv_rows, bass.ds(t * P, P)],
                                  wq=v["wq"], wk=v["wk"], wv=v["wv"][:], wo=v["li1_w"], o_bias=v["li1_b"][:], scale=32 ** -0.5,
                                  keep_mask=keep if a == "a1" else None, resid=z, out=h)
                        layer_norm(nc, const, h, t_outs=[(xt, v["ln3_g"][:, 0:1], v["ln3_b"][:, 0:1])])
                        feed_forward(nc, const, src_t=xt, up=v["li2_w"], up_bias=v["li2_b"], down=v["li3_w"],
                                     down_bias=v["li3_b"][:], rows=P, chunks=4, act_func=ACT.Gelu, resid=h)
                    add_all(nc, z[:], z[:], h[:])
                    if a == "a1":
                        layer_norm(nc, const, z, row_out=z, row_affine=(b["ln2_g"], b["ln2_b"]))
                add_all(nc, x[:], z[:], x[:], gates[:, 1:2])

        def chosen_tokens_layer():
            experts, capacity = 8, TOKENS // 8
            with memory(nc) as (sb, ps):
                b, loads = buffers(sb, "f1.router f1.router_b f1.up_w f1.up_b f1.down_w f1.down_b")
                probs = sb("probs", [P, TILES, experts])
                above = sb("above", [P, TILES, experts])
                equal = sb("equal", [P, TILES, experts])
                ranks = sb("ranks", [P, TILES, experts])
                threshold = sb("threshold", [P, experts])
                missing = sb("missing", [P, experts])
                wide = [P, TILES, experts]
                layer_norm(nc, const, x, t_outs=[(xt, None, None)], loads=loads)
                router(nc, const, xt, b["router"][:], b["router_b"], probs, experts)
                expert_thresholds(nc, const, probs, threshold, missing, equal, above, experts, capacity)
                ranks_over_tokens(nc, const, equal, ranks, experts)
                chosen_weights(nc, probs, above, equal, ranks, missing, gates[:, 5:6], experts)
                mix_chosen_tokens(nc, const, src_t=xt, up_w=b["up_w"], up_b=b["up_b"], down_w=b["down_w"], down_b=b["down_b"],
                                  weights=probs[:].rearrange("p t e -> p (t e)"), resid=x)

        def local_transformer_layer():
            layer_norm(nc, const, x, row_out=z)
            for layer in range(2):
                with memory(nc) as (sb, ps):
                    names = "wqkv q_scale k_scale q_scale_swap k_scale_swap wo ln_g ln_b wa wg ba bg w2 b2"
                    b, loads = buffers(sb, " ".join(f"f2.{layer}.{n}" for n in names.split()))
                    mask = sb("mask", [P, 4 * P])
                    mask_bf16 = sb("mask_bf16", [P, 4 * P], BF16)
                    tables = sb("tables", [P, 4, 64])
                    loads += [(mask[:], w["window_mask"]), (tables[:], w["rotary_tables"])]
                    shift_tokens(nc, const, z, h)
                    layer_norm(nc, const, h, t_outs=[(xt, None, None)], normalize=False, loads=loads)
                    prepare_window(nc, tables, (b["q_scale"], b["q_scale_swap"], b["k_scale"], b["k_scale_swap"]),
                                   mask, mask_bf16)
                    with memory(nc) as (sb2, _):
                        queries = sb2("queries", [P, TILES // 2, 512])
                        keys = spare[:].rearrange("p a (t c) -> p (a t) c", c=512)
                        for half in range(2):
                            tiles = slice(half * (TILES // 2), (half + 1) * (TILES // 2))
                            source = xt[:, half * (TOKENS // 2):(half + 1) * (TOKENS // 2)]
                            rotary_rows(nc, const, heads=8, dk=64, src_t=lambda t: tile_cols(source, t),
                                        wq=b["wqkv"][:, 0:512], wk=b["wqkv"][:, 512:1024],
                                        tables=[tables[:, i, :] for i in range(4)], turned=(queries, keys),
                                        tiles=TILES // 2)
                            attention(nc, const, heads=8, dk=64, kv_rows=D, head_mask=head_mask[:, 20:22],
                                      q_src=None, kv_src=lambda t: tile_cols(source, t), wq=None, wk=None,
                                      wv=b["wqkv"][:, 1024:1536], wo=b["wo"], scale=8.0, add_mask=mask_bf16[:],
                                      ready=(queries, keys), resid=z[:, tiles, :], out=z[:, tiles, :],
                                      tiles=TILES // 2)
                    shift_tokens(nc, const, z, h)
                    layer_norm(nc, const, h, t_outs=[(xt, b["ln_g"][:, 0:1], b["ln_b"][:, 0:1])])
                    feed_forward(nc, const, src_t=xt, up=b["wg"], up_bias=b["bg"], value=b["wa"], value_bias=b["ba"], down=b["w2"],
                                 down_bias=b["b2"][:], rows=114, chunks=3, act_func=ACT.Gelu, resid=z)
            add_all(nc, x[:], z[:], x[:], gates[:, 6:7])

        def capacity_experts_layer():
            experts, capacity = 8, TOKENS // 8
            with memory(nc) as (sb, ps):
                names = "wq wk wv bq bk bv wo bo ln1_g ln1_b ln2_g ln2_b router"
                b, loads = buffers(sb, " ".join(f"f3.{n}" for n in names.split()))
                merged = sb("merged", [P, experts * D])
                merged_b = sb("merged_b", [1, experts * D])
                mask = sb("mask", [P, 4 * P])
                mask_bf16 = sb("mask_bf16", [P, 4 * P], BF16)
                loads.append((mask[:], w["block_mask"]))
                with memory(nc) as (sb2, _):
                    e, e_loads = buffers(sb2, "f3.w1_t f3.w2 f3.b1 f3.b2")
                    layer_norm(nc, const, x, row_out=z, t_outs=[(xt, None, None)], loads=loads + e_loads)
                    merge_linear_experts(nc, const, e["w1_t"], e["w2"], e["b1"], e["b2"], merged, merged_b, experts, 4)
                by_token = xt[:].rearrange("p (l n c) -> p n c l", l=TILES, c=4)
                out_by_token = yt[:].rearrange("p (l n c) -> p n c l", l=TILES, c=4)
                prepare_window(nc, None, (), mask, mask_bf16)
                attention(nc, const, heads=4, dk=32, kv_rows=D, head_mask=head_mask[:, 16:20],
                          q_src=lambda t: by_token[:, bass.ds(t, 1), :, :].rearrange("p n c l -> p (n c) l"),
                          kv_src=lambda t: by_token[:, bass.ds(t, 1), :, :].rearrange("p n c l -> p (n c) l"),
                          wq=b["wq"], wk=b["wk"], wv=b["wv"][:], q_bias=b["bq"], k_bias=b["bk"], v_bias=b["bv"][:],
                          scale=float(1.0 / np.float32(np.sqrt(32))), add_mask=mask_bf16[:],
                          turned_out=lambda t: out_by_token[:, bass.ds(t, 1), :, :].rearrange("p n c l -> p (n c) l"))
                project_rows(nc, const, src_t=yt, weight=b["wo"][:], bias=b["bo"][:], resid=z, out=h)
                layer_norm(nc, const, h, row_out=z, row_affine=(b["ln1_g"], b["ln1_b"]))
                layer_norm(nc, const, z, t_outs=[(xt, None, None)], normalize=False)
                probs = sb("probs", [P, TILES, experts])
                picked = sb("picked", [P, TILES, experts])
                ranks = sb("ranks", [P, TILES, experts])
                most = sb("most", [P, TILES])
                router(nc, const, xt, b["router"][:], None, probs, experts)
                most_probable(nc, probs, most)
                pick_first(nc, probs[:], most, 1, picked, experts)
                ranks_over_tokens(nc, const, picked, ranks, experts)
                capped_weights(nc, probs, picked, ranks, capacity)
                mix_merged_experts(nc, const, src_t=xt, merged=merged, merged_b=merged_b,
                                   weights=probs[:].rearrange("p t e -> p (t e)"), resid=z, experts=experts)
                layer_norm(nc, const, z, row_out=h, row_affine=(b["ln2_g"], b["ln2_b"]))
                add_all(nc, x[:], h[:], x[:], gates[:, 7:8])

        for n in range(start, until):
            if n in (0, 4, 6):
                cross_attention(f"x{n // 2}", n // 2, n != 4)
            elif n == 1:
                top_experts_layer()
            elif n == 2:
                transformer_block_layer()
            elif n == 3:
                chosen_tokens_layer()
            elif n == 5:
                local_transformer_layer()
            else:
                capacity_experts_layer()

        with stage(nc, "stored") as (block, s):

            @block.sync
            def _(sp):
                sp.dma_start(out.rearrange("t p d -> p t d"), x[:]).then_inc(s["stored"], 16)
                sp.wait_ge(s["stored"], 16)


def load_weights(nc, loads):
    with stage(nc, "loaded") as (block, s):

        @block.sync
        def _(sp):
            for dst, source in loads:
                sp.dma_start(dst, source).then_inc(s["loaded"], 16)
            sp.wait_ge(s["loaded"], 16 * len(loads))



def rotary_tables():
    half_idx = np.arange(0, 64, 2, dtype=np.float32)
    inv_freq = (1.0 / 10000.0 ** (half_idx / 64)).astype(np.float32)
    t = np.arange(P, dtype=np.float32)
    freqs = np.concatenate([t[:, None] * inv_freq[None, :]] * 2, axis=-1)
    base = (half_idx + np.float32(0.4 * 64)) / np.float32(1.4 * 64)
    power = (t - P // 2) / np.float32(32)
    scale = np.concatenate([base[None, :] ** power[:, None]] * 2, axis=-1)
    sign = np.concatenate([-np.ones(32), np.ones(32)]).astype(np.float32)
    cos, sin = np.cos(freqs), np.sin(freqs) * sign
    return np.stack([cos * scale, sin * scale, cos / scale, sin / scale], axis=1).astype(np.float32)


def layout(a):
    def rows(v):
        return np.repeat(np.asarray(v)[None, :], P, axis=0)

    def col(v):
        return np.asarray(v)[:, None]

    def on_partitions(m, chunk):
        m = np.asarray(m)
        chunks = -(-m.shape[0] // chunk)
        wide = np.zeros((chunks * chunk,) + m.shape[1:], m.dtype)
        wide[:m.shape[0]] = m
        return np.moveaxis(wide.reshape((chunks, chunk) + m.shape[1:]), 0, 1)

    def padded_cols(m, n):
        m = np.asarray(m)
        wide = np.zeros(m.shape[:-1] + (n,), m.dtype)
        wide[..., :m.shape[-1]] = m
        return wide

    def swapped(v):
        return np.concatenate([v[32:], v[:32]])

    w = {}
    i, j = np.arange(P)[:, None], np.arange(P)[None, :]
    w["ident"] = (i == j).astype(np.float32)
    w["earlier"] = (i < j).astype(np.float32)
    w["previous"] = (i == j - 1).astype(np.float32)
    w["keys_kept"] = (i > j).astype(np.float32)
    w["window_mask"] = np.tile(np.where((j <= i) & (i - j <= 64), 0.0, -1e30).astype(np.float32), (1, 4))
    w["block_mask"] = np.tile(np.where(i // 32 == j // 32, 0.0, -1e30).astype(np.float32), (1, 4))
    w["head_masks"] = np.concatenate([i // dk == np.arange(P // dk)[None, :] for dk in (8, 32, 64)], axis=1).astype(np.float32)
    w["rotary_tables"] = rotary_tables()
    w["x"] = a["x"]
    w["ctx"] = a["ctx_512"]
    w["ctx_t"] = np.asarray(a["ctx_512"]).reshape(TOKENS, CTX).T
    w["gates"] = np.concatenate([rows(a["g_xattn"]), rows(a["g_ffn"])], axis=1)
    for k in (0, 3):
        p = f"L{k}_xattn_"
        w[f"x{k}.wq"] = a[p + "Wq"]
        w[f"x{k}.wk"] = a[p + "Wk"]
        w[f"x{k}.wv"] = a[p + "Wv"]
        w[f"x{k}.wo"] = np.asarray(a[p + "Wo"])[:, None, :]
        w[f"x{k}.bq"] = col(a[p + "bq"])
        w[f"x{k}.bk"] = col(a[p + "bk"])
        w[f"x{k}.bv"] = rows(a[p + "bv"])
        w[f"x{k}.bo"] = np.asarray(a[p + "bo"])[None, :]
    kv = np.asarray(a["L2_xattn_Wkv"])
    w["x2.wq"] = np.asarray(a["L2_xattn_Wq"]).T
    w["x2.wk"] = kv[:D].T
    w["x2.wv"] = kv[D:].T
    w["x2.wo"] = np.asarray(a["L2_xattn_Wo"]).T[:, None, :]

    gate_up = np.asarray(a["L0_ffn_gate_up_proj"])
    w["f0.router"] = np.asarray(a["L0_ffn_router_weight"]).T
    w["f0.score_bias"] = rows(a["L0_ffn_e_score_bias"])
    w["f0.gate_w"] = np.concatenate([gate_up[:, :64].reshape(2048, D), a["L0_ffn_shared_gate_w"]]).T
    w["f0.up_w"] = np.concatenate([gate_up[:, 64:].reshape(2048, D), a["L0_ffn_shared_up_w"]]).T
    down = np.concatenate([np.moveaxis(np.asarray(a["L0_ffn_down_proj"]), 2, 1).reshape(2048, D),
                           np.asarray(a["L0_ffn_shared_down_w"]).T])
    w["f0.down_w"] = on_partitions(down, P)

    for n in ("ln1_g", "ln1_b", "ln2_g", "ln2_b"):
        w[f"x1.{n}"] = rows(a[f"L1_xattn_{n}"])
    for k in ("a1", "a2"):
        p = f"L1_xattn_{k}_"
        for n in ("wq", "wk", "wv"):
            w[f"{k}.{n}"] = np.moveaxis(np.asarray(a[p + n]), 0, 1).reshape(-1, 512)
        w[f"{k}.li1_w"] = on_partitions(a[p + "li1_w"], P)
        w[f"{k}.li1_b"] = np.asarray(a[p + "li1_b"])[None, :]
        for n in ("lnx_g", "lnx_b", "lny_g", "lny_b", "ln3_g", "ln3_b"):
            w[f"{k}.{n}"] = col(a[p + n])
        w[f"{k}.li2_w"] = a[p + "li2_w"]
        w[f"{k}.li2_b"] = np.asarray(a[p + "li2_b"]).reshape(4, P).T
        w[f"{k}.li3_w"] = on_partitions(a[p + "li3_w"], P)
        w[f"{k}.li3_b"] = np.asarray(a[p + "li3_b"])[None, :]

    w["f1.router"] = a["L1_ffn_Wr"]
    w["f1.router_b"] = rows(a["L1_ffn_br"])
    w["f1.up_w"] = np.moveaxis(padded_cols(a["L1_ffn_W_up"], 342), 0, 1).reshape(D, 4 * 342)
    w["f1.up_b"] = padded_cols(a["L1_ffn_b_up"], 342).reshape(12, 114).T
    w["f1.down_w"] = on_partitions(np.moveaxis(np.asarray(a["L1_ffn_W_down"]), 0, 1).reshape(341, 8 * D), 114)
    w["f1.down_b"] = np.asarray(a["L1_ffn_b_down"]).reshape(1, 8 * D)

    for k in range(2):
        q, p = f"f2.{k}.", "L2_ffn_"
        w[q + "wqkv"] = np.asarray(a[p + "wqkv"])[k]
        for n in ("q_scale", "k_scale"):
            w[q + n] = rows(np.asarray(a[p + n])[k])
            w[q + n + "_swap"] = rows(swapped(np.asarray(a[p + n])[k]))
        w[q + "wo"] = on_partitions(np.asarray(a[p + "wo"])[k], P)
        w[q + "ln_g"] = col(np.asarray(a[p + "ln_g"])[k])
        w[q + "ln_b"] = col(np.asarray(a[p + "ln_b"])[k])
        w1, b1 = np.asarray(a[p + "w1"])[k], np.asarray(a[p + "b1"])[k]
        w[q + "wa"] = padded_cols(w1[:, :341], 342)
        w[q + "wg"] = padded_cols(w1[:, 341:], 342)
        w[q + "ba"] = padded_cols(b1[:341], 342).reshape(3, 114).T
        w[q + "bg"] = padded_cols(b1[341:], 342).reshape(3, 114).T
        w[q + "w2"] = on_partitions(np.asarray(a[p + "w2"])[k], 114)
        w[q + "b2"] = np.asarray(a[p + "b2"])[k][None, :]

    proj, proj_b = np.asarray(a["L3_ffn_in_proj_w"]), np.asarray(a["L3_ffn_in_proj_b"])
    for k, n in enumerate("qkv"):
        w[f"f3.w{n}"] = proj[k * D:(k + 1) * D].T
    w["f3.bq"], w["f3.bk"] = col(proj_b[:D]), col(proj_b[D:2 * D])
    w["f3.bv"] = rows(proj_b[2 * D:])
    w["f3.wo"] = np.asarray(a["L3_ffn_out_proj_w"]).T
    w["f3.bo"] = np.asarray(a["L3_ffn_out_proj_b"])[None, :]
    for n in ("ln1_g", "ln1_b", "ln2_g", "ln2_b"):
        w[f"f3.{n}"] = rows(a[f"L3_ffn_{n}"])
    w["f3.router"] = a["L3_ffn_wg"]
    w["f3.w1_t"] = np.transpose(np.asarray(a["L3_ffn_w1"]).reshape(8, D, 4, P), (3, 2, 0, 1))
    w["f3.w2"] = np.transpose(np.asarray(a["L3_ffn_w2"]).reshape(8, 4, P, D), (2, 1, 0, 3))
    w["f3.b1"] = np.transpose(np.asarray(a["L3_ffn_b1"]).reshape(8, 4, P), (2, 1, 0))
    w["f3.b2"] = np.asarray(a["L3_ffn_b2"]).reshape(1, 8 * D)
    return {name: np.ascontiguousarray(v) for name, v in w.items()}


def kernel(**inputs):
    from concourse import bacc
    from concourse.bass_utils import run_bass_kernel_spmd

    nc = bacc.Bacc("TRN2", target_bir_lowering=False, num_devices=1)
    laid_out = layout(inputs)
    arrays = {"in_" + name.replace(".", "_"): v for name, v in laid_out.items()}
    tensors = {name: nc.dram_tensor("in_" + name.replace(".", "_"), v.shape, F32, kind="ExternalInput").ap()
               for name, v in laid_out.items()}
    out = nc.dram_tensor("out", (TILES, P, D), F32, kind="ExternalOutput").ap()
    program(nc, tensors, out)
    result = run_bass_kernel_spmd(nc, [arrays], core_ids=[0])
    return np.asarray(result.results[0]["out"])
```

```python
from contextlib import ExitStack, contextmanager

import numpy as np

import concourse.bass as bass
from concourse import mybir

ALU = mybir.AluOpType
ACT = mybir.ActivationFunctionType
AX = mybir.AxisListType
F32 = mybir.dt.float32
I32 = mybir.dt.int32
BF16 = mybir.dt.bfloat16

P = 128
TILES = 32
D = 128
CTX = 64
TOKENS = TILES * P
BANK = 512
EPS = 1e-5


@contextmanager
def stage(nc, names):
    semaphores = {name: nc.alloc_semaphore(nc.get_next_instruction_name() + name) for name in names.split()}
    with nc.Block() as block:
        yield block, semaphores
    nc.clear_and_free_semaphores(list(semaphores.values()))
    nc.all_engine_barrier()


@contextmanager
def memory(nc):
    with ExitStack() as held:
        def sb(name, shape, dtype=F32):
            return held.enter_context(nc.sbuf_tensor(nc.get_next_instruction_name() + name, shape, dtype))

        def ps(name, shape):
            return held.enter_context(nc.psum_tensor(nc.get_next_instruction_name() + name, shape, F32))

        yield sb, ps


def tile_cols(tensor, t, n=1):
    return tensor[:, bass.ds(t * P, n * P)]


def spread(ap, shape):
    return ap.to_broadcast(shape)



def layer_norm(nc, const, src, width=D, t_outs=(), row_out=None, row_affine=None, loads=(), normalize=True,
               has_stats=False, shifted=False):
    second = len(t_outs) > 1
    turned_out = bool(t_outs)
    direct = row_out is not None and row_affine is None and not turned_out
    buffered_rows = row_out is not None and not direct
    shared = normalize and (second or not turned_out)
    with memory(nc) as (sb, ps):
        stats = const["row_stats"]
        work = sb("work", [P, 4, TILES])
        std = sb("std", [P, TILES])
        mean = sb("mean", [P, TILES])
        rstd = sb("rstd", [P, TILES])
        minus_mean = sb("minus_mean", [P, TILES])
        xn = sb("xn", [P, 8, D])
        scaled = sb("scaled", [P, 8, width])
        bank = ps("turned", [P, 2, BANK])
        with stage(nc, "loaded stats_done chain std_ready first_half_ready second_half_ready turned "
                       "first_copied second_copied row_scaled row_done padded zeros_set") as (block, s):

            def wait_for_rows(engine, it, half):
                if shared:
                    engine.wait_ge(s["second_half_ready"] if half else s["first_half_ready"], it * 4 + 4)
                else:
                    engine.wait_ge(s["first_half_ready"], (it * 2 + half) * 4 + 4)

            def wait_for_buffer(engine, it, half):
                if turned_out:
                    engine.wait_ge(s["turned"], it * 2 + half + 1)
                if buffered_rows:
                    engine.wait_ge(s["row_scaled"] if row_affine else s["row_done"], it * 2 + half + 1)

            def target(it, u):
                if direct:
                    return row_out[:, bass.ds(it * 8 + u, 1), :]
                return xn[:, u:u + 1, 0:width]

            @block.sync
            def _(sp):
                for dst, source in loads:
                    sp.dma_start(dst, source).then_inc(s["loaded"], 16)
                if loads:
                    sp.wait_ge(s["loaded"], 16 * len(loads))

            @block.vector
            def _(dve):
                if normalize:
                    if not has_stats:
                        with dve.Fori(0, TILES // 8) as it:
                            for u in range(8):
                                nc.vector.bn_stats(stats[:, bass.ds(it * 8 + u, 1), :],
                                                   src[:, bass.ds(it * 8 + u, 1), :]).then_inc(s["stats_done"], 1)
                        dve.wait_ge(s["stats_done"], TILES)
                    nc.vector.tensor_tensor(work[:, 0, :], stats[:, :, 1], stats[:, :, 4], ALU.add).then_inc(s["chain"], 1)
                    nc.vector.tensor_tensor(work[:, 1, :], stats[:, :, 1], stats[:, :, 4],
                                            ALU.subtract).then_inc(s["chain"], 1)
                    nc.vector.tensor_tensor(work[:, 2, :], stats[:, :, 2], stats[:, :, 5], ALU.add).then_inc(s["chain"], 1)
                    dve.wait_ge(s["chain"], 3)
                    nc.vector.tensor_scalar(mean[:], work[:, 0, :], 0.5, None, ALU.mult).then_inc(s["chain"], 1)
                    nc.vector.tensor_tensor(work[:, 3, :], work[:, 1, :], work[:, 1, :], ALU.mult).then_inc(s["chain"], 1)
                    dve.wait_ge(s["chain"], 5)
                    nc.vector.scalar_tensor_tensor(out=work[:, 0, :], in0=work[:, 3, :], scalar=width / 4.0,
                                                   in1=work[:, 2, :], op0=ALU.mult, op1=ALU.add).then_inc(s["chain"], 1)
                    dve.wait_ge(s["std_ready"], 1)
                    nc.vector.reciprocal(rstd[:], std[:]).then_inc(s["chain"], 1)
                    dve.wait_ge(s["chain"], 7)
                    nc.vector.scalar_tensor_tensor(out=minus_mean[:], in0=mean[:], scalar=-1.0, in1=rstd[:],
                                                   op0=ALU.mult, op1=ALU.mult).then_inc(s["chain"], 1)
                if width < D:
                    dve.wait_ge(s["padded"], 1)
                with dve.Fori(0, TILES // 8) as it:
                    for half in range(1 if shared else 2):
                        wait_for_buffer(dve, it, half)
                        for u in range(half * 4, half * 4 + 4):
                            t = it * 8 + u
                            if normalize:
                                ins = nc.vector.tensor_scalar(target(it, u), src[:, bass.ds(t, 1), :],
                                                              mean[:, bass.ds(t, 1)], rstd[:, bass.ds(t, 1)],
                                                              ALU.subtract, ALU.mult)
                            else:
                                ins = nc.vector.tensor_copy(target(it, u), src[:, bass.ds(t, 1), :])
                            ins.then_inc(s["first_half_ready"], 1)
                    if row_affine is not None:
                        for half in range(2):
                            bank_no = it * 2 + half
                            dve.wait_ge(s["row_scaled"], bank_no + 3)
                            nc.vector.tensor_tensor(row_out[:, bass.ds(bank_no * 4, 4), :],
                                                    scaled[:, half * 4:half * 4 + 4, :],
                                                    spread(row_affine[1][:, None, :], [P, 4, width]),
                                                    ALU.add).then_inc(s["row_done"], 1)
                    if second:
                        for half in range(2):
                            bank_no = it * 2 + half
                            dst, gain, shift = t_outs[1]
                            dve.wait_ge(s["first_copied"], bank_no + 3)
                            nc.vector.tensor_scalar(dst[0:width, bass.ds(bank_no * BANK, BANK)],
                                                    bank[0:width, half, :], gain, shift,
                                                    ALU.mult, ALU.add).then_inc(s["second_copied"], 1)

            @block.tensor
            def _(pe):
                if not turned_out:
                    return
                pe.sem_inc(s["turned"], 2)
                with pe.Fori(0, TILES // 8) as it:
                    for half in range(2):
                        bank_no = it * 2 + half
                        pe.wait_ge(s["first_copied"], bank_no + 1)
                        if second:
                            pe.wait_ge(s["second_copied"], bank_no + 1)
                        wait_for_rows(pe, it, half)
                        for k in range(4):
                            last = nc.tensor.transpose(bank[:, half, k * P:(k + 1) * P],
                                                       xn[:, half * 4 + k, :], const["ident"][:])
                        last.then_inc(s["turned"], 1)

            @block.scalar
            def _(act):
                act.sem_inc(s["first_copied"], 2)
                act.sem_inc(s["second_copied"], 2)
                if normalize:
                    act.wait_ge(s["chain"], 6)
                    nc.scalar.activation(std[:], work[:, 0, :], ACT.Sqrt, bias=const["eps"][:, 0:1],
                                         scale=1.0 / width).then_inc(s["std_ready"], 1)
                    act.wait_ge(s["chain"], 8)
                if width < D:
                    act.wait_ge(s["padded"], 1)
                with act.Fori(0, TILES // 8) as it:
                    if shared:
                        wait_for_buffer(act, it, 1)
                        for u in range(4, 8):
                            t = it * 8 + u
                            nc.scalar.activation(target(it, u), src[:, bass.ds(t, 1), :], ACT.Identity,
                                                 bias=minus_mean[:, bass.ds(t, 1)], scale=rstd[:, bass.ds(t, 1)]
                                                 ).then_inc(s["second_half_ready"], 1)
                    if turned_out:
                        dst, gain, shift = t_outs[0]
                        for half in range(2):
                            bank_no = it * 2 + half
                            act.wait_ge(s["turned"], bank_no + 3)
                            out = dst[0:width, bass.ds(bank_no * BANK, BANK)]
                            if shifted:
                                upper = width // 2
                                act.wait_ge(s["zeros_set"], 1)
                                nc.scalar.activation(out[0:upper, :], bank[0:upper, half, :], ACT.Copy)
                                ins = nc.scalar.activation(
                                    out[upper:width, :].rearrange("p (k n) -> p k n", n=P)[:, :, 1:P],
                                    bank[upper:width, half, :].rearrange("p (k n) -> p k n", n=P)[:, :, 0:P - 1], ACT.Copy)
                            elif gain is None:
                                ins = nc.scalar.activation(out, bank[0:width, half, :], ACT.Copy)
                            else:
                                ins = nc.scalar.activation(out, bank[0:width, half, :], ACT.Identity,
                                                           bias=shift, scale=gain)
                            ins.then_inc(s["first_copied"], 1)

            @block.gpsimd
            def _(pool):
                if width < D:
                    nc.gpsimd.memset(xn[:], 0.0).then_inc(s["padded"], 1)
                if shifted:
                    first_tokens = t_outs[0][0][width // 2:width, :].rearrange("p (t n) -> p t n", n=P)[:, :, 0:1]
                    nc.gpsimd.memset(first_tokens, 0.0).then_inc(s["zeros_set"], 1)
                if not buffered_rows:
                    return
                pool.sem_inc(s["row_done"], 2)
                pool.sem_inc(s["row_scaled"], 2)
                with pool.Fori(0, TILES // 8) as it:
                    for half in range(2):
                        bank_no = it * 2 + half
                        wait_for_rows(pool, it, half)
                        xs = xn[:, half * 4:half * 4 + 4, 0:width]
                        if row_affine is None:
                            nc.gpsimd.tensor_copy(row_out[:, bass.ds(bank_no * 4, 4), :], xs).then_inc(s["row_done"], 1)
                        else:
                            pool.wait_ge(s["row_done"], bank_no + 1)
                            nc.gpsimd.tensor_tensor(scaled[:, half * 4:half * 4 + 4, :], xs,
                                                    spread(row_affine[0][:, None, :], [P, 4, width]),
                                                    ALU.mult).then_inc(s["row_scaled"], 1)



def attention(nc, const, *, heads, dk, kv_rows, q_src, kv_src, wq, wk, wv, scale, head_mask,
              q_bias=None, k_bias=None, v_bias=None, add_mask=None, keep_mask=None, ready=None,
              wo=None, o_bias=None, gate=None, resid=None, out=None, turned_out=None, tiles=TILES,
              keep_stats=False):
    steps = heads // 4
    inner = heads * dk
    groups = inner // P
    per_group = heads // groups
    v_cols = dk if keep_mask is not None else dk + 1
    per_bank = heads // 2
    with memory(nc) as (sb, ps):
        qt = sb("qt", [P, 2, inner])
        kt = sb("kt", [P, 2, inner]) if ready is None else None
        masked_k = sb("masked_k", [P, 2, heads, P])
        kv_tile = sb("kv_tile", [kv_rows, 2, P])
        v = sb("v", [P, 2, heads, dk + 1])
        probs = sb("probs", [P, 2, BANK])
        probs_t = sb("probs_t", [P, 2, BANK])
        maxes = sb("maxes", [P, 2, 4])
        sums = sb("sums", [P, 2, heads])
        inv = sb("inv", [P, heads])
        o = sb("o", [P, inner])
        ot = sb("ot", [P, inner])
        with_bias = sb("with_bias", [P, 2, D])
        bias_rows = sb("bias_rows", [P, D])
        p0 = ps("p0", [P, BANK])
        p1 = ps("p1", [P, BANK])
        sc = ps("sc", [P, 2, BANK])
        tp = ps("tp", [P, 2, BANK])
        ov = ps("ov", [P, 2, BANK])
        ov_heads = ov[:, :, 0:per_bank * v_cols].rearrange("p a (h c) -> p a h c", c=v_cols)

        def v_out(h):
            return ov[:, h // per_bank, (h % per_bank) * v_cols:(h % per_bank + 1) * v_cols]

        def slot(u, j):
            return (u * steps + j) % 2

        with stage(nc, "const_ready kv_copied v_done q_done k_done q_copied k_copied "
                       "v_copied keys_masked scores_ready max_ready scores_used probs_ready probs_turned "
                       "probs_t_ready weighed inv_ready o_ready o_turned ot_copied y_done y_used biased scaled stats_done"
                   ) as (block, s):

            @block.tensor
            def _(pe):
                def project_queries(t, first=False):
                    if ready is not None:
                        return
                    if steps == 1 and not first:
                        pe.wait_ge(s["q_copied"], t)
                    pe.wait_ge(s["ot_copied"], t + 1)
                    for g in range(groups):
                        last = nc.tensor.matmul(p1[:, g * P:(g + 1) * P], wq[:, g * P:(g + 1) * P], q_src(t),
                                                start=True, stop=True)
                    last.then_inc(s["q_done"], 1)

                def project_keys(t, first=False, second=False):
                    if ready is not None:
                        return
                    if wo is not None:
                        pe.wait_ge(s["y_used"], t + 1)
                    elif second:
                        pe.wait_ge(s["k_copied"], 1)
                    elif not first:
                        pe.wait_ge(s["v_copied"], t - 1)
                    for g in range(groups):
                        last = nc.tensor.matmul(p0[:, g * P:(g + 1) * P], wk[:, g * P:(g + 1) * P], kv_src(t),
                                                start=True, stop=True)
                    last.then_inc(s["k_done"], 1)

                def project_values(t, u, last_tile=False):
                    pe.wait_ge(s["kv_copied"], t + 1)
                    if steps == 1:
                        if last_tile:
                            pe.wait_ge(s["v_copied"], t)
                        else:
                            pe.wait_ge(s["k_copied"], t + 2)
                    elif ready is None:
                        pe.wait_ge(s["k_copied"], t + 1)
                    else:
                        pe.wait_ge(s["y_used"], t + 1)
                    nc.tensor.matmul(p0[:, 0:inner], kv_tile[:, u, :], wv, start=True, stop=True
                                     ).then_inc(s["v_done"], 1)

                def scores(t, u, j):
                    n = t * steps + j
                    if j == 0:
                        pe.wait_ge(s["q_copied"], t + 1)
                    pe.wait_ge(s["keys_masked"], n + 1)
                    pe.wait_ge(s["scores_used"], n + 1)
                    bank = sc[:, slot(u, j), :]
                    if add_mask is not None:
                        nc.tensor.matmul(bank, const["ident_bf16"][:], add_mask, start=True, stop=False,
                                         skip_group_check=True)
                    h = 4 * j
                    while h < 4 * j + 4:
                        g, n_heads = h // per_group, min(4, per_group)
                        cols = slice((h - 4 * j) * P, (h - 4 * j + n_heads) * P)
                        last = nc.tensor.matmul(bank[:, cols], qt[:, u, g * P:(g + 1) * P],
                                                masked_k[:, u, h:h + n_heads, :].rearrange("p h k -> p (h k)"),
                                                start=add_mask is None, stop=True,
                                                skip_group_check=add_mask is not None)
                        h += n_heads
                    last.then_inc(s["scores_ready"], 1)

                def turn_probs(t, u, j):
                    n = t * steps + j
                    pe.wait_ge(s["probs_ready"], n + 1)
                    pe.wait_ge(s["probs_t_ready"], n + 1)
                    for i in range(4):
                        last = nc.tensor.transpose(tp[:, slot(u, j), i * P:(i + 1) * P],
                                                   probs[:, slot(u, j), i * P:(i + 1) * P], const["ident"][:])
                    last.then_inc(s["probs_turned"], 1)

                def weigh(t, u, j):
                    n = t * steps + j
                    pe.wait_ge(s["probs_t_ready"], n + 3)
                    if j == 0:
                        pe.wait_ge(s["v_copied"], t + 1)
                        pe.wait_ge(s["o_ready"], t + 1)
                    for i in range(4):
                        h = 4 * j + i
                        last = nc.tensor.matmul(v_out(h), probs_t[:, slot(u, j), i * P:(i + 1) * P],
                                                v[:, u, h, 0:v_cols], start=True, stop=True)
                    last.then_inc(s["weighed"], 1)

                def turn_outputs(t, following=False, last_tile=False):
                    pe.wait_ge(s["o_ready"], t + 2)
                    if ready is None:
                        if steps == 1 and following:
                            pe.wait_ge(s["q_copied"], t + 4)
                        elif steps == 1:
                            pe.wait_ge(s["ot_copied"], t + 4)
                        elif not last_tile:
                            pe.wait_ge(s["q_copied"], t + 2)
                    for c in range(groups):
                        last = nc.tensor.transpose(p1[:, c * P:(c + 1) * P], o[:, c * P:(c + 1) * P],
                                                   const["ident"][:])
                    last.then_inc(s["o_turned"], 1)

                def project_outputs(t, following=False):
                    if wo is None:
                        return
                    pe.wait_ge(s["ot_copied"], t + 3)
                    if following:
                        pe.wait_ge(s["v_copied"], t + 3)
                    for c in range(groups):
                        last = nc.tensor.matmul(p0[:, 0:D], ot[:, c * P:(c + 1) * P], wo[:, c, :], start=c == 0,
                                                stop=c == groups - 1)
                    last.then_inc(s["y_done"], 1)

                def pair(it, first, end):
                    for u in range(2):
                        t = it * 2 + u
                        earlier = not (first and u == 0)
                        following = not (end and u == 1)
                        if steps == 4:
                            scores(t, u, 1)
                            turn_probs(t, u, 0)
                            if earlier:
                                weigh(t - 1, 1 - u, 3)
                            scores(t, u, 2)
                            if following:
                                project_keys(t + 1)
                            turn_probs(t, u, 1)
                            weigh(t, u, 0)
                            if earlier:
                                turn_outputs(t - 1, following)
                            scores(t, u, 3)
                            if following:
                                project_values(t + 1, 1 - u)
                            turn_probs(t, u, 2)
                            if following:
                                project_queries(t + 1)
                            weigh(t, u, 1)
                            if earlier:
                                project_outputs(t - 1, following)
                            if following:
                                scores(t + 1, 1 - u, 0)
                            turn_probs(t, u, 3)
                            weigh(t, u, 2)
                        elif steps == 2:
                            scores(t, u, 1)
                            turn_probs(t, u, 0)
                            if earlier:
                                weigh(t - 1, 1 - u, 1)
                            if following:
                                project_values(t + 1, 1 - u)
                                scores(t + 1, 1 - u, 0)
                            if earlier:
                                turn_outputs(t - 1, following)
                            turn_probs(t, u, 1)
                            weigh(t, u, 0)
                            if earlier:
                                project_outputs(t - 1, following)
                        else:
                            if following:
                                scores(t + 1, 1 - u, 0)
                            turn_probs(t, u, 0)
                            if not end:
                                project_queries(t + 2)
                                project_keys(t + 2)
                            if earlier:
                                weigh(t - 1, 1 - u, 0)
                            if following:
                                project_values(t + 1, 1 - u, end)
                            if earlier:
                                turn_outputs(t - 1, not end)

                project_queries(0, True)
                project_keys(0, True)
                if steps == 1:
                    project_queries(1)
                    project_keys(1, second=True)
                project_values(0, 0)
                scores(0, 0, 0)
                pair(0, True, False)
                with pe.Fori(1, tiles // 2 - 1) as it:
                    pair(it, False, False)
                pair(tiles // 2 - 1, False, True)
                weigh(tiles - 1, 1, steps - 1)
                turn_outputs(tiles - 1, last_tile=True)
                project_outputs(tiles - 1)

            @block.vector
            def _(dve):
                def subtract_max(t, u, j):
                    n = t * steps + j
                    dve.wait_ge(s["scores_ready"], n + 1)
                    scores = sc[:, slot(u, j), :].rearrange("p (g k) -> p g k", k=P)
                    most = maxes[:, slot(u, j), :]
                    nc.vector.tensor_reduce(most, scores, AX.X, ALU.max).then_inc(s["max_ready"], 1)
                    dve.wait_ge(s["probs_turned"], n + 1)
                    dve.wait_ge(s["max_ready"], n + 1)
                    nc.vector.tensor_tensor(probs[:, slot(u, j), :].rearrange("p (g k) -> p g k", k=P), scores,
                                            spread(most[:, :, None], [P, 4, P]),
                                            ALU.subtract).then_inc(s["scores_used"], 1)

                def mask_probs(t, u, j):
                    if keep_mask is None:
                        return
                    dve.wait_ge(s["probs_turned"], t * steps + j + 3)
                    nc.vector.tensor_tensor(probs_t[:, slot(u, j), :].rearrange("p (g k) -> p g k", k=P),
                                            tp[:, slot(u, j), :].rearrange("p (g k) -> p g k", k=P),
                                            spread(keep_mask[:, None, :], [P, 4, P]),
                                            ALU.mult).then_inc(s["probs_t_ready"], 1)

                def normalise(t, u):
                    dve.wait_ge(s["weighed"], (t + 1) * steps)
                    inv_heads = inv[:].rearrange("p (a h) -> p a h", a=2)
                    if keep_mask is None:
                        nc.vector.reciprocal(inv_heads[:, :, :, None], ov_heads[:, :, :, dk:dk + 1]
                                             ).then_inc(s["inv_ready"], 1)
                    else:
                        dve.wait_ge(s["probs_ready"], (t + 1) * steps)
                        nc.vector.reciprocal(inv[:], sums[:, u, :]).then_inc(s["inv_ready"], 1)
                    dve.wait_ge(s["inv_ready"], t + 3)
                    dve.wait_ge(s["o_turned"], t + 1)
                    nc.vector.tensor_tensor(o[:].rearrange("p (a h c) -> p a h c", a=2, c=dk), ov_heads[:, :, :, 0:dk],
                                            spread(inv_heads[:, :, :, None], [P, 2, per_bank, dk]),
                                            ALU.mult).then_inc(s["o_ready"], 1)

                def add_residual(t, u):
                    if wo is None:
                        return
                    dve.wait_ge(s["y_done"], t + 1)
                    if o_bias is None:
                        rows = resid[:, bass.ds(t, 1), :]
                    else:
                        dve.wait_ge(s["biased"], t + 1)
                        rows = with_bias[:, u:u + 1, :]
                    if gate is None:
                        ins = nc.vector.tensor_tensor(out[:, bass.ds(t, 1), :], p0[:, None, 0:D], rows, ALU.add)
                    else:
                        ins = nc.vector.scalar_tensor_tensor(out=out[:, bass.ds(t, 1), :], in0=p0[:, None, 0:D],
                                                             scalar=gate, in1=rows, op0=ALU.mult, op1=ALU.add)
                    ins.then_inc(s["y_used"], 1)

                def row_stats(t):
                    if not keep_stats:
                        return
                    dve.wait_ge(s["y_used"], t + 4)
                    nc.vector.bn_stats(const["row_stats"][:, bass.ds(t, 1), :], out[:, bass.ds(t, 1), :]
                                       ).then_inc(s["stats_done"], 1)

                def copy_queries(t, u):
                    if ready is not None:
                        return
                    dve.wait_ge(s["q_done"], t + 1)
                    if q_bias is None:
                        ins = nc.vector.tensor_copy(qt[:, u, :], p1[:, 0:inner])
                    else:
                        ins = nc.vector.tensor_scalar(qt[:, u, :], p1[:, 0:inner], q_bias[:, 0:1], None, ALU.add)
                    ins.then_inc(s["q_copied"], 1)

                def add_value_bias(t, u):
                    if v_bias is None:
                        return
                    dve.wait_ge(s["v_done"], t + 1)
                    nc.vector.tensor_tensor(v[:, u, :, 0:dk], p0[:, 0:inner].rearrange("p (h c) -> p h c", c=dk),
                                            v_bias.rearrange("p (h c) -> p h c", c=dk),
                                            ALU.add).then_inc(s["v_copied"], 1)

                def pair(it, first, end):
                    for u in range(2):
                        t = it * 2 + u
                        earlier = not (first and u == 0)
                        following = not (end and u == 1)
                        if steps == 4:
                            subtract_max(t, u, 1)
                            mask_probs(t, u, 0)
                            if earlier:
                                normalise(t - 1, 1 - u)
                            subtract_max(t, u, 2)
                            mask_probs(t, u, 1)
                            subtract_max(t, u, 3)
                            if following:
                                add_value_bias(t + 1, 1 - u)
                                copy_queries(t + 1, 1 - u)
                            mask_probs(t, u, 2)
                            if following:
                                subtract_max(t + 1, 1 - u, 0)
                            if earlier:
                                add_residual(t - 1, 1 - u)
                            mask_probs(t, u, 3)
                            if earlier:
                                row_stats(t - 1)
                        elif steps == 2:
                            subtract_max(t, u, 1)
                            if earlier:
                                normalise(t - 1, 1 - u)
                            if following:
                                add_value_bias(t + 1, 1 - u)
                                subtract_max(t + 1, 1 - u, 0)
                            if earlier:
                                add_residual(t - 1, 1 - u)
                        else:
                            if following:
                                subtract_max(t + 1, 1 - u, 0)
                            if not end:
                                copy_queries(t + 2, u)
                            if earlier:
                                normalise(t - 1, 1 - u)
                            if following:
                                add_value_bias(t + 1, 1 - u)

                dve.sem_inc(s["y_used"], 3)
                dve.sem_inc(s["scores_used"], 2)
                dve.sem_inc(s["o_ready"], 1)
                dve.sem_inc(s["inv_ready"], 2)
                dve.wait_ge(s["const_ready"], 1)
                copy_queries(0, 0)
                if steps == 1:
                    copy_queries(1, 1)
                add_value_bias(0, 0)
                subtract_max(0, 0, 0)
                pair(0, True, False)
                with dve.Fori(1, tiles // 2 - 1) as it:
                    pair(it, False, False)
                pair(tiles // 2 - 1, False, True)
                normalise(tiles - 1, 1)
                add_residual(tiles - 1, 1)
                row_stats(tiles - 1)

            @block.scalar
            def _(act):
                def exponentials(t, u, j):
                    act.wait_ge(s["scores_used"], t * steps + j + 3)
                    if keep_mask is None:
                        half = probs[:, slot(u, j), :]
                        nc.scalar.activation(half, half, ACT.Exp, scale=scale).then_inc(s["probs_ready"], 1)
                        return
                    if j == 0:
                        act.wait_ge(s["inv_ready"], t + 1)
                    for i in range(4):
                        head = probs[:, slot(u, j), i * P:(i + 1) * P]
                        last = nc.scalar.activation(head, head, ACT.Exp, scale=scale,
                                                    accum_out=sums[:, u, 4 * j + i:4 * j + i + 1])
                    last.then_inc(s["probs_ready"], 1)

                def copy_probs(t, u, j):
                    if keep_mask is not None:
                        return
                    act.wait_ge(s["probs_turned"], t * steps + j + 3)
                    nc.scalar.activation(probs_t[:, slot(u, j), :], tp[:, slot(u, j), :],
                                         ACT.Copy).then_inc(s["probs_t_ready"], 1)

                def copy_turned(t):
                    act.wait_ge(s["o_turned"], t + 2)
                    if wo is None:
                        ins = nc.scalar.activation(turned_out(t), p1[:, 0:inner].rearrange("p (c l) -> p c l", c=4),
                                                   ACT.Copy)
                    else:
                        ins = nc.scalar.activation(ot[:], p1[:, 0:inner], ACT.Copy)
                    ins.then_inc(s["ot_copied"], 1)

                def copy_keys(t, u):
                    if ready is not None:
                        nc.scalar.activation(qt[:, u:u + 1, :], ready[0][:, bass.ds(t, 1), :],
                                             ACT.Copy).then_inc(s["q_copied"], 1)
                        return
                    act.wait_ge(s["k_done"], t + 1)
                    if k_bias is None:
                        ins = nc.scalar.activation(kt[:, u, :], p0[:, 0:inner], ACT.Copy)
                    else:
                        ins = nc.scalar.activation(kt[:, u, :], p0[:, 0:inner], ACT.Identity, bias=k_bias[:, 0:1])
                    ins.then_inc(s["k_copied"], 1)

                def copy_values(t, u):
                    if v_bias is not None:
                        return
                    act.wait_ge(s["v_done"], t + 1)
                    nc.scalar.activation(v[:, u, :, 0:dk], p0[:, 0:inner].rearrange("p (h c) -> p h c", c=dk),
                                         ACT.Copy).then_inc(s["v_copied"], 1)

                def pair(it, first, end):
                    for u in range(2):
                        t = it * 2 + u
                        earlier = not (first and u == 0)
                        following = not (end and u == 1)
                        if steps == 4:
                            exponentials(t, u, 1)
                            copy_probs(t, u, 0)
                            exponentials(t, u, 2)
                            if following:
                                copy_keys(t + 1, 1 - u)
                            copy_probs(t, u, 1)
                            if earlier:
                                copy_turned(t - 1)
                            exponentials(t, u, 3)
                            if following:
                                copy_values(t + 1, 1 - u)
                            copy_probs(t, u, 2)
                            if following:
                                exponentials(t + 1, 1 - u, 0)
                            copy_probs(t, u, 3)
                        elif steps == 2:
                            if following:
                                copy_keys(t + 1, 1 - u)
                            exponentials(t, u, 1)
                            copy_probs(t, u, 0)
                            if following:
                                copy_values(t + 1, 1 - u)
                            if earlier:
                                copy_turned(t - 1)
                            if following:
                                exponentials(t + 1, 1 - u, 0)
                            copy_probs(t, u, 1)
                        else:
                            copy_probs(t, u, 0)
                            if not end:
                                copy_keys(t + 2, u)
                            if following:
                                copy_values(t + 1, 1 - u)
                                exponentials(t + 1, 1 - u, 0)
                            if earlier:
                                copy_turned(t - 1)

                act.sem_inc(s["ot_copied"], 4 if steps == 1 else 2)
                act.sem_inc(s["probs_t_ready"], 2)
                act.wait_ge(s["const_ready"], 1)
                copy_keys(0, 0)
                if steps == 1:
                    copy_keys(1, 1)
                copy_values(0, 0)
                exponentials(0, 0, 0)
                pair(0, True, False)
                with act.Fori(1, tiles // 2 - 1) as it:
                    pair(it, False, False)
                pair(tiles // 2 - 1, False, True)
                copy_turned(tiles - 1)

            @block.gpsimd
            def _(pool):
                def copy_kv(t, u, first=False):
                    if not first:
                        pool.wait_ge(s["v_done"], t - 1)
                    view = kv_tile[:, u, :]
                    source = kv_src(t)
                    if len(source.shape) == 3:
                        view = view.rearrange("p (c l) -> p c l", c=4)
                    nc.gpsimd.tensor_copy(view, source).then_inc(s["kv_copied"], 1)

                def mask_keys(t, u, j, first=False):
                    if j == 0 and ready is None:
                        pool.wait_ge(s["k_copied"], t + 1)
                    elif j == 0 and not first:
                        pool.wait_ge(s["scores_ready"], (t - 1) * steps)
                    g = 4 * j // per_group
                    n_groups = max(1, 4 // per_group)
                    n_heads = 4 // n_groups
                    wide = [P, n_groups, n_heads, P]
                    cols = slice(g * P, (g + n_groups) * P)
                    if ready is None:
                        keys = kt[:, u, cols].rearrange("p (g k) -> p g k", k=P)
                    else:
                        keys = ready[1][:, bass.ds(t, 1), cols].rearrange("p a (g k) -> p (a g) k", k=P)
                    i = 4 * j % per_group
                    nc.gpsimd.tensor_tensor(
                        masked_k[:, u, 4 * j:4 * j + 4, :].rearrange("p (g h) k -> p g h k", g=n_groups),
                        spread(keys[:, :, None, :], wide),
                        spread(head_mask[:, None, i:i + n_heads, None], wide), ALU.mult).then_inc(s["keys_masked"], 1)

                def add_output_bias(t, u):
                    if o_bias is None:
                        return
                    pool.wait_ge(s["y_used"], t + 2)
                    nc.gpsimd.tensor_tensor(with_bias[:, u:u + 1, :], resid[:, bass.ds(t, 1), :],
                                            bias_rows[:, None, :], ALU.add).then_inc(s["biased"], 1)

                def pair(it, first, end):
                    for u in range(2):
                        t = it * 2 + u
                        following = not (end and u == 1)
                        second = first and u == 0
                        add_output_bias(t, u)
                        if following and not second:
                            copy_kv(t + 1, 1 - u)
                        if steps == 1:
                            if not end:
                                mask_keys(t + 2, u, 0)
                        elif following:
                            for j in range(steps):
                                mask_keys(t + 1, 1 - u, j, second)

                pool.sem_inc(s["probs_turned"], 2)
                pool.sem_inc(s["o_turned"], 1)
                nc.gpsimd.memset(v[:], 1.0).then_inc(s["const_ready"], 1)
                if o_bias is not None:
                    if gate is None:
                        nc.gpsimd.tensor_copy(bias_rows[:], o_bias).then_inc(s["scaled"], 1)
                    else:
                        nc.gpsimd.tensor_tensor(bias_rows[:], o_bias, spread(gate, [P, D]), ALU.mult).then_inc(s["scaled"], 1)
                    pool.wait_ge(s["scaled"], 1)
                copy_kv(0, 0, True)
                copy_kv(1, 1, True)
                for j in range(steps):
                    mask_keys(0, 0, j, True)
                if steps == 1:
                    mask_keys(1, 1, 0, True)
                pair(0, True, False)
                with pool.Fori(1, tiles // 2 - 1) as it:
                    pair(it, False, False)
                pair(tiles // 2 - 1, False, True)



def rotary_rows(nc, const, *, heads, dk, src_t, wq, wk, tables, turned, tiles):
    inner = heads * dk
    groups = inner // P
    half = dk // 2
    with memory(nc) as (sb, ps):
        x_tile = sb("x_tile", [P, 2, P])
        same = sb("same", [P, 4, heads, dk])
        swap = sb("swap", [P, 4, heads, dk])
        square = sb("square", [P, 4, inner])
        length = sb("length", [P, 4, heads])
        clamped = sb("clamped", [P, 4, heads])
        root = sb("root", [P, 4, heads])
        inv_len = sb("inv_len", [P, 4, heads])
        added = sb("added", [P, 4, heads, dk])
        unit_rows = sb("unit_rows", [P, 2, 2, heads, dk])
        rows = ps("rows", [P, 4, BANK])
        turned_ps = ps("turned_ps", [P, 4, BANK])
        with stage(nc, "x_copied rows_done squared rotated summed clamped rooted inv_ready added_ready "
                       "rows_ready turned_done turned_copied") as (block, s):

            def tile_pairs(engine, body, tail):
                body(0, 0, False, False, True, True)
                body(1, 1, True, False, True, True)
                with engine.Fori(1, tiles // 2 - 1) as it:
                    for u in range(2):
                        body(it * 2 + u, u, True, True, True, True)
                body(tiles - 2, 0, True, True, True, False)
                body(tiles - 1, 1, True, True, False, False)
                tail()

            @block.tensor
            def _(pe):
                def project(t, u):
                    pe.wait_ge(s["x_copied"], t + 1)
                    for i, weight in ((0, wq), (1, wk)):
                        pe.wait_ge(s["rotated"], 3 * (2 * t + i) + 3)
                        nc.tensor.matmul(rows[:, 2 * u + i, 0:inner], x_tile[:, u, :], weight, start=True,
                                         stop=True).then_inc(s["rows_done"], 1)

                def turn(t, u):
                    for i in range(2):
                        pe.wait_ge(s["rows_ready"], 2 * t + i + 5)
                        pe.wait_ge(s["turned_copied"], 2 * t + i + 1)
                        flat = unit_rows[:, u, i, :, :].rearrange("p h c -> p (h c)")
                        for g in range(groups):
                            last = nc.tensor.transpose(turned_ps[:, 2 * u + i, g * P:(g + 1) * P],
                                                       flat[:, g * P:(g + 1) * P], const["ident"][:])
                        last.then_inc(s["turned_done"], 1)

                def body(t, u, earlier, before, following, ahead):
                    if following:
                        project(t + 1, 1 - u)
                    if earlier:
                        turn(t - 1, 1 - u)

                project(0, 0)
                tile_pairs(pe, body, lambda: turn(tiles - 1, 1))

            @block.scalar
            def _(act):
                def copy_x(t, u):
                    nc.scalar.activation(x_tile[:, u, :], src_t(t), ACT.Copy).then_inc(s["x_copied"], 1)

                def square_rows(t, u):
                    for i in range(2):
                        act.wait_ge(s["rows_done"], 2 * t + i + 1)
                        act.wait_ge(s["summed"], 2 * t + i + 1)
                        nc.scalar.activation(square[:, 2 * u + i, :], rows[:, 2 * u + i, 0:inner],
                                             ACT.Square).then_inc(s["squared"], 1)

                def take_roots(t, u):
                    act.wait_ge(s["clamped"], t + 1)
                    nc.scalar.activation(root[:, 2 * u:2 * u + 2, :], clamped[:, 2 * u:2 * u + 2, :],
                                         ACT.Sqrt).then_inc(s["rooted"], 1)

                def copy_out(t, u):
                    for i in range(2):
                        act.wait_ge(s["turned_done"], 2 * t + i + 5)
                        nc.scalar.activation(turned[i][:, bass.ds(t, 1), :], turned_ps[:, 2 * u + i:2 * u + i + 1, 0:inner],
                                             ACT.Copy).then_inc(s["turned_copied"], 1)

                def body(t, u, earlier, before, following, ahead):
                    square_rows(t, u)
                    if ahead:
                        copy_x(t + 2, u)
                    if earlier:
                        take_roots(t - 1, 1 - u)
                    if before:
                        copy_out(t - 2, u)

                def tail():
                    take_roots(tiles - 1, 1)
                    copy_out(tiles - 2, 0)
                    copy_out(tiles - 1, 1)

                act.sem_inc(s["turned_copied"], 4)
                copy_x(0, 0)
                copy_x(1, 1)
                tile_pairs(act, body, tail)

            @block.vector
            def _(dve):
                def rotate(t, u, i):
                    n = 2 * t + i
                    bank = rows[:, 2 * u + i, 0:inner].rearrange("p (h c) -> p h c", c=dk)
                    c_same, c_swap = tables[2 * i], tables[2 * i + 1]
                    dve.wait_ge(s["squared"], n + 1)
                    dve.wait_ge(s["added_ready"], n + 1)
                    nc.vector.tensor_tensor(same[:, 2 * u + i, :, :], bank, spread(c_same[:, None, :], [P, heads, dk]),
                                            ALU.mult).then_inc(s["rotated"], 1)
                    nc.vector.tensor_tensor(swap[:, 2 * u + i, :, 0:half], bank[:, :, half:dk],
                                            spread(c_swap[:, None, 0:half], [P, heads, half]),
                                            ALU.mult).then_inc(s["rotated"], 1)
                    nc.vector.tensor_tensor(swap[:, 2 * u + i, :, half:dk], bank[:, :, 0:half],
                                            spread(c_swap[:, None, half:dk], [P, heads, half]),
                                            ALU.mult).then_inc(s["rotated"], 1)
                    nc.vector.tensor_reduce(length[:, 2 * u + i, :],
                                            square[:, 2 * u + i, :].rearrange("p (h c) -> p h c", c=dk),
                                            AX.X, ALU.add).then_inc(s["summed"], 1)

                def invert(t, u):
                    dve.wait_ge(s["rooted"], t + 1)
                    dve.wait_ge(s["rows_ready"], 2 * t + 2)
                    nc.vector.reciprocal(inv_len[:, 2 * u:2 * u + 2, :], root[:, 2 * u:2 * u + 2, :]
                                         ).then_inc(s["inv_ready"], 1)

                def body(t, u, earlier, before, following, ahead):
                    rotate(t, u, 0)
                    if earlier:
                        invert(t - 1, 1 - u)
                    rotate(t, u, 1)
                    dve.wait_ge(s["summed"], 2 * t + 6)
                    nc.vector.tensor_scalar(clamped[:, 2 * u:2 * u + 2, :], length[:, 2 * u:2 * u + 2, :], 1e-24, None,
                                            ALU.max).then_inc(s["clamped"], 1)

                dve.sem_inc(s["rotated"], 12)
                dve.sem_inc(s["summed"], 4)
                tile_pairs(dve, body, lambda: invert(tiles - 1, 1))

            @block.gpsimd
            def _(pool):
                def scale_rows(t, u):
                    pool.wait_ge(s["inv_ready"], t + 1)
                    for i in range(2):
                        pool.wait_ge(s["turned_done"], 2 * t + i + 1)
                        pool.wait_ge(s["added_ready"], 2 * t + i + 5)
                        nc.gpsimd.tensor_tensor(unit_rows[:, u, i, :, :], added[:, 2 * u + i, :, :],
                                                spread(inv_len[:, 2 * u + i, :, None], [P, heads, dk]),
                                                ALU.mult).then_inc(s["rows_ready"], 1)

                def add(t, u, i):
                    pool.wait_ge(s["rotated"], 12 + 3 * (2 * t + i) + 3)
                    pool.wait_ge(s["rows_ready"], 2 * t + i + 1)
                    nc.gpsimd.tensor_tensor(added[:, 2 * u + i, :, :], same[:, 2 * u + i, :, :],
                                            swap[:, 2 * u + i, :, :], ALU.add).then_inc(s["added_ready"], 1)

                def body(t, u, earlier, before, following, ahead):
                    add(t, u, 0)
                    if earlier:
                        scale_rows(t - 1, 1 - u)
                    add(t, u, 1)

                pool.sem_inc(s["added_ready"], 4)
                pool.sem_inc(s["rows_ready"], 4)
                pool.sem_inc(s["turned_done"], 4)
                tile_pairs(pool, body, lambda: scale_rows(tiles - 1, 1))



def feed_forward(nc, const, *, src_t, up, up_bias, down, down_bias, rows, chunks, act_func, resid,
                 value=None, value_bias=None):
    gated = value is not None
    with memory(nc) as (sb, ps):
        hidden = sb("hidden", [rows, 2, chunks, BANK])
        acted = sb("acted", [rows, 2, BANK])
        up_ps = ps("up_ps", [P, 2, BANK])
        value_ps = ps("value_ps", [P, 2, BANK])
        down_ps = ps("down_ps", [P, 2, BANK])
        with stage(nc, "up_done value_done acted_ready hidden_ready down_done y_used biased") as (block, s):

            @block.tensor
            def _(pe):
                def expand(i, b):
                    for c in range(chunks):
                        n = i * chunks + c
                        slot = (b * chunks + c) % 2
                        cols = slice(c * rows, (c + 1) * rows)
                        pe.wait_ge(s["acted_ready"], n + 1)
                        nc.tensor.matmul(up_ps[0:rows, slot, :], up[:, cols], src_t[:, bass.ds(i * BANK, BANK)],
                                         start=True, stop=True).then_inc(s["up_done"], 1)
                        if gated:
                            pe.wait_ge(s["hidden_ready"], n + 1)
                            nc.tensor.matmul(value_ps[0:rows, slot, :], value[:, cols],
                                             src_t[:, bass.ds(i * BANK, BANK)],
                                             start=True, stop=True).then_inc(s["value_done"], 1)

                def contract(i, b):
                    if gated:
                        pe.wait_ge(s["hidden_ready"], (i + 1) * chunks + 2)
                    else:
                        pe.wait_ge(s["acted_ready"], (i + 1) * chunks + 2)
                    pe.wait_ge(s["y_used"], i + 1)
                    for k in range(4):
                        for c in range(chunks):
                            last = nc.tensor.matmul(down_ps[:, b, k * P:(k + 1) * P],
                                                    hidden[:, b, c, k * P:(k + 1) * P], down[:, c, :],
                                                    start=c == 0, stop=c == chunks - 1)
                    last.then_inc(s["down_done"], 1)

                expand(0, 0)
                with pe.Fori(0, TILES // 8 - 1) as it:
                    expand(it * 2 + 1, 1)
                    contract(it * 2, 0)
                    expand(it * 2 + 2, 0)
                    contract(it * 2 + 1, 1)
                expand(TILES // 4 - 1, 1)
                contract(TILES // 4 - 2, 0)
                contract(TILES // 4 - 1, 1)

            @block.scalar
            def _(act):
                act.sem_inc(s["acted_ready"], 2)
                with act.Fori(0, TILES // 8) as it:
                    for b in range(2):
                        i = it * 2 + b
                        for c in range(chunks):
                            n = i * chunks + c
                            slot = (b * chunks + c) % 2
                            act.wait_ge(s["up_done"], n + 1)
                            if gated:
                                act.wait_ge(s["hidden_ready"], n + 1)
                                dst = acted[:, slot, :]
                            else:
                                if c == 0:
                                    act.wait_ge(s["down_done"], i + 1)
                                dst = hidden[:, b, c, :]
                            nc.scalar.activation(dst, up_ps[0:rows, slot, :], act_func,
                                                 bias=up_bias[0:rows, c:c + 1]).then_inc(s["acted_ready"], 1)

            @block.vector
            def _(dve):
                dve.sem_inc(s["hidden_ready"], 2)
                dve.sem_inc(s["y_used"], 2)
                dve.sem_inc(s["down_done"], 2)

                def multiply(i, b):
                    if not gated:
                        return
                    for c in range(chunks):
                        n = i * chunks + c
                        slot = (b * chunks + c) % 2
                        dve.wait_ge(s["value_done"], n + 1)
                        dve.wait_ge(s["acted_ready"], n + 3)
                        if c == 0:
                            dve.wait_ge(s["down_done"], i + 1)
                        nc.vector.scalar_tensor_tensor(out=hidden[:, b, c, :], in0=value_ps[0:rows, slot, :],
                                                       scalar=value_bias[0:rows, c:c + 1], in1=acted[:, slot, :],
                                                       op0=ALU.add, op1=ALU.mult).then_inc(s["hidden_ready"], 1)

                def add(i, b):
                    dve.wait_ge(s["down_done"], i + 3)
                    dve.wait_ge(s["biased"], i + 1)
                    rows_ = resid[:, bass.ds(i * 4, 4), :]
                    nc.vector.tensor_tensor(rows_, down_ps[:, b, :].rearrange("p (k d) -> p k d", d=D), rows_,
                                            ALU.add).then_inc(s["y_used"], 1)

                multiply(0, 0)
                with dve.Fori(0, TILES // 8 - 1) as it:
                    multiply(it * 2 + 1, 1)
                    add(it * 2, 0)
                    multiply(it * 2 + 2, 0)
                    add(it * 2 + 1, 1)
                multiply(TILES // 4 - 1, 1)
                add(TILES // 4 - 2, 0)
                add(TILES // 4 - 1, 1)

            @block.gpsimd
            def _(pool):
                with pool.Fori(0, TILES // 4) as i:
                    rows_ = resid[:, bass.ds(i * 4, 4), :]
                    nc.gpsimd.tensor_tensor(rows_, rows_, spread(down_bias[:, None, :], [P, 4, D]),
                                            ALU.add).then_inc(s["biased"], 1)



def router(nc, const, src_t, weight, bias, probs, experts):
    with memory(nc) as (sb, ps):
        tile = sb("tile", [P, 2, 4, P])
        shifted = sb("shifted", [P, TILES, experts])
        most = sb("most", [P, TILES])
        total = sb("total", [P, TILES])
        inv = sb("inv", [P, TILES])
        logits = ps("logits", [P, 2, BANK])
        with stage(nc, "tile_copied logits_done logits_used chain exp_done") as (block, s):

            @block.tensor
            def _(pe):
                with pe.Fori(0, TILES // 8) as it:
                    for u in range(2):
                        n = it * 2 + u
                        pe.wait_ge(s["tile_copied"], n + 1)
                        pe.wait_ge(s["logits_used"], n + 1)
                        for k in range(4):
                            last = nc.tensor.matmul(logits[:, u, k * experts:(k + 1) * experts], tile[:, u, k, :],
                                                    weight, start=True, stop=True)
                        last.then_inc(s["logits_done"], 1)

            @block.vector
            def _(dve):
                dve.sem_inc(s["logits_used"], 2)
                with dve.Fori(0, TILES // 8) as it:
                    for u in range(2):
                        n = it * 2 + u
                        dve.wait_ge(s["logits_done"], n + 3)
                        src = logits[:, u, 0:4 * experts].rearrange("p (k e) -> p k e", e=experts)
                        dst = shifted[:, bass.ds(n * 4, 4), :]
                        if bias is None:
                            ins = nc.vector.tensor_copy(dst, src)
                        else:
                            ins = nc.vector.tensor_tensor(dst, src, spread(bias[:, None, :], [P, 4, experts]), ALU.add)
                        ins.then_inc(s["logits_used"], 1)
                dve.wait_ge(s["logits_used"], TILES // 4 + 2)
                nc.vector.tensor_reduce(most[:], shifted[:], AX.X, ALU.max).then_inc(s["chain"], 1)
                dve.wait_ge(s["chain"], 1)
                nc.vector.tensor_tensor(shifted[:], shifted[:], spread(most[:, :, None], [P, TILES, experts]),
                                        ALU.subtract).then_inc(s["chain"], 1)
                dve.wait_ge(s["exp_done"], 1)
                nc.vector.tensor_reduce(total[:], shifted[:], AX.X, ALU.add).then_inc(s["chain"], 1)
                dve.wait_ge(s["chain"], 3)
                nc.vector.reciprocal(inv[:], total[:]).then_inc(s["chain"], 1)
                dve.wait_ge(s["chain"], 4)
                nc.vector.tensor_tensor(probs[:], shifted[:], spread(inv[:, :, None], [P, TILES, experts]),
                                        ALU.mult).then_inc(s["chain"], 1)

            @block.scalar
            def _(act):
                act.sem_inc(s["logits_done"], 2)
                with act.Fori(0, TILES // 8) as it:
                    for u in range(2):
                        act.wait_ge(s["logits_done"], it * 2 + u + 1)
                        nc.scalar.activation(tile[:, u, :, :].rearrange("p k n -> p (k n)"),
                                             src_t[:, bass.ds((it * 2 + u) * BANK, BANK)],
                                             ACT.Copy).then_inc(s["tile_copied"], 1)
                act.wait_ge(s["chain"], 2)
                nc.scalar.activation(shifted[:], shifted[:], ACT.Exp).then_inc(s["exp_done"], 1)


def pick_first(nc, values, threshold, quota, picked, experts):
    with memory(nc) as (sb, ps):
        above = sb("above", [P, TILES, experts])
        equal = sb("equal", [P, TILES, experts])
        ones = sb("ones", [P, TILES * experts])
        upto = sb("upto", [P, TILES, experts])
        before = sb("before", [P, TILES])
        count = sb("count", [P, TILES])
        with stage(nc, "chain") as (block, s):

            @block.vector
            def _(dve):
                wide = [P, TILES, experts]
                nc.vector.memset(ones[:], 1.0).then_inc(s["chain"], 1)
                nc.vector.memset(before[:], 0.0).then_inc(s["chain"], 1)
                nc.vector.tensor_tensor(above[:], values, spread(threshold[:, :, None], wide),
                                        ALU.is_gt).then_inc(s["chain"], 1)
                nc.vector.tensor_tensor(equal[:], values, spread(threshold[:, :, None], wide),
                                        ALU.is_equal).then_inc(s["chain"], 1)
                dve.wait_ge(s["chain"], 4)
                nc.vector.tensor_reduce(count[:], above[:], AX.X, ALU.add).then_inc(s["chain"], 1)
                nc.vector.tensor_tensor_scan(upto[:].rearrange("p t e -> p (t e)"), ones[:],
                                             equal[:].rearrange("p t e -> p (t e)"), 0.0, ALU.mult,
                                             ALU.add).then_inc(s["chain"], 1)
                dve.wait_ge(s["chain"], 6)
                nc.vector.tensor_copy(before[:, 1:TILES], upto[:, 0:TILES - 1, experts - 1]).then_inc(s["chain"], 1)
                dve.wait_ge(s["chain"], 7)
                nc.vector.tensor_tensor(before[:], before[:], count[:], ALU.subtract).then_inc(s["chain"], 1)
                dve.wait_ge(s["chain"], 8)
                nc.vector.tensor_tensor(upto[:], upto[:], spread(before[:, :, None], wide),
                                        ALU.subtract).then_inc(s["chain"], 1)
                dve.wait_ge(s["chain"], 9)
                nc.vector.scalar_tensor_tensor(out=equal[:], in0=upto[:], scalar=float(quota), in1=equal[:],
                                               op0=ALU.is_le, op1=ALU.mult).then_inc(s["chain"], 1)
                dve.wait_ge(s["chain"], 10)
                nc.vector.tensor_tensor(picked[:], above[:], equal[:], ALU.add).then_inc(s["chain"], 1)


def rank_largest(nc, values, threshold, experts, rank):
    with memory(nc) as (sb, ps):
        rows = sb("rows", [P, 8, experts])
        largest = sb("largest", [P, 8, 8])
        scratch = sb("scratch", [P, 1])
        with stage(nc, "rows_copied found taken") as (block, s):

            @block.vector
            def _(dve):
                dve.sem_inc(s["found"], 8)
                dve.sem_inc(s["taken"], 1)
                with dve.Fori(0, TILES // 8) as it:
                    dve.wait_ge(s["found"], it * 8 + 8)
                    nc.vector.tensor_copy(rows[:], values[:, bass.ds(it * 8, 8), :]).then_inc(s["rows_copied"], 1)
                    dve.wait_ge(s["taken"], it + 1)
                    dve.wait_ge(s["rows_copied"], it * 2 + 1)
                    nc.vector.memset(scratch[:], 0.0).then_inc(s["rows_copied"], 1)
                    for k in range(8):
                        nc.vector.max(largest[:, k, :], rows[:, k, :]).then_inc(s["found"], 1)
                    dve.wait_ge(s["found"], it * 8 + 16)
                    nc.vector.tensor_copy(threshold[:, bass.ds(it * 8, 8)],
                                          largest[:, :, rank - 1]).then_inc(s["taken"], 1)


def ranks_over_tokens(nc, const, mask, ranks, experts):
    with memory(nc) as (sb, ps):
        ones = sb("ones", [P, TILES])
        upto = sb("upto", [P, TILES, experts])
        counts = ps("counts", [P, BANK])
        with stage(nc, "ones_set scanned counted copied") as (block, s):

            @block.vector
            def _(dve):
                nc.vector.memset(ones[:], 1.0).then_inc(s["ones_set"], 1)
                dve.wait_ge(s["ones_set"], 1)
                for e in range(experts):
                    nc.vector.tensor_tensor_scan(upto[:, :, e], ones[:], mask[:, :, e], 0.0, ALU.mult,
                                                 ALU.add).then_inc(s["scanned"], 1)
                dve.wait_ge(s["scanned"], experts)
                nc.vector.tensor_tensor(upto[:], upto[:], mask[:], ALU.subtract).then_inc(s["scanned"], 1)
                dve.wait_ge(s["counted"], 1)
                nc.vector.tensor_copy(ranks[:], counts[:, 0:TILES * experts].rearrange("p (t e) -> p t e", e=experts)
                                      ).then_inc(s["copied"], 1)

            @block.tensor
            def _(pe):
                pe.wait_ge(s["scanned"], experts + 1)
                nc.tensor.matmul(counts[:, 0:TILES * experts], const["ones"][:], upto[:].rearrange("p t e -> p (t e)"),
                                 start=True, stop=False)
                nc.tensor.matmul(counts[:, 0:TILES * experts], const["earlier"][:], mask[:].rearrange("p t e -> p (t e)"),
                                 start=False, stop=True).then_inc(s["counted"], 1)


def expert_thresholds(nc, const, probs, threshold, missing, equal, above, experts, capacity):
    with memory(nc) as (sb, ps):
        bit = sb("bit", [P, experts], I32)
        trial = sb("trial", [P, experts])
        passed = sb("passed", [P, TILES, experts])
        count = sb("count", [P, experts])
        kept = sb("kept", [P, experts])
        totals = ps("totals", [P, BANK])
        wide = [P, TILES, experts]
        with stage(nc, "ready tried passed_ready counted summed decided lowered") as (block, s):

            @block.vector
            def _(dve):
                nc.vector.memset(bit[:], 1 << 30).then_inc(s["ready"], 1)
                nc.vector.memset(threshold[:], 0.0).then_inc(s["ready"], 1)
                dve.wait_ge(s["ready"], 2)
                dve.sem_inc(s["lowered"], 2)
                with dve.Fori(0, 31) as i:
                    dve.wait_ge(s["lowered"], i * 2 + 2)
                    nc.vector.tensor_tensor(trial[:].bitcast(I32), threshold[:].bitcast(I32), bit[:],
                                            ALU.bitwise_or).then_inc(s["tried"], 1)
                    dve.wait_ge(s["tried"], i + 1)
                    nc.vector.tensor_tensor(passed[:], probs[:], spread(trial[:, None, :], wide),
                                            ALU.is_ge).then_inc(s["passed_ready"], 1)
                    dve.wait_ge(s["passed_ready"], i + 1)
                    nc.vector.tensor_reduce(count[:], passed[:].rearrange("p t e -> p e t"), AX.X,
                                            ALU.add).then_inc(s["counted"], 1)
                    nc.vector.tensor_single_scalar(bit[:], bit[:], 1, ALU.logical_shift_right).then_inc(s["lowered"], 1)
                    dve.wait_ge(s["summed"], i + 1)
                    nc.vector.scalar_tensor_tensor(out=kept[:], in0=totals[:, 0:experts], scalar=float(capacity),
                                                   in1=trial[:], op0=ALU.is_ge, op1=ALU.mult).then_inc(s["decided"], 1)
                    dve.wait_ge(s["decided"], i + 1)
                    nc.vector.tensor_tensor(threshold[:], threshold[:], kept[:], ALU.max).then_inc(s["lowered"], 1)
                dve.wait_ge(s["lowered"], 64)
                nc.vector.tensor_tensor(above[:], probs[:], spread(threshold[:, None, :], wide),
                                        ALU.is_gt).then_inc(s["ready"], 1)
                nc.vector.tensor_tensor(equal[:], probs[:], spread(threshold[:, None, :], wide),
                                        ALU.is_equal).then_inc(s["ready"], 1)
                dve.wait_ge(s["ready"], 3)
                nc.vector.tensor_reduce(count[:], above[:].rearrange("p t e -> p e t"), AX.X,
                                        ALU.add).then_inc(s["counted"], 1)
                dve.wait_ge(s["summed"], 32)
                nc.vector.tensor_scalar(missing[:], totals[:, 0:experts], -1.0, float(capacity), ALU.mult,
                                        ALU.add).then_inc(s["ready"], 1)

            @block.tensor
            def _(pe):
                with pe.Fori(0, 32) as i:
                    pe.wait_ge(s["counted"], i + 1)
                    nc.tensor.matmul(totals[:, 0:experts], const["ones"][:], count[:], start=True,
                                     stop=True).then_inc(s["summed"], 1)



def mix_top_experts(nc, const, *, src_t, gate_w, up_w, down_w, combine, resid, gate):
    widths = [BANK] * 4 + [P]
    chunks = len(widths)
    with memory(nc) as (sb, ps):
        tile = sb("tile", [P, 2, P])
        acted = sb("acted", [P, 2, BANK])
        product = sb("product", [P, 2, BANK])
        weighted = sb("weighted", [P, 2, BANK])
        hidden_t = sb("hidden_t", [P, 2, BANK])
        gate_ps = ps("gate_ps", [P, 2, BANK])
        up_ps = ps("up_ps", [P, 2, BANK])
        turned_ps = ps("turned_ps", [P, 2, BANK])
        y_ps = ps("y_ps", [P, 2, BANK])
        with stage(nc, "tile_copied projected acted_ready product_ready weighted_ready turned t_copied y_done "
                       "y_used stats_done") as (block, s):

            def steps(it, first, end):
                def at(k):
                    if k < 0:
                        return None if first else (it * 2 - 1, 1, k + chunks, (k + 2 * chunks) % 2)
                    u, c = divmod(k, chunks)
                    return (it * 2 + u, u, c, k % 2)

                return [(at(k), at(k - 1), at(k - 2)) for k in range(2 * chunks)]

            @block.tensor
            def _(pe):
                def project(t, u, c, slot):
                    n = t * chunks + c
                    if c == 0:
                        pe.wait_ge(s["tile_copied"], t + 1)
                    pe.wait_ge(s["product_ready"], n + 1)
                    cols = slice(c * BANK, c * BANK + widths[c])
                    nc.tensor.matmul(gate_ps[:, slot, 0:widths[c]], tile[:, u, :], gate_w[:, cols], start=True,
                                     stop=True)
                    nc.tensor.matmul(up_ps[:, slot, 0:widths[c]], tile[:, u, :], up_w[:, cols], start=True,
                                     stop=True).then_inc(s["projected"], 1)

                def turn(t, u, c, slot):
                    n = t * chunks + c
                    pe.wait_ge(s["weighted_ready"], n + 3)
                    pe.wait_ge(s["t_copied"], n + 1)
                    for q in range(widths[c] // P):
                        last = nc.tensor.transpose(turned_ps[:, slot, q * P:(q + 1) * P],
                                                   weighted[:, slot, q * P:(q + 1) * P], const["ident"][:])
                    last.then_inc(s["turned"], 1)

                def contract(t, u, c, slot):
                    n = t * chunks + c
                    pe.wait_ge(s["t_copied"], n + 3)
                    if c == 0:
                        pe.wait_ge(s["y_used"], t + 1)
                    for q in range(widths[c] // P):
                        last = nc.tensor.matmul(y_ps[:, u, 0:D], hidden_t[:, slot, q * P:(q + 1) * P],
                                                down_w[:, 4 * c + q, :], start=c == 0 and q == 0,
                                                stop=c == chunks - 1)
                    if c == chunks - 1:
                        last.then_inc(s["y_done"], 1)

                def pair(it, first, end):
                    for now, before, two_before in steps(it, first, end):
                        project(*now)
                        if two_before:
                            contract(*two_before)
                        if before:
                            turn(*before)

                pair(0, True, False)
                with pe.Fori(1, TILES // 2) as it:
                    pair(it, False, False)
                contract(TILES - 1, 1, chunks - 2, 0)
                turn(TILES - 1, 1, chunks - 1, 1)
                contract(TILES - 1, 1, chunks - 1, 1)

            @block.scalar
            def _(act):
                def activate(t, u, c, slot):
                    act.wait_ge(s["projected"], t * chunks + c + 1)
                    nc.scalar.activation(acted[:, slot, 0:widths[c]], gate_ps[:, slot, 0:widths[c]],
                                         ACT.Silu).then_inc(s["acted_ready"], 1)

                def copy_turned(t, u, c, slot):
                    act.wait_ge(s["turned"], t * chunks + c + 3)
                    nc.scalar.activation(hidden_t[:, slot, 0:widths[c]], turned_ps[:, slot, 0:widths[c]],
                                         ACT.Copy).then_inc(s["t_copied"], 1)

                def pair(it, first, end):
                    for now, before, _ in steps(it, first, end):
                        activate(*now)
                        if before:
                            copy_turned(*before)

                act.sem_inc(s["t_copied"], 2)
                pair(0, True, False)
                with act.Fori(1, TILES // 2) as it:
                    pair(it, False, False)
                copy_turned(TILES - 1, 1, chunks - 1, 1)

            @block.vector
            def _(dve):
                def multiply(t, u, c, slot):
                    n = t * chunks + c
                    dve.wait_ge(s["acted_ready"], n + 1)
                    dve.wait_ge(s["weighted_ready"], n + 1)
                    nc.vector.tensor_tensor(product[:, slot, 0:widths[c]], up_ps[:, slot, 0:widths[c]],
                                            acted[:, slot, 0:widths[c]], ALU.mult).then_inc(s["product_ready"], 1)

                def add(t, u):
                    dve.wait_ge(s["y_done"], t + 1)
                    rows = resid[:, bass.ds(t, 1), :]
                    nc.vector.scalar_tensor_tensor(out=rows, in0=y_ps[:, u:u + 1, 0:D], scalar=gate, in1=rows,
                                                   op0=ALU.mult, op1=ALU.add).then_inc(s["y_used"], 1)

                def row_stats(t):
                    dve.wait_ge(s["y_used"], t + 3)
                    nc.vector.bn_stats(const["row_stats"][:, bass.ds(t, 1), :], resid[:, bass.ds(t, 1), :]
                                       ).then_inc(s["stats_done"], 1)

                def pair(it, first, end):
                    for k, (now, _, _) in enumerate(steps(it, first, end)):
                        multiply(*now)
                        if k % chunks == 3 and not (first and k < chunks):
                            row_stats(now[0] - 1)
                        if k % chunks == 2 and not (first and k < chunks):
                            add(now[0] - 1, 1 - now[1])

                dve.sem_inc(s["product_ready"], 2)
                dve.sem_inc(s["y_used"], 2)
                pair(0, True, False)
                with dve.Fori(1, TILES // 2) as it:
                    pair(it, False, False)
                add(TILES - 1, 1)
                row_stats(TILES - 1)

            @block.gpsimd
            def _(pool):
                def copy_tile(t, u):
                    nc.gpsimd.tensor_copy(tile[:, u, :], tile_cols(src_t, t)).then_inc(s["tile_copied"], 1)

                def weight(t, u, c, slot):
                    n = t * chunks + c
                    pool.wait_ge(s["product_ready"], n + 3)
                    pool.wait_ge(s["turned"], n + 1)
                    experts = widths[c] // 64
                    nc.gpsimd.tensor_tensor(
                        weighted[:, slot, 0:widths[c]].rearrange("p (e i) -> p e i", i=64),
                        product[:, slot, 0:widths[c]].rearrange("p (e i) -> p e i", i=64),
                        spread(combine[:, bass.ds(t, 1), c * 8:c * 8 + experts].rearrange("p t e -> p (t e)")[:, :, None],
                               [P, experts, 64]), ALU.mult).then_inc(s["weighted_ready"], 1)

                def pair(it, first, end):
                    for k, (now, _, _) in enumerate(steps(it, first, end)):
                        t, u, c, _slot = now
                        if c == 1 and not (end and u == 1):
                            if not (first and u == 0):
                                pool.wait_ge(s["projected"], t * chunks)
                            copy_tile(t + 1, 1 - u)
                        weight(*now)

                pool.sem_inc(s["weighted_ready"], 2)
                pool.sem_inc(s["turned"], 2)
                copy_tile(0, 0)
                pair(0, True, False)
                with pool.Fori(1, TILES // 2 - 1) as it:
                    pair(it, False, False)
                pair(TILES // 2 - 1, False, True)


def mix_chosen_tokens(nc, const, *, src_t, up_w, up_b, down_w, weights, resid):
    groups, chunks, rows = 4, 3, 114
    steps = TOKENS // BANK
    with memory(nc) as (sb, ps):
        hidden = sb("hidden", [rows, 2, chunks, BANK])
        up_ps = ps("up_ps", [P, 2, BANK])
        down_ps = ps("down_ps", [P, 2, BANK])
        with stage(nc, "up_done acted_ready down_done added") as (block, s):

            @block.tensor
            def _(pe):
                def expand(it, g):
                    m = it * groups + g
                    for c in range(chunks):
                        slot = (g * chunks + c) % 2
                        pe.wait_ge(s["acted_ready"], m * chunks + c + 1)
                        nc.tensor.matmul(up_ps[0:rows, slot, :], up_w[:, (g * chunks + c) * rows:(g * chunks + c + 1) * rows],
                                         src_t[:, bass.ds(it * BANK, BANK)], start=True, stop=True).then_inc(s["up_done"], 1)

                def contract(it, g):
                    m = it * groups + g
                    pe.wait_ge(s["acted_ready"], (m + 1) * chunks + 2)
                    for k in range(4):
                        n = m * 4 + k
                        pe.wait_ge(s["added"], n * 2 + 6)
                        for c in range(chunks):
                            last = nc.tensor.matmul(down_ps[:, k % 2, 0:2 * D], hidden[:, g % 2, c, k * P:(k + 1) * P],
                                             down_w[:, c, g * 2 * D:(g + 1) * 2 * D], start=c == 0,
                                             stop=c == chunks - 1)
                        last.then_inc(s["down_done"], 1)

                def step(it, end):
                    for g in range(groups):
                        if g < groups - 1:
                            expand(it, g + 1)
                        elif not end:
                            expand(it + 1, 0)
                        contract(it, g)

                expand(0, 0)
                with pe.Fori(0, steps - 1) as it:
                    step(it, False)
                step(steps - 1, True)

            @block.scalar
            def _(act):
                act.sem_inc(s["acted_ready"], 2)
                with act.Fori(0, steps) as it:
                    for g in range(groups):
                        for c in range(chunks):
                            act.wait_ge(s["up_done"], (it * groups + g) * chunks + c + 1)
                            nc.scalar.activation(hidden[:, g % 2, c, :], up_ps[0:rows, (g * chunks + c) % 2, :],
                                                 ACT.Silu, bias=up_b[0:rows, g * chunks + c:g * chunks + c + 1]
                                                 ).then_inc(s["acted_ready"], 1)

            @block.vector
            def _(dve):
                dve.sem_inc(s["added"], 8)
                with dve.Fori(0, steps) as it:
                    for g in range(groups):
                        for k in range(4):
                            n = (it * groups + g) * 4 + k
                            dve.wait_ge(s["down_done"], n + 1)
                            row = resid[:, bass.ds(it * 4 + k, 1), :]
                            for e in range(2):
                                dve.wait_ge(s["added"], n * 2 + 2 if e == 0 else n * 2 + 9)
                                nc.vector.scalar_tensor_tensor(
                                    out=row, in0=down_ps[:, k % 2:k % 2 + 1, e * D:(e + 1) * D],
                                    scalar=weights[:, bass.ds((it * 4 + k) * 8 + g * 2 + e, 1)], in1=row,
                                    op0=ALU.mult, op1=ALU.add).then_inc(s["added"], 1)


def merge_linear_experts(nc, const, w1_t, w2, b1, b2, merged, merged_b, experts, chunks):
    with memory(nc) as (sb, ps):
        w_ps = ps("w_ps", [P, 2, BANK])
        b_ps = ps("b_ps", [P, 2, BANK])
        with stage(nc, "w_done b_done w_copied b_copied") as (block, s):

            @block.tensor
            def _(pe):
                for e in range(experts):
                    if e >= 2:
                        pe.wait_ge(s["w_copied"], e - 1)
                        pe.wait_ge(s["b_copied"], e - 1)
                    for c in range(chunks):
                        last = nc.tensor.matmul(w_ps[:, e % 2, 0:D], w1_t[:, c, e, :], w2[:, c, e, :], start=c == 0,
                                                stop=c == chunks - 1)
                    last.then_inc(s["w_done"], 1)
                    for c in range(chunks):
                        nc.tensor.matmul(b_ps[0:1, e % 2, 0:D], b1[:, c, e:e + 1], w2[:, c, e, :], start=c == 0,
                                         stop=False)
                    nc.tensor.matmul(b_ps[0:1, e % 2, 0:D], const["ones"][0:1, 0:1], b2[0:1, e * D:(e + 1) * D],
                                     start=False, stop=True).then_inc(s["b_done"], 1)

            @block.vector
            def _(dve):
                for e in range(experts):
                    dve.wait_ge(s["w_done"], e + 1)
                    nc.vector.tensor_copy(merged[:, e * D:(e + 1) * D], w_ps[:, e % 2, 0:D]).then_inc(s["w_copied"], 1)

            @block.scalar
            def _(act):
                for e in range(experts):
                    act.wait_ge(s["b_done"], e + 1)
                    nc.scalar.activation(merged_b[0:1, e * D:(e + 1) * D], b_ps[0:1, e % 2, 0:D],
                                         ACT.Copy).then_inc(s["b_copied"], 1)


def mix_merged_experts(nc, const, *, src_t, merged, weights, resid, experts):
    halves = experts * D // BANK
    per_bank = experts // halves
    with memory(nc) as (sb, ps):
        tile = sb("tile", [P, 4, P])
        y_ps = ps("y_ps", [P, 4, halves, BANK])
        with stage(nc, "tile_copied y_done added") as (block, s):

            @block.scalar
            def _(act):
                act.sem_inc(s["y_done"], 4)
                with act.Fori(0, TILES // 4) as it:
                    for v in range(4):
                        act.wait_ge(s["y_done"], it * 4 + v + 1)
                        nc.scalar.activation(tile[:, v, :], tile_cols(src_t, it * 4 + v),
                                             ACT.Copy).then_inc(s["tile_copied"], 1)

            @block.tensor
            def _(pe):
                with pe.Fori(0, TILES // 4) as it:
                    for v in range(4):
                        t = it * 4 + v
                        pe.wait_ge(s["tile_copied"], t + 1)
                        pe.wait_ge(s["added"], (it * 2 + v // 2 + 1) * 2 * experts)
                        for a in range(halves):
                            cols = slice(a * BANK, (a + 1) * BANK)
                            last = nc.tensor.matmul(y_ps[:, v, a, :], tile[:, v, :], merged[:, cols], start=True,
                                                    stop=True)
                        last.then_inc(s["y_done"], 1)

            @block.vector
            def _(dve):
                dve.sem_inc(s["added"], 4 * experts)
                with dve.Fori(0, TILES // 4) as it:
                    for pair in range(2):
                        dve.wait_ge(s["y_done"], it * 4 + pair * 2 + 6)
                        for e in range(experts):
                            for u in range(2):
                                v = pair * 2 + u
                                row = resid[:, bass.ds(it * 4 + v, 1), :]
                                if e > 0:
                                    dve.wait_ge(s["added"], (it * 2 + pair + 2) * 2 * experts + 2 * e + u - 1)
                                nc.vector.scalar_tensor_tensor(
                                    out=row, in0=y_ps[:, v, e // per_bank:e // per_bank + 1,
                                                      (e % per_bank) * D:(e % per_bank + 1) * D],
                                    scalar=weights[:, bass.ds((it * 4 + v) * experts + e, 1)], in1=row,
                                    op0=ALU.mult, op1=ALU.add).then_inc(s["added"], 1)


def add_weighted_biases(nc, const, weights, biases, resid, experts=8):
    per_block = P // experts
    blocks = TILES // per_block
    banks = per_block * D // BANK
    with memory(nc) as (sb, ps):
        weights_t = sb("weights_t", [P, blocks, P])
        masked = sb("masked", [P, experts, D])
        of_row = sb("of_row", [P, D])
        rows = sb("rows", [P, per_block, D])
        turned = ps("turned", [P, BANK])
        all_ps = ps("all_ps", [P, 2, BANK])
        y_ps = ps("y_ps", [P, 4, BANK])
        with stage(nc, "turned t_copied repeated masked row_ready rows_ready y_done y_used") as (block, s):

            @block.tensor
            def _(pe):
                for i in range(blocks):
                    last = nc.tensor.transpose(turned[:, i * P:(i + 1) * P], weights[:, i * P:(i + 1) * P],
                                               const["ident"][:])
                last.then_inc(s["turned"], 1)
                for a in range(2):
                    last = nc.tensor.matmul(all_ps[:, a, :], const["ones"][0:1, :], biases[0:1, a * BANK:(a + 1) * BANK],
                                            start=True, stop=True)
                last.then_inc(s["repeated"], 1)
                pe.wait_ge(s["t_copied"], 1)
                pe.wait_ge(s["rows_ready"], 1)
                for n in range(blocks * banks):
                    if n >= 4:
                        pe.wait_ge(s["y_used"], n - 3)
                    i, c = divmod(n, banks)
                    nc.tensor.matmul(y_ps[:, n % 4, :], weights_t[:, i, :],
                                     rows[:, c * 4:(c + 1) * 4, :].rearrange("p t d -> p (t d)"), start=True,
                                     stop=True).then_inc(s["y_done"], 1)

            @block.scalar
            def _(act):
                act.wait_ge(s["turned"], 1)
                nc.scalar.activation(weights_t[:].rearrange("p i n -> p (i n)"), turned[:, 0:blocks * P],
                                     ACT.Copy).then_inc(s["t_copied"], 1)

            @block.vector
            def _(dve):
                dve.wait_ge(s["repeated"], 1)
                for a in range(2):
                    half = slice(a * experts // 2, (a + 1) * experts // 2)
                    nc.vector.tensor_tensor(masked[:, half, :], all_ps[:, a, :].rearrange("p (e d) -> p e d", d=D),
                                            spread(const["expert_of_row"][:, half, None], [P, experts // 2, D]),
                                            ALU.mult).then_inc(s["masked"], 1)
                dve.wait_ge(s["masked"], 2)
                nc.vector.tensor_reduce(of_row[:], masked[:].rearrange("p e d -> p d e"), AX.X,
                                        ALU.add).then_inc(s["row_ready"], 1)
                dve.wait_ge(s["row_ready"], 1)
                nc.vector.tensor_tensor(rows[:], spread(of_row[:, None, :], [P, per_block, D]),
                                        spread(const["tile_of_row"][:, :, None], [P, per_block, D]),
                                        ALU.mult).then_inc(s["rows_ready"], 1)
                for n in range(blocks * banks):
                    dve.wait_ge(s["y_done"], n + 1)
                    out = resid[:, n * 4:(n + 1) * 4, :]
                    nc.vector.tensor_tensor(out, y_ps[:, n % 4, :].rearrange("p (t d) -> p t d", d=D), out,
                                            ALU.add).then_inc(s["y_used"], 1)



def add_all(nc, out, a, b, scale=None):
    with stage(nc, "added") as (block, s):

        @block.vector
        def _(dve):
            if scale is None:
                nc.vector.tensor_tensor(out, a, b, ALU.add).then_inc(s["added"], 1)
            else:
                nc.vector.scalar_tensor_tensor(out=out, in0=a, scalar=scale, in1=b, op0=ALU.mult,
                                               op1=ALU.add).then_inc(s["added"], 1)


def most_probable(nc, probs, most):
    with stage(nc, "found") as (block, s):

        @block.vector
        def _(dve):
            nc.vector.tensor_reduce(most[:], probs[:], AX.X, ALU.max).then_inc(s["found"], 1)


def combine_weights(nc, probs, picked, total, combine, experts):
    with stage(nc, "ones_set weighted summed") as (block, s):

        @block.vector
        def _(dve):
            nc.vector.memset(combine[:], 1.0).then_inc(s["ones_set"], 1)
            nc.vector.tensor_tensor(picked[:], picked[:], probs[:], ALU.mult).then_inc(s["weighted"], 1)
            dve.wait_ge(s["weighted"], 1)
            nc.vector.tensor_reduce(total[:], picked[:], AX.X, ALU.add).then_inc(s["summed"], 1)
            dve.wait_ge(s["summed"], 1)
            nc.vector.tensor_scalar(total[:], total[:], 1e-12, None, ALU.max).then_inc(s["summed"], 1)
            dve.wait_ge(s["summed"], 2)
            nc.vector.reciprocal(total[:], total[:]).then_inc(s["summed"], 1)
            dve.wait_ge(s["summed"], 3)
            dve.wait_ge(s["ones_set"], 1)
            nc.vector.tensor_tensor(combine[:, :, 0:experts], picked[:], spread(total[:, :, None], [P, TILES, experts]),
                                    ALU.mult).then_inc(s["weighted"], 1)


def chosen_weights(nc, probs, above, equal, ranks, missing, gate, experts):
    with stage(nc, "within taken chosen weighted") as (block, s):

        @block.vector
        def _(dve):
            nc.vector.tensor_tensor(ranks[:], ranks[:], spread(missing[:, None, :], [P, TILES, experts]),
                                    ALU.is_lt).then_inc(s["within"], 1)
            dve.wait_ge(s["within"], 1)
            nc.vector.tensor_tensor(equal[:], equal[:], ranks[:], ALU.mult).then_inc(s["taken"], 1)
            dve.wait_ge(s["taken"], 1)
            nc.vector.tensor_tensor(above[:], above[:], equal[:], ALU.add).then_inc(s["chosen"], 1)
            dve.wait_ge(s["chosen"], 1)
            nc.vector.scalar_tensor_tensor(out=probs[:], in0=probs[:], scalar=gate, in1=above[:], op0=ALU.mult,
                                           op1=ALU.mult).then_inc(s["weighted"], 1)


def capped_weights(nc, probs, picked, ranks, capacity):
    with stage(nc, "kept weighted") as (block, s):

        @block.vector
        def _(dve):
            nc.vector.scalar_tensor_tensor(out=ranks[:], in0=ranks[:], scalar=float(capacity), in1=picked[:],
                                           op0=ALU.is_lt, op1=ALU.mult).then_inc(s["kept"], 1)
            dve.wait_ge(s["kept"], 1)
            nc.vector.tensor_tensor(probs[:], probs[:], ranks[:], ALU.mult).then_inc(s["weighted"], 1)


def prepare_window(nc, tables, scales, mask, mask_bf16):
    with stage(nc, "scaled copied") as (block, s):

        @block.gpsimd
        def _(pool):
            nc.gpsimd.tensor_copy(mask_bf16[:], mask[:]).then_inc(s["copied"], 1)

        @block.vector
        def _(dve):
            for i, scale in enumerate(scales):
                nc.vector.tensor_tensor(tables[:, i, :], tables[:, i, :], scale[:], ALU.mult).then_inc(s["scaled"], 1)


def shift_tokens(nc, const, src, dst):
    half = D // 2
    with memory(nc) as (sb, ps):
        bank = ps("shifted", [P, BANK])
        with stage(nc, "copied shifted used") as (block, s):

            @block.gpsimd
            def _(pool):
                nc.gpsimd.tensor_copy(dst[:, :, 0:half], src[:, :, 0:half]).then_inc(s["copied"], 1)

            @block.tensor
            def _(pe):
                with pe.Fori(0, TILES // 8) as it:
                    pe.wait_ge(s["used"], it + 1)
                    nc.tensor.matmul(bank[:], const["previous"][:], src[:, bass.ds(it * 8, 8), half:D], start=True,
                                     stop=True).then_inc(s["shifted"], 1)

            @block.scalar
            def _(act):
                act.sem_inc(s["used"], 1)
                with act.Fori(0, TILES // 8) as it:
                    act.wait_ge(s["shifted"], it + 1)
                    nc.scalar.activation(dst[:, bass.ds(it * 8, 8), half:D],
                                         bank[:].rearrange("p (t d) -> p t d", d=half), ACT.Copy).then_inc(s["used"], 1)


def project_rows(nc, const, *, src_t, weight, bias, resid, out):
    with memory(nc) as (sb, ps):
        tile = sb("tile", [P, 2, BANK])
        y_ps = ps("y_ps", [P, 2, BANK])
        with stage(nc, "tile_copied y_done y_used biased") as (block, s):

            @block.scalar
            def _(act):
                act.sem_inc(s["y_done"], 2)
                with act.Fori(0, TILES // 8) as it:
                    for u in range(2):
                        n = it * 2 + u
                        act.wait_ge(s["y_done"], n + 1)
                        nc.scalar.activation(tile[:, u, :], src_t[:, bass.ds(n * BANK, BANK)],
                                             ACT.Copy).then_inc(s["tile_copied"], 1)

            @block.tensor
            def _(pe):
                with pe.Fori(0, TILES // 8) as it:
                    for u in range(2):
                        n = it * 2 + u
                        pe.wait_ge(s["tile_copied"], n + 1)
                        pe.wait_ge(s["y_used"], n + 1)
                        for k in range(4):
                            last = nc.tensor.matmul(y_ps[:, u, k * D:(k + 1) * D], tile[:, u, k * P:(k + 1) * P], weight,
                                                    start=True, stop=True)
                        last.then_inc(s["y_done"], 1)

            @block.gpsimd
            def _(pool):
                with pool.Fori(0, TILES // 4) as n:
                    nc.gpsimd.tensor_tensor(out[:, bass.ds(n * 4, 4), :], resid[:, bass.ds(n * 4, 4), :],
                                            spread(bias[:, None, :], [P, 4, D]), ALU.add).then_inc(s["biased"], 1)

            @block.vector
            def _(dve):
                dve.sem_inc(s["y_used"], 2)
                with dve.Fori(0, TILES // 8) as it:
                    for u in range(2):
                        n = it * 2 + u
                        dve.wait_ge(s["y_done"], n + 3)
                        dve.wait_ge(s["biased"], n + 1)
                        rows = out[:, bass.ds(n * 4, 4), :]
                        nc.vector.tensor_tensor(rows, y_ps[:, u, :].rearrange("p (t d) -> p t d", d=D), rows,
                                                ALU.add).then_inc(s["y_used"], 1)



def program(nc, w, out):
    with memory(nc) as (sb, ps):
        const = dict(ident=sb("ident", [P, P]), ones=sb("ones", [P, P]), ident_bf16=sb("ident_bf16", [P, P], BF16),
                     earlier=sb("earlier", [P, P]), previous=sb("previous", [P, P]), eps=sb("eps", [P, 1]))
        gates = sb("gates", [P, 8])
        head_mask = sb("head_mask", [P, 30])
        const["row_stats"] = sb("row_stats", [P, TILES, 6])
        const["tile_of_row"] = head_mask[:, 0:16]
        const["expert_of_row"] = head_mask[:, 22:30]
        x = sb("x", [P, TILES, D])
        z = sb("z", [P, TILES, D])
        spare = sb("spare", [P, 2, TILES * D])
        h = spare[:, 0, :].rearrange("p (t d) -> p t d", d=D)
        xt = sb("xt", [P, TOKENS])
        yt = spare[:, 1, :]
        ctx_t = sb("ctx_t", [CTX, TOKENS])

        def buffers(sb, names):
            bufs = {}
            loads = []
            for name in names.split():
                shape = list(w[name].shape)
                buf = sb("w", shape)
                bufs[name.split(".")[-1]] = buf
                index = tuple(slice(None) for _ in shape)
                loads.append((buf[index], w[name][index]))
            return bufs, loads

        with stage(nc, "loaded eps_set gates_ready") as (block, s):

            @block.sync
            def _(sp):
                sp.dma_start(x[:], w["x"].rearrange("t p d -> p t d")).then_inc(s["loaded"], 16)
                sp.dma_start(gates[:], w["gates"]).then_inc(s["loaded"], 16)
                sp.dma_start(const["ident"][:], w["ident"]).then_inc(s["loaded"], 16)
                sp.dma_start(const["earlier"][:], w["earlier"]).then_inc(s["loaded"], 16)
                sp.dma_start(const["previous"][:], w["previous"]).then_inc(s["loaded"], 16)
                sp.dma_start(ctx_t[:], w["ctx_t"]).then_inc(s["loaded"], 16)
                sp.dma_start(head_mask[:], w["head_masks"]).then_inc(s["loaded"], 16)
                sp.wait_ge(s["loaded"], 112)

            @block.gpsimd
            def _(pool):
                pool.wait_ge(s["loaded"], 112)
                nc.gpsimd.tensor_copy(const["ident_bf16"][:], const["ident"][:])
                nc.gpsimd.memset(const["eps"][:], EPS)
                nc.gpsimd.memset(const["ones"][:], 1.0)

            @block.scalar
            def _(act):
                act.wait_ge(s["loaded"], 112)
                nc.scalar.activation(gates[:], gates[:], ACT.Tanh).then_inc(s["gates_ready"], 1)

        def cross_attention(layer, gate_col, biased):
            with memory(nc) as (sb, ps):
                names = "wq wk wv wo" + (" bq bk bv bo" if biased else "")
                b, loads = buffers(sb, " ".join(f"{layer}.{n}" for n in names.split()))
                layer_norm(nc, const, x, t_outs=[(xt, None, None)], loads=loads)
                attention(nc, const, heads=16, dk=8, kv_rows=CTX, head_mask=head_mask[:, 0:16],
                          q_src=lambda t: tile_cols(xt, t), kv_src=lambda t: tile_cols(ctx_t, t),
                          wq=b["wq"], wk=b["wk"], wv=b["wv"][:], wo=b["wo"], scale=8 ** -0.5,
                          q_bias=b["bq"] if biased else None, k_bias=b["bk"] if biased else None,
                          v_bias=b["bv"][:] if biased else None, o_bias=b["bo"][:] if biased else None,
                          gate=gates[:, gate_col:gate_col + 1], resid=x, out=x, keep_stats=True)

        def top_experts_layer():
            with memory(nc) as (sb, ps):
                b, loads = buffers(sb, "f0.router f0.score_bias f0.gate_w f0.up_w f0.down_w")
                probs = sb("probs", [P, TILES, 32])
                corrected = sb("corrected", [P, TILES, 32])
                threshold = sb("threshold", [P, TILES])
                total = sb("total", [P, TILES])
                combine = sb("combine", [P, TILES, 34])
                wide = [P, TILES, 32]
                layer_norm(nc, const, x, t_outs=[(xt, None, None)], loads=loads, has_stats=True)
                router(nc, const, xt, b["router"][:], None, probs, 32)
                add_all(nc, corrected[:], probs[:], spread(b["score_bias"][:, None, :], wide))
                rank_largest(nc, corrected, threshold, 32, 6)
                pick_first(nc, corrected[:], threshold, 6, corrected, 32)
                combine_weights(nc, probs, corrected, total, combine, 32)
                mix_top_experts(nc, const, src_t=xt, gate_w=b["gate_w"], up_w=b["up_w"], down_w=b["down_w"],
                                combine=combine, resid=x, gate=gates[:, 4:5])

        def transformer_block_layer():
            with memory(nc) as (sb, ps):
                ctx = sb("ctx", [P, TILES, CTX])
                b, loads = buffers(sb, "x1.ln1_g x1.ln1_b x1.ln2_g x1.ln2_b")
                names = "wq wk wv li1_w li1_b lnx_g lnx_b lny_g lny_b ln3_g ln3_b li2_w li2_b li3_w li3_b"
                parts = {a: buffers(sb, " ".join(f"{a}.{n}" for n in names.split())) for a in ("a1", "a2")}
                keep = sb("keep", [P, P])
                layer_norm(nc, const, x, row_out=h, has_stats=True,
                           loads=loads + [(keep[:], w["keys_kept"])] + parts["a1"][1])
                layer_norm(nc, const, h, row_out=z, row_affine=(b["ln1_g"], b["ln1_b"]),
                           loads=[(ctx[:], w["ctx"].rearrange("t p d -> p t d"))] + parts["a2"][1])
                for a in ("a1", "a2"):
                    v = parts[a][0]
                    if a == "a1":
                        layer_norm(nc, const, z, t_outs=[(xt, v["lnx_g"][:, 0:1], v["lnx_b"][:, 0:1]),
                                                         (yt, v["lny_g"][:, 0:1], v["lny_b"][:, 0:1])])
                    else:
                        layer_norm(nc, const, z, t_outs=[(xt, v["lnx_g"][:, 0:1], v["lnx_b"][:, 0:1])])
                        layer_norm(nc, const, ctx, width=CTX, t_outs=[(yt, v["lny_g"][:, 0:1], v["lny_b"][:, 0:1])])
                    kv_rows = D if a == "a1" else CTX
                    attention(nc, const, heads=16, dk=32, kv_rows=kv_rows, head_mask=head_mask[:, 16:20],
                              q_src=lambda t: tile_cols(xt, t),
                              kv_src=lambda t: yt[0:kv_rows, bass.ds(t * P, P)],
                              wq=v["wq"], wk=v["wk"], wv=v["wv"][:], wo=v["li1_w"], o_bias=v["li1_b"][:],
                              scale=32 ** -0.5,
                              keep_mask=keep if a == "a1" else None, resid=z, out=h,
                              keep_stats=True)
                    layer_norm(nc, const, h, t_outs=[(xt, v["ln3_g"][:, 0:1], v["ln3_b"][:, 0:1])], has_stats=True)
                    feed_forward(nc, const, src_t=xt, up=v["li2_w"], up_bias=v["li2_b"], down=v["li3_w"],
                                 down_bias=v["li3_b"][:], rows=P, chunks=4, act_func=ACT.Gelu, resid=h)
                    add_all(nc, z[:], z[:], h[:])
                    if a == "a1":
                        layer_norm(nc, const, z, row_out=z, row_affine=(b["ln2_g"], b["ln2_b"]))
                add_all(nc, x[:], z[:], x[:], gates[:, 1:2])

        def chosen_tokens_layer():
            experts, capacity = 8, TOKENS // 8
            with memory(nc) as (sb, ps):
                b, loads = buffers(sb, "f1.router f1.router_b f1.up_w f1.up_b f1.down_w f1.down_b")
                probs = sb("probs", [P, TILES, experts])
                above = sb("above", [P, TILES, experts])
                equal = sb("equal", [P, TILES, experts])
                ranks = sb("ranks", [P, TILES, experts])
                threshold = sb("threshold", [P, experts])
                missing = sb("missing", [P, experts])
                wide = [P, TILES, experts]
                layer_norm(nc, const, x, t_outs=[(xt, None, None)], loads=loads)
                router(nc, const, xt, b["router"][:], b["router_b"], probs, experts)
                expert_thresholds(nc, const, probs, threshold, missing, equal, above, experts, capacity)
                ranks_over_tokens(nc, const, equal, ranks, experts)
                chosen_weights(nc, probs, above, equal, ranks, missing, gates[:, 5:6], experts)
                mix_chosen_tokens(nc, const, src_t=xt, up_w=b["up_w"], up_b=b["up_b"], down_w=b["down_w"],
                                  weights=probs[:].rearrange("p t e -> p (t e)"), resid=x)
                add_weighted_biases(nc, const, probs[:].rearrange("p t e -> p (t e)"), b["down_b"], x)

        def local_transformer_layer():
            layer_norm(nc, const, x, row_out=z, has_stats=True)
            for layer in range(2):
                with memory(nc) as (sb, ps):
                    names = "wqkv q_scale k_scale q_scale_swap k_scale_swap wo ln_g ln_b wa wg ba bg w2 b2"
                    b, loads = buffers(sb, " ".join(f"f2.{layer}.{n}" for n in names.split()))
                    mask = sb("mask", [P, 4 * P])
                    mask_bf16 = sb("mask_bf16", [P, 4 * P], BF16)
                    tables = sb("tables", [P, 4, 64])
                    loads += [(mask[:], w["window_mask"]), (tables[:], w["rotary_tables"])]
                    layer_norm(nc, const, z, t_outs=[(xt, None, None)], normalize=False, shifted=True, loads=loads)
                    prepare_window(nc, tables, (b["q_scale"], b["q_scale_swap"], b["k_scale"], b["k_scale_swap"]),
                                   mask, mask_bf16)
                    with memory(nc) as (sb2, _):
                        queries = sb2("queries", [P, TILES // 2, 512])
                        keys = spare[:].rearrange("p a (t c) -> p (a t) c", c=512)
                        for half in range(2):
                            tiles = slice(half * (TILES // 2), (half + 1) * (TILES // 2))
                            source = xt[:, half * (TOKENS // 2):(half + 1) * (TOKENS // 2)]
                            rotary_rows(nc, const, heads=8, dk=64, src_t=lambda t: tile_cols(source, t),
                                        wq=b["wqkv"][:, 0:512], wk=b["wqkv"][:, 512:1024],
                                        tables=[tables[:, i, :] for i in range(4)], turned=(queries, keys),
                                        tiles=TILES // 2)
                            attention(nc, const, heads=8, dk=64, kv_rows=D, head_mask=head_mask[:, 20:22],
                                      q_src=None, kv_src=lambda t: tile_cols(source, t), wq=None, wk=None,
                                      wv=b["wqkv"][:, 1024:1536], wo=b["wo"], scale=8.0, add_mask=mask_bf16[:],
                                      ready=(queries, keys), resid=z[:, tiles, :], out=z[:, tiles, :],
                                      tiles=TILES // 2)
                    shift_tokens(nc, const, z, h)
                    layer_norm(nc, const, h, t_outs=[(xt, b["ln_g"][:, 0:1], b["ln_b"][:, 0:1])])
                    feed_forward(nc, const, src_t=xt, up=b["wg"], up_bias=b["bg"], value=b["wa"],
                                 value_bias=b["ba"], down=b["w2"], down_bias=b["b2"][:], rows=114, chunks=3, act_func=ACT.Gelu, resid=z)
            add_all(nc, x[:], z[:], x[:], gates[:, 6:7])

        def capacity_experts_layer():
            experts, capacity = 8, TOKENS // 8
            with memory(nc) as (sb, ps):
                names = "wq wk wv bq bk bv wo bo ln1_g ln1_b ln2_g ln2_b router"
                b, loads = buffers(sb, " ".join(f"f3.{n}" for n in names.split()))
                merged = sb("merged", [P, experts * D])
                merged_b = sb("merged_b", [1, experts * D])
                mask = sb("mask", [P, 4 * P])
                mask_bf16 = sb("mask_bf16", [P, 4 * P], BF16)
                loads.append((mask[:], w["block_mask"]))
                with memory(nc) as (sb2, _):
                    e, e_loads = buffers(sb2, "f3.w1_t f3.w2 f3.b1 f3.b2")
                    layer_norm(nc, const, x, row_out=z, t_outs=[(xt, None, None)], loads=loads + e_loads,
                               has_stats=True)
                    merge_linear_experts(nc, const, e["w1_t"], e["w2"], e["b1"], e["b2"], merged, merged_b, experts, 4)
                by_token = xt[:].rearrange("p (l n c) -> p n c l", l=TILES, c=4)
                out_by_token = yt[:].rearrange("p (l n c) -> p n c l", l=TILES, c=4)
                prepare_window(nc, None, (), mask, mask_bf16)
                attention(nc, const, heads=4, dk=32, kv_rows=D, head_mask=head_mask[:, 16:20],
                          q_src=lambda t: by_token[:, bass.ds(t, 1), :, :].rearrange("p n c l -> p (n c) l"),
                          kv_src=lambda t: by_token[:, bass.ds(t, 1), :, :].rearrange("p n c l -> p (n c) l"),
                          wq=b["wq"], wk=b["wk"], wv=b["wv"][:], q_bias=b["bq"], k_bias=b["bk"], v_bias=b["bv"][:],
                          scale=float(1.0 / np.float32(np.sqrt(32))), add_mask=mask_bf16[:],
                          turned_out=lambda t: out_by_token[:, bass.ds(t, 1), :, :].rearrange("p n c l -> p (n c) l"))
                project_rows(nc, const, src_t=yt, weight=b["wo"][:], bias=b["bo"][:], resid=z, out=h)
                layer_norm(nc, const, h, row_out=z, row_affine=(b["ln1_g"], b["ln1_b"]))
                layer_norm(nc, const, z, t_outs=[(xt, None, None)], normalize=False)
                probs = sb("probs", [P, TILES, experts])
                picked = sb("picked", [P, TILES, experts])
                ranks = sb("ranks", [P, TILES, experts])
                most = sb("most", [P, TILES])
                router(nc, const, xt, b["router"][:], None, probs, experts)
                most_probable(nc, probs, most)
                pick_first(nc, probs[:], most, 1, picked, experts)
                ranks_over_tokens(nc, const, picked, ranks, experts)
                capped_weights(nc, probs, picked, ranks, capacity)
                mix_merged_experts(nc, const, src_t=xt, merged=merged,
                                   weights=probs[:].rearrange("p t e -> p (t e)"), resid=z, experts=experts)
                add_weighted_biases(nc, const, probs[:].rearrange("p t e -> p (t e)"), merged_b, z)
                layer_norm(nc, const, z, row_out=h, row_affine=(b["ln2_g"], b["ln2_b"]))
                add_all(nc, x[:], h[:], x[:], gates[:, 7:8])

        cross_attention("x0", 0, True)
        top_experts_layer()
        transformer_block_layer()
        chosen_tokens_layer()
        cross_attention("x2", 2, False)
        local_transformer_layer()
        cross_attention("x3", 3, True)
        capacity_experts_layer()

        with stage(nc, "stored") as (block, s):

            @block.sync
            def _(sp):
                sp.dma_start(out.rearrange("t p d -> p t d"), x[:]).then_inc(s["stored"], 16)
                sp.wait_ge(s["stored"], 16)



def rotary_tables():
    half_idx = np.arange(0, 64, 2, dtype=np.float32)
    inv_freq = (1.0 / 10000.0 ** (half_idx / 64)).astype(np.float32)
    t = np.arange(P, dtype=np.float32)
    freqs = np.concatenate([t[:, None] * inv_freq[None, :]] * 2, axis=-1)
    base = (half_idx + np.float32(0.4 * 64)) / np.float32(1.4 * 64)
    power = (t - P // 2) / np.float32(32)
    scale = np.concatenate([base[None, :] ** power[:, None]] * 2, axis=-1)
    sign = np.concatenate([-np.ones(32), np.ones(32)]).astype(np.float32)
    cos, sin = np.cos(freqs), np.sin(freqs) * sign
    return np.stack([cos * scale, sin * scale, cos / scale, sin / scale], axis=1).astype(np.float32)


def layout(a):
    def rows(v):
        return np.repeat(np.asarray(v)[None, :], P, axis=0)

    def col(v):
        return np.asarray(v)[:, None]

    def on_partitions(m, chunk):
        m = np.asarray(m)
        chunks = -(-m.shape[0] // chunk)
        wide = np.zeros((chunks * chunk,) + m.shape[1:], m.dtype)
        wide[:m.shape[0]] = m
        return np.moveaxis(wide.reshape((chunks, chunk) + m.shape[1:]), 0, 1)

    def padded_cols(m, n):
        m = np.asarray(m)
        wide = np.zeros(m.shape[:-1] + (n,), m.dtype)
        wide[..., :m.shape[-1]] = m
        return wide

    def swapped(v):
        return np.concatenate([v[32:], v[:32]])

    w = {}
    i, j = np.arange(P)[:, None], np.arange(P)[None, :]
    w["ident"] = (i == j).astype(np.float32)
    w["earlier"] = (i < j).astype(np.float32)
    w["previous"] = (i == j - 1).astype(np.float32)
    w["keys_kept"] = (i > j).astype(np.float32)
    w["window_mask"] = np.tile(np.where((j <= i) & (i - j <= 64), 0.0, -1e30).astype(np.float32), (1, 4))
    w["block_mask"] = np.tile(np.where(i // 32 == j // 32, 0.0, -1e30).astype(np.float32), (1, 4))
    w["head_masks"] = np.concatenate([i // dk == np.arange(P // dk)[None, :] for dk in (8, 32, 64)]
                                     + [i % 8 == np.arange(8)[None, :]], axis=1).astype(np.float32)
    w["rotary_tables"] = rotary_tables()
    w["x"] = a["x"]
    w["ctx"] = a["ctx_512"]
    w["ctx_t"] = np.asarray(a["ctx_512"]).reshape(TOKENS, CTX).T
    w["gates"] = np.concatenate([rows(a["g_xattn"]), rows(a["g_ffn"])], axis=1)
    for k in (0, 3):
        p = f"L{k}_xattn_"
        w[f"x{k}.wq"] = a[p + "Wq"]
        w[f"x{k}.wk"] = a[p + "Wk"]
        w[f"x{k}.wv"] = a[p + "Wv"]
        w[f"x{k}.wo"] = np.asarray(a[p + "Wo"])[:, None, :]
        w[f"x{k}.bq"] = col(a[p + "bq"])
        w[f"x{k}.bk"] = col(a[p + "bk"])
        w[f"x{k}.bv"] = rows(a[p + "bv"])
        w[f"x{k}.bo"] = rows(a[p + "bo"])
    kv = np.asarray(a["L2_xattn_Wkv"])
    w["x2.wq"] = np.asarray(a["L2_xattn_Wq"]).T
    w["x2.wk"] = kv[:D].T
    w["x2.wv"] = kv[D:].T
    w["x2.wo"] = np.asarray(a["L2_xattn_Wo"]).T[:, None, :]

    gate_up = np.asarray(a["L0_ffn_gate_up_proj"])
    w["f0.router"] = np.asarray(a["L0_ffn_router_weight"]).T
    w["f0.score_bias"] = rows(a["L0_ffn_e_score_bias"])
    w["f0.gate_w"] = np.concatenate([gate_up[:, :64].reshape(2048, D), a["L0_ffn_shared_gate_w"]]).T
    w["f0.up_w"] = np.concatenate([gate_up[:, 64:].reshape(2048, D), a["L0_ffn_shared_up_w"]]).T
    down = np.concatenate([np.moveaxis(np.asarray(a["L0_ffn_down_proj"]), 2, 1).reshape(2048, D),
                           np.asarray(a["L0_ffn_shared_down_w"]).T])
    w["f0.down_w"] = on_partitions(down, P)

    for n in ("ln1_g", "ln1_b", "ln2_g", "ln2_b"):
        w[f"x1.{n}"] = rows(a[f"L1_xattn_{n}"])
    for k in ("a1", "a2"):
        p = f"L1_xattn_{k}_"
        for n in ("wq", "wk", "wv"):
            w[f"{k}.{n}"] = np.moveaxis(np.asarray(a[p + n]), 0, 1).reshape(-1, 512)
        w[f"{k}.li1_w"] = on_partitions(a[p + "li1_w"], P)
        w[f"{k}.li1_b"] = rows(a[p + "li1_b"])
        for n in ("lnx_g", "lnx_b", "lny_g", "lny_b", "ln3_g", "ln3_b"):
            w[f"{k}.{n}"] = col(a[p + n])
        w[f"{k}.li2_w"] = a[p + "li2_w"]
        w[f"{k}.li2_b"] = np.asarray(a[p + "li2_b"]).reshape(4, P).T
        w[f"{k}.li3_w"] = on_partitions(a[p + "li3_w"], P)
        w[f"{k}.li3_b"] = rows(a[p + "li3_b"])

    w["f1.router"] = a["L1_ffn_Wr"]
    w["f1.router_b"] = rows(a["L1_ffn_br"])
    w["f1.up_w"] = np.moveaxis(padded_cols(a["L1_ffn_W_up"], 342), 0, 1).reshape(D, 4 * 342)
    w["f1.up_b"] = padded_cols(a["L1_ffn_b_up"], 342).reshape(12, 114).T
    w["f1.down_w"] = on_partitions(np.moveaxis(np.asarray(a["L1_ffn_W_down"]), 0, 1).reshape(341, 8 * D), 114)
    w["f1.down_b"] = np.asarray(a["L1_ffn_b_down"]).reshape(1, 8 * D)

    for k in range(2):
        q, p = f"f2.{k}.", "L2_ffn_"
        w[q + "wqkv"] = np.asarray(a[p + "wqkv"])[k]
        for n in ("q_scale", "k_scale"):
            w[q + n] = rows(np.asarray(a[p + n])[k])
            w[q + n + "_swap"] = rows(swapped(np.asarray(a[p + n])[k]))
        w[q + "wo"] = on_partitions(np.asarray(a[p + "wo"])[k], P)
        w[q + "ln_g"] = col(np.asarray(a[p + "ln_g"])[k])
        w[q + "ln_b"] = col(np.asarray(a[p + "ln_b"])[k])
        w1, b1 = np.asarray(a[p + "w1"])[k], np.asarray(a[p + "b1"])[k]
        w[q + "wa"] = padded_cols(w1[:, :341], 342)
        w[q + "wg"] = padded_cols(w1[:, 341:], 342)
        w[q + "ba"] = padded_cols(b1[:341], 342).reshape(3, 114).T
        w[q + "bg"] = padded_cols(b1[341:], 342).reshape(3, 114).T
        w[q + "w2"] = on_partitions(np.asarray(a[p + "w2"])[k], 114)
        w[q + "b2"] = rows(np.asarray(a[p + "b2"])[k])

    proj, proj_b = np.asarray(a["L3_ffn_in_proj_w"]), np.asarray(a["L3_ffn_in_proj_b"])
    for k, n in enumerate("qkv"):
        w[f"f3.w{n}"] = proj[k * D:(k + 1) * D].T
    w["f3.bq"], w["f3.bk"] = col(proj_b[:D]), col(proj_b[D:2 * D])
    w["f3.bv"] = rows(proj_b[2 * D:])
    w["f3.wo"] = np.asarray(a["L3_ffn_out_proj_w"]).T
    w["f3.bo"] = rows(a["L3_ffn_out_proj_b"])
    for n in ("ln1_g", "ln1_b", "ln2_g", "ln2_b"):
        w[f"f3.{n}"] = rows(a[f"L3_ffn_{n}"])
    w["f3.router"] = a["L3_ffn_wg"]
    w["f3.w1_t"] = np.transpose(np.asarray(a["L3_ffn_w1"]).reshape(8, D, 4, P), (3, 2, 0, 1))
    w["f3.w2"] = np.transpose(np.asarray(a["L3_ffn_w2"]).reshape(8, 4, P, D), (2, 1, 0, 3))
    w["f3.b1"] = np.transpose(np.asarray(a["L3_ffn_b1"]).reshape(8, 4, P), (2, 1, 0))
    w["f3.b2"] = np.asarray(a["L3_ffn_b2"]).reshape(1, 8 * D)
    return {name: np.ascontiguousarray(v) for name, v in w.items()}


def kernel(**inputs):
    from concourse import bacc
    from concourse.bass_utils import run_bass_kernel_spmd

    nc = bacc.Bacc("TRN2", target_bir_lowering=False, num_devices=1)
    laid_out = layout(inputs)
    arrays = {"in_" + name.replace(".", "_"): v for name, v in laid_out.items()}
    tensors = {name: nc.dram_tensor("in_" + name.replace(".", "_"), v.shape, F32, kind="ExternalInput").ap()
               for name, v in laid_out.items()}
    out = nc.dram_tensor("out", (TILES, P, D), F32, kind="ExternalOutput").ap()
    program(nc, tensors, out)
    result = run_bass_kernel_spmd(nc, [arrays], core_ids=[0])
    return np.asarray(result.results[0]["out"])
```
